# Optimizing a Trainium2 kernel written in Bass

```python
import numpy as np
import jax
import jax.numpy as jnp

def _softmax(x, axis=-1):
    return jax.nn.softmax(x, axis=axis)

def _gelu(x):
    return jax.nn.gelu(x, approximate=True)

def _silu(x):
    return jax.nn.silu(x)

def _sigmoid(x):
    return jax.nn.sigmoid(x)

def _layernorm(x, axis=-1, eps=1e-05):
    m = jnp.mean(x, axis=axis, keepdims=True)
    v = jnp.var(x, axis=axis, keepdims=True)
    return (x - m) / jnp.sqrt(v + eps)

def _scatter_add(tgt, idx, src, axis=0):
    return tgt.at[idx].add(src)

def _segment_sum(src, seg, n):
    return jax.ops.segment_sum(src, seg, n)
kernel_name = 'mk_gps_d1_gnn_r32_ae7279'

def setup_inputs(seed: int=0):
    np.random.seed(seed)
    _w = jnp.asarray

    def _rec_inputs():
        import jax
        import jax.numpy as jnp
        _gk = jax.random.key(seed)
        x = -8.776e-05 + 1 * jax.random.normal(jax.random.fold_in(_gk, 1), (3125, 256), jnp.float32)
        src = jax.random.randint(jax.random.fold_in(_gk, 2), (50000,), 0, 3125, jnp.int32)
        dst = jnp.minimum((3125 * jax.random.uniform(jax.random.fold_in(_gk, 3), (50000,)) ** 2.0).astype(jnp.int32), 99999)
        _o = jnp.argsort(dst, stable=True)
        src = src[_o]
        dst = dst[_o]
        return (x, src, dst)
    x, src, dst = _rec_inputs()

    def _L0_gnn_setup():
        import jax, jax.numpy as jnp
        import numpy as np
        N = 625
        E = 10000
        D_IN = 256
        HID = 64
        HEADS = 4
        D_OUT = 256
        EPS = 1e-05
        SLOPE = 0.2

        def _gat(x, src, dst, W, a_src, a_dst, b, heads, ch, concat):
            n = x.shape[0]
            h = (x @ W).reshape(n, heads, ch)
            es = (h * a_src).sum(-1)
            ed = (h * a_dst).sum(-1)
            e = jax.nn.leaky_relu(es[src] + ed[dst], SLOPE)
            m = jax.ops.segment_max(e, dst, num_segments=n)
            w = jnp.exp(e - m[dst])
            den = jax.ops.segment_sum(w, dst, num_segments=n)
            alpha = w / den[dst]
            msg = h[src] * alpha[:, :, None]
            out = jax.ops.segment_sum(msg, dst, num_segments=n)
            out = out.reshape(n, heads * ch) if concat else out.mean(axis=1)
            return out + b

        def _layernorm(x, g, b):
            mu = x.mean(-1, keepdims=True)
            v = ((x - mu) ** 2).mean(-1, keepdims=True)
            return (x - mu) * jax.lax.rsqrt(v + EPS) * g + b
        key = jax.random.key(seed)
        ks = jax.random.split(key, 10)

        def glorot(k, shape):
            fan_in, fan_out = (shape[0], int(np.prod(shape[1:])))
            s = np.sqrt(2.0 / (fan_in + fan_out)).astype(np.float32)
            return jax.random.normal(k, shape, dtype=jnp.float32) * s
        x = jax.random.normal(ks[0], (N, D_IN), dtype=jnp.float32)
        edge_index = jax.random.randint(ks[1], (2, E), 0, N, dtype=jnp.int64)
        return {'x': x, 'edge_index': edge_index, 'W1': glorot(ks[2], (D_IN, HEADS * HID)), 'a1_src': glorot(ks[3], (HEADS, HID)), 'a1_dst': glorot(ks[4], (HEADS, HID)), 'b1': jnp.zeros((HEADS * HID,), jnp.float32), 'ln_g': jnp.ones((HEADS * HID,), jnp.float32), 'ln_b': jnp.zeros((HEADS * HID,), jnp.float32), 'W2': glorot(ks[5], (HEADS * HID, D_OUT)), 'a2_src': glorot(ks[6], (1, D_OUT)), 'a2_dst': glorot(ks[7], (1, D_OUT)), 'b2': jnp.zeros((D_OUT,), jnp.float32)}
    _L0_gnn_all = _L0_gnn_setup()
    _L0_gnn_in = {k: v for k, v in _L0_gnn_all.items() if k in ('W1', 'a1_src', 'a1_dst', 'b1', 'ln_g', 'ln_b', 'W2', 'a2_src', 'a2_dst', 'b2')}
    del _L0_gnn_all

    def _L0_mix_setup():
        import jax, jax.numpy as jnp
        import numpy as np
        B, N, C = (8, 256, 256)
        HEADS, DH, KR = (8, 32, 4)
        INNER = HEADS * DH
        FF = 4 * C
        EPS = 1e-05

        def layernorm(x, g, b):
            mu = jnp.mean(x, axis=-1, keepdims=True)
            var = jnp.mean((x - mu) ** 2, axis=-1, keepdims=True)
            return (x - mu) * jax.lax.rsqrt(var + EPS) * g + b
        key = jax.random.key(seed)
        ks = jax.random.split(key, 16)
        s = 0.02
        return {'x': jax.random.normal(ks[0], (B, N, C), jnp.float32), 'ln1_g': jnp.ones((C,), jnp.float32), 'ln1_b': jnp.zeros((C,), jnp.float32), 'Wx': jax.random.normal(ks[1], (C, INNER), jnp.float32) * s, 'bx': jnp.zeros((INNER,), jnp.float32), 'Wq': jax.random.normal(ks[2], (DH, KR), jnp.float32) * s, 'Wk': jax.random.normal(ks[3], (DH, KR), jnp.float32) * s, 'Wv': jax.random.normal(ks[4], (DH, DH), jnp.float32) * s, 'Wo': jax.random.normal(ks[5], (INNER, C), jnp.float32) * s, 'bo': jnp.zeros((C,), jnp.float32), 'ln2_g': jnp.ones((C,), jnp.float32), 'ln2_b': jnp.zeros((C,), jnp.float32), 'W1': jax.random.normal(ks[6], (C, FF), jnp.float32) * s, 'b1': jnp.zeros((FF,), jnp.float32), 'W2': jax.random.normal(ks[7], (FF, C), jnp.float32) * s, 'b2': jnp.zeros((C,), jnp.float32)}
    _L0_mix_all = _L0_mix_setup()
    _L0_mix_in = {k: v for k, v in _L0_mix_all.items() if k in ('ln1_g', 'ln1_b', 'Wx', 'bx', 'Wq', 'Wk', 'Wv', 'Wo', 'bo', 'ln2_g', 'ln2_b', 'W1', 'b1', 'W2', 'b2')}
    del _L0_mix_all

    def _L0_ffn_setup():
        import jax, jax.numpy as jnp
        import numpy as np
        D_MODEL = 256
        EXPERT_DIM = 512
        NUM_EXPERTS = 8
        TOP_K = 2
        SEQ_LEN = 64
        BATCH = 2
        key = jax.random.key(seed)
        ks = jax.random.split(key, 8)
        s = 0.02
        x = jax.random.normal(ks[0], (SEQ_LEN, BATCH, D_MODEL), dtype=jnp.float32)
        Wg = jax.random.normal(ks[1], (D_MODEL, NUM_EXPERTS), dtype=jnp.float32) * s
        bg = jax.random.normal(ks[2], (NUM_EXPERTS,), dtype=jnp.float32) * s
        bias = jnp.zeros((NUM_EXPERTS,), dtype=jnp.float32)
        W1 = jax.random.normal(ks[3], (NUM_EXPERTS, D_MODEL, EXPERT_DIM), dtype=jnp.float32) * s
        b1 = jax.random.normal(ks[4], (NUM_EXPERTS, EXPERT_DIM), dtype=jnp.float32) * s
        W2 = jax.random.normal(ks[5], (NUM_EXPERTS, EXPERT_DIM, D_MODEL), dtype=jnp.float32) * s
        b2 = jax.random.normal(ks[6], (NUM_EXPERTS, D_MODEL), dtype=jnp.float32) * s
        return {'x': x, 'Wg': Wg, 'bg': bg, 'bias': bias, 'W1': W1, 'b1': b1, 'W2': W2, 'b2': b2}
    _L0_ffn_all = _L0_ffn_setup()
    _L0_ffn_in = {k: v for k, v in _L0_ffn_all.items() if k in ('Wg', 'bg', 'bias', 'W1', 'b1', 'W2', 'b2')}
    del _L0_ffn_all
    return {'x': x, 'src': src, 'dst': dst, 'L0_gnn_W1': _L0_gnn_in['W1'], 'L0_gnn_a1_src': _L0_gnn_in['a1_src'], 'L0_gnn_a1_dst': _L0_gnn_in['a1_dst'], 'L0_gnn_b1': _L0_gnn_in['b1'], 'L0_gnn_ln_g': _L0_gnn_in['ln_g'], 'L0_gnn_ln_b': _L0_gnn_in['ln_b'], 'L0_gnn_W2': _L0_gnn_in['W2'], 'L0_gnn_a2_src': _L0_gnn_in['a2_src'], 'L0_gnn_a2_dst': _L0_gnn_in['a2_dst'], 'L0_gnn_b2': _L0_gnn_in['b2'], 'L0_mix_ln1_g': _L0_mix_in['ln1_g'], 'L0_mix_ln1_b': _L0_mix_in['ln1_b'], 'L0_mix_Wx': _L0_mix_in['Wx'], 'L0_mix_bx': _L0_mix_in['bx'], 'L0_mix_Wq': _L0_mix_in['Wq'], 'L0_mix_Wk': _L0_mix_in['Wk'], 'L0_mix_Wv': _L0_mix_in['Wv'], 'L0_mix_Wo': _L0_mix_in['Wo'], 'L0_mix_bo': _L0_mix_in['bo'], 'L0_mix_ln2_g': _L0_mix_in['ln2_g'], 'L0_mix_ln2_b': _L0_mix_in['ln2_b'], 'L0_mix_W1': _L0_mix_in['W1'], 'L0_mix_b1': _L0_mix_in['b1'], 'L0_mix_W2': _L0_mix_in['W2'], 'L0_mix_b2': _L0_mix_in['b2'], 'L0_ffn_Wg': _L0_ffn_in['Wg'], 'L0_ffn_bg': _L0_ffn_in['bg'], 'L0_ffn_bias': _L0_ffn_in['bias'], 'L0_ffn_W1': _L0_ffn_in['W1'], 'L0_ffn_b1': _L0_ffn_in['b1'], 'L0_ffn_W2': _L0_ffn_in['W2'], 'L0_ffn_b2': _L0_ffn_in['b2']}

def reference(x, src, dst, L0_gnn_W1, L0_gnn_a1_src, L0_gnn_a1_dst, L0_gnn_b1, L0_gnn_ln_g, L0_gnn_ln_b, L0_gnn_W2, L0_gnn_a2_src, L0_gnn_a2_dst, L0_gnn_b2, L0_mix_ln1_g, L0_mix_ln1_b, L0_mix_Wx, L0_mix_bx, L0_mix_Wq, L0_mix_Wk, L0_mix_Wv, L0_mix_Wo, L0_mix_bo, L0_mix_ln2_g, L0_mix_ln2_b, L0_mix_W1, L0_mix_b1, L0_mix_W2, L0_mix_b2, L0_ffn_Wg, L0_ffn_bg, L0_ffn_bias, L0_ffn_W1, L0_ffn_b1, L0_ffn_W2, L0_ffn_b2):
    import jax
    import jax.numpy as jnp

    def _L0_gnn_ref(x, edge_index, W1, a1_src, a1_dst, b1, ln_g, ln_b, W2, a2_src, a2_dst, b2):
        import jax, jax.numpy as jnp
        import numpy as np
        N = 625
        E = 10000
        D_IN = 256
        HID = 64
        HEADS = 4
        D_OUT = 256
        EPS = 1e-05
        SLOPE = 0.2

        def _gat(x, src, dst, W, a_src, a_dst, b, heads, ch, concat):
            n = x.shape[0]
            h = (x @ W).reshape(n, heads, ch)
            es = (h * a_src).sum(-1)
            ed = (h * a_dst).sum(-1)
            e = jax.nn.leaky_relu(es[src] + ed[dst], SLOPE)
            m = jax.ops.segment_max(e, dst, num_segments=n)
            w = jnp.exp(e - m[dst])
            den = jax.ops.segment_sum(w, dst, num_segments=n)
            alpha = w / den[dst]
            msg = h[src] * alpha[:, :, None]
            out = jax.ops.segment_sum(msg, dst, num_segments=n)
            out = out.reshape(n, heads * ch) if concat else out.mean(axis=1)
            return out + b

        def _layernorm(x, g, b):
            mu = x.mean(-1, keepdims=True)
            v = ((x - mu) ** 2).mean(-1, keepdims=True)
            return (x - mu) * jax.lax.rsqrt(v + EPS) * g + b
        loops = jnp.arange(N, dtype=edge_index.dtype)
        src = jnp.concatenate([edge_index[0], loops])
        dst = jnp.concatenate([edge_index[1], loops])
        h = _gat(x, src, dst, W1, a1_src, a1_dst, b1, HEADS, HID, True)
        h = jax.nn.relu(_layernorm(h, ln_g, ln_b))
        out = _gat(h, src, dst, W2, a2_src, a2_dst, b2, 1, D_OUT, False)
        return out

    def _L0_mix_ref(x, ln1_g, ln1_b, Wx, bx, Wq, Wk, Wv, Wo, bo, ln2_g, ln2_b, W1, b1, W2, b2):
        import jax, jax.numpy as jnp
        import numpy as np
        B, N, C = (8, 256, 256)
        HEADS, DH, KR = (8, 32, 4)
        INNER = HEADS * DH
        FF = 4 * C
        EPS = 1e-05

        def layernorm(x, g, b):
            mu = jnp.mean(x, axis=-1, keepdims=True)
            var = jnp.mean((x - mu) ** 2, axis=-1, keepdims=True)
            return (x - mu) * jax.lax.rsqrt(var + EPS) * g + b
        b, n, c = x.shape
        h = layernorm(x, ln1_g, ln1_b)
        xm = h @ Wx + bx
        xm = xm.reshape(b, n, HEADS, DH).transpose(0, 2, 1, 3)
        q = jax.nn.softmax(xm @ Wq, axis=-1)
        k = jax.nn.softmax(xm @ Wk, axis=-2)
        v = xm @ Wv
        kv = jnp.einsum('bhnr,bhnd->bhrd', k, v)
        qkv = jnp.einsum('bhnr,bhrd->bhnd', q, kv)
        attn = qkv.transpose(0, 2, 1, 3).reshape(b, n, INNER) @ Wo + bo
        fx = attn + x
        h2 = layernorm(fx, ln2_g, ln2_b)
        m = jax.nn.gelu(h2 @ W1 + b1, approximate=False) @ W2 + b2
        return m + fx

    def _L0_ffn_ref(x, Wg, bg, bias, W1, b1, W2, b2):
        import jax, jax.numpy as jnp
        import numpy as np
        D_MODEL = 256
        EXPERT_DIM = 512
        NUM_EXPERTS = 8
        TOP_K = 2
        SEQ_LEN = 64
        BATCH = 2
        x_flat = x.reshape(-1, D_MODEL)
        gate_logits = x_flat @ Wg + bg + bias
        topk_vals, topk_idx = jax.lax.top_k(gate_logits, TOP_K)
        topk_w = jax.nn.softmax(topk_vals, axis=-1)
        combine = (jax.nn.one_hot(topk_idx, NUM_EXPERTS, dtype=x.dtype) * topk_w[..., None]).sum(axis=1)
        h = jax.nn.relu(jnp.einsum('td,edh->teh', x_flat, W1) + b1)
        y = jnp.einsum('teh,ehd->ted', h, W2) + b2
        out = jnp.einsum('ted,te->td', y, combine)
        return out.reshape(x.shape)
    edge_index = jnp.stack([src, dst])
    xn = _layernorm(x, axis=-1)
    x = x + _L0_gnn_ref(xn, edge_index, L0_gnn_W1, L0_gnn_a1_src, L0_gnn_a1_dst, L0_gnn_b1, L0_gnn_ln_g, L0_gnn_ln_b, L0_gnn_W2, L0_gnn_a2_src, L0_gnn_a2_dst, L0_gnn_b2) + _L0_mix_ref(xn[None], L0_mix_ln1_g, L0_mix_ln1_b, L0_mix_Wx, L0_mix_bx, L0_mix_Wq, L0_mix_Wk, L0_mix_Wv, L0_mix_Wo, L0_mix_bo, L0_mix_ln2_g, L0_mix_ln2_b, L0_mix_W1, L0_mix_b1, L0_mix_W2, L0_mix_b2)[0]
    x = x + _L0_ffn_ref(_layernorm(x, axis=-1)[None], L0_ffn_Wg, L0_ffn_bg, L0_ffn_bias, L0_ffn_W1, L0_ffn_b1, L0_ffn_W2, L0_ffn_b2)[0]
    return x

_drawn_inputs = setup_inputs


def setup_inputs(seed=0):
    import zlib

    import numpy as np

    out = dict(_drawn_inputs(seed))
    spreads = {'L0_gnn_b1': (0.0, 0.394),
     'L0_gnn_ln_g': (1.0, 0.6),
     'L0_gnn_ln_b': (0.0, 0.8),
     'L0_gnn_b2': (0.0, 0.551),
     'L0_mix_ln1_g': (1.0, 0.6),
     'L0_mix_ln1_b': (0.0, 0.8),
     'L0_mix_bx': (0.0, 0.8),
     'L0_mix_bo': (0.0, 0.611),
     'L0_mix_ln2_g': (1.0, 0.6),
     'L0_mix_ln2_b': (0.0, 2.0),
     'L0_mix_b1': (0.0, 1.444),
     'L0_mix_b2': (0.0, 0.589),
     'L0_ffn_bias': (0.0, 1.553)}
    factors = {'L0_gnn_a2_dst': 22.804,
     'L0_mix_Wx': 8.0,
     'L0_mix_Wq': 8.0,
     'L0_mix_Wk': 8.0,
     'L0_mix_Wv': 8.0,
     'L0_mix_Wo': 8.0,
     'L0_ffn_bg': 64.0,
     'L0_ffn_b1': 64.0,
     'L0_ffn_b2': 28.733,
     'L0_gnn_a1_dst': 6.838,
     'L0_gnn_a2_src': 4.574,
     'L0_ffn_Wg': 7.771,
     'L0_ffn_W1': 6.476,
     'L0_ffn_W2': 5.126}
    for name, (base, spread) in spreads.items():
        noise = np.random.default_rng([zlib.crc32(name.encode()), seed]).standard_normal(out[name].shape)
        drawn = base * np.exp(spread * noise) if base else spread * noise
        out[name] = jnp.asarray(drawn.astype(out[name].dtype))
    for name, factor in factors.items():
        out[name] = (out[name] * factor).astype(out[name].dtype)
    return out
```

```python
from contextlib import ExitStack, contextmanager

import concourse.bass as bass
from concourse import mybir

F32 = mybir.dt.float32
I32 = mybir.dt.int32
U32 = mybir.dt.uint32
ALU = mybir.AluOpType
ACT = mybir.ActivationFunctionType
AX = mybir.AxisListType

P = 128
N, C, E = 3125, 256, 50000
NT = -(-N // P)
NP = NT * P
LAST = N - (NT - 1) * P
LOOPS = 625
CC = C // P
HEADS1, HID = 4, C // 4
MH, DH, KR = 8, 32, 4
FF = 4 * C
FM = FF // P
EX, ED = 8, 512
FE = ED // P
EPS = 1e-5
SLOPE = 0.2

HALF = 4
EC = -(-E // (P * 2 * HALF)) * 2 * HALF
BATCH = 4
TILES = -(-(E // P + NT) // (2 * BATCH)) * 2 * BATCH
NB = TILES // BATCH
DEPTH = 4
assert NB % DEPTH == 0
TT = TILES + BATCH
TR = TT // 4
SLOTS = TT * P
PAD_DST = NP + P - 1
FAR = float(1 << 22)


def blocks_of(nc, engine, k, b):
    _, found = nc.values_load_multi_w_load_instructions(
        k["block_row"][0:1, bass.ds((b + 1) * BATCH, BATCH)], engines=(engine,), min_val=0, max_val=NT - 1,
        skip_runtime_bounds_check_because="edge_tables bounds them")
    return found


class Steps:

    def __init__(self, eng, sem):
        self.eng, self.sem, self.n, self.turn = eng, sem, 0, None

    def did(self, ins):
        ins.then_inc(self.sem, 1)
        self.n += 1

    def settle(self):
        self.eng.wait_ge(self.sem, self.n if self.turn is None else self.turn * self.per + self.n)

    def link(self, ins):
        self.did(ins)
        self.settle()

    @contextmanager
    def loop(self, count, per):
        n0 = self.n
        with self.eng.Fori(0, count) as i:
            self.turn, self.per = i, per
            yield i
            assert self.n - n0 == per, (self.n - n0, per)
        self.n, self.turn = n0 + per * count, None


def build(nc, a, out, dbg=None):
    with ExitStack() as top:
        phases = iter(range(99))

        def alloc(stack):
            n = next(phases)
            return lambda name, shape, dt=F32: stack.enter_context(nc.sbuf_tensor(f"{name}_{n}", shape, dt))

        def sems(stack):
            taken = []

            def sem(name):
                taken.append(nc.alloc_semaphore(name=name))
                return taken[-1]

            def clear():
                nc.clear_and_free_semaphores(taken)
                nc.all_engine_barrier()
            stack.callback(clear)
            return sem

        sorted_edges = nc.dram_tensor("sorted_edges", [SLOTS, 2], I32).ap()
        dst_row = nc.dram_tensor("dst_row", [SLOTS], F32).ap()
        src_row = nc.dram_tensor("src_row", [SLOTS], F32).ap()
        table1 = nc.dram_tensor("table1", [NP, C + HEADS1], F32).ap()
        table2 = nc.dram_tensor("table2", [NP, C + 1], F32).ap()
        mixed = nc.dram_tensor("mixed", [NP, C], F32).ap()

        g = alloc(top)
        k = {
            "ident": g("ident", [P, P]), "ones": g("ones", [P, P]), "below": g("below", [P, P]),
            "iota_row": g("iota_row", [P, P]), "iota_col": g("iota_col", [P, 1]),
            "h1": g("h1", [P, NT, C]),
            "es1": g("es1", [P, NT, HEADS1]), "ed1": g("ed1", [P, NT, HEADS1]),
            "loops": g("loops", [P, NT]),
            "es2": g("es2", [P, NT, 1]), "ed2": g("ed2", [P, NT, 1]),
            "gat2_w": g("gat2_w", [P, CC, C + 2]),
            "src_col": g("src_col", [P, TT], I32), "dst_col": g("dst_col", [P, TT]),
            "hi_col": g("hi_col", [P, TT]), "block_row": g("block_row", [1, BATCH + TT], I32),
        }
        node_phase(nc, a, k, alloc, sems, sorted_edges, table1, mixed)
        edge_tables(nc, k, alloc, sems, sorted_edges, dst_row, src_row)
        with ExitStack() as layer:
            acc = alloc(layer)("acc1", [P, NT, C + HEADS1])
            wself = alloc(layer)("wself1", [P, NT, HEADS1])
            with ExitStack() as st:
                top_e = alloc(st)("top1", [P, NT, HEADS1])
                em = alloc(st)("em1", [P, NT, 2 * HEADS1])
                segment_max(nc, 1, HEADS1, k, k["es1"], k["ed1"], top_e, em, alloc, sems, src_row)
                weighted_sum(nc, 1, HEADS1, k, em, k["es1"], acc, wself, table1, alloc, sems, dst_row)
            between_layers(nc, a, k, acc, wself, alloc, sems, table2)
        with ExitStack() as layer:
            acc = alloc(layer)("acc2", [P, NT, C + 1])
            wself = alloc(layer)("wself2", [P, NT, 1])
            with ExitStack() as st:
                top_e = alloc(st)("top2", [P, NT, 1])
                em = alloc(st)("em2", [P, NT, 2])
                segment_max(nc, 2, 1, k, k["es2"], k["ed2"], top_e, em, alloc, sems, src_row)
                weighted_sum(nc, 2, 1, k, em, k["es2"], acc, wself, table2, alloc, sems, dst_row)
            experts(nc, a, k, acc, wself, alloc, sems, mixed, out)


def node_phase(nc, a, k, alloc, sems, sorted_edges, table1, mixed):
    with ExitStack() as st:
        sb, sem = alloc(st), sems(st)
        ident, ones, below = k["ident"], k["ones"], k["below"]
        dst_raw, src_raw = sb("dst_raw", [P, EC], I32), sb("src_raw", [P, EC], I32)
        fill = sb("fill", [P, TT, 2], I32)
        pair = sb("pair", [P, EC, 2], I32)
        blk_i = sb("blk_i", [P, EC], I32)
        blk, mask, rank, slot = (sb(n, [P, EC]) for n in ("blk", "mask", "rank", "slot"))
        slot_i = sb("slot_i", [P, EC], I32)
        ones_e = sb("ones_e", [P, EC])
        bnum = sb("bnum", [P, NT + 1])
        cnt, off, tl = sb("cnt", [P, NT]), sb("off", [P, NT]), sb("tl", [P, NT])
        tl_i = sb("tl_i", [P, NT], I32)
        cur_slot = sb("cur_slot", [P, 2, HALF], I32)
        cur_pair = sb("cur_pair", [P, 2, HALF, 2], I32)
        scratch = sb("pool_scratch", [1, 1])

        xn = sb("xn", [P, NT, C])
        stats, mv = sb("stats", [P, 6]), sb("mv", [P, NT, 2])
        mv_t, tick = sb("mv_t", [P, 2]), sb("tick", [1, 1])
        std, rstd = sb("std", [P, NT]), sb("rstd", [P, NT])
        hn, xcur = sb("hn", [P, C]), sb("xcur", [P, C])
        gat_w = sb("gat1_w", [P, CC, C + 2 * HEADS1])
        a_row = sb("a_row", [P, 4, C])
        prod = sb("prod", [P, C])
        xnT, hnT, xmT = (sb(n, [P, CC, P]) for n in ("xnT", "hnT", "xmT"))
        wx, wo = sb("wx", [P, CC, C]), sb("wo", [P, CC, C])
        wq, wk, wv = sb("wq", [P, CC, MH * KR]), sb("wk", [P, CC, MH * KR]), sb("wv", [P, CC, C])
        bias_cols = sb("bias_cols", [P, 5, CC])
        b1_col = sb("mix_b1_col", [P, FM])
        bo_row, b2_row = sb("bo_row", [1, C]), sb("mix_b2_row", [1, C])
        w1, w2 = sb("mix_w1", [P, CC, FF]), sb("mix_w2", [P, FM, C])
        v1 = sb("v1", [P, NT, C + 1])
        q = sb("q", [P, NT, MH, KR])
        qm = sb("qm", [P, NT, MH])
        QK = MH * KR
        kT, qT = sb("kT", [QK, NP]), sb("qT", [QK, NP])
        kmax = sb("kmax", [QK, 1])
        qcur, kcur, qTcur = sb("qcur", [P, QK]), sb("kcur", [QK, P]), sb("qTcur", [QK, P])
        zrow = sb("zrow", [1, C + 1])
        ek = sb("ek", [P, QK])
        kv, kvr = sb("kv", [QK, C]), sb("kvr", [QK, 1])
        headmask = sb("headmask", [QK, C])
        kvT = sb("kvT", [P, CC, QK])
        ko = sb("ko", [QK, C])
        gT = sb("gT", [P, FM, P])
        mixrow = sb("mixrow", [P, C])
        es1, ed1, h1 = k["es1"], k["ed1"], k["h1"]
        tabrow = sb("tabrow", [P, C + HEADS1])

        def pt(name, shape):
            return st.enter_context(nc.psum_tensor(name, shape, F32))
        ps_a, ps_b, ps_c, ps_d = (pt(f"ps_{n}", [P, 512]) for n in "abcd")
        ps_e, ps_f = pt("ps_e", [P, 512]), pt("ps_f", [P, 512])
        ps_g = pt("ps_g", [P, 2, 512])

        edges_pad, consts, fill_set, fill_out = (sem(n) for n in ("edges_pad", "consts", "fill_set", "fill_out"))
        edges_in, x_in, w_in, small_in = (sem(n) for n in ("edges_in", "x_in", "w_in", "small_in"))
        zeroed, v_own = sem("zeroed"), sem("node_dve_own")
        counted, prefixed, slots_set = sem("counted"), sem("prefixed"), sem("slots_set")
        pool_copied, scattered = sem("pool_copied"), [sem(f"scattered{j}") for j in range(2 * HALF)]
        w_set, var_set, std_set = sem("w_set"), sem("var_set"), sem("std_set")
        hn_set, xcur_set, turned = sem("hn_set"), sem("xcur_set"), sem("turned")
        xnT_set, hnT_set, xmT_set = sem("xnT_set"), sem("hnT_set"), sem("xmT_set")
        h_done, xm_done, qkv_done = sem("h_done"), sem("xm_done"), sem("qkv_done")
        row_set, h_out, v_out, qk_out, tab_out = (sem(n) for n in ("row_set", "h_out", "v_out", "qk_out", "tab_out"))
        q_set, qexp_set, qsoft_set, kmax_set, kexp_set = (sem(n) for n in ("q_set", "qexp_set", "qsoft_set", "kmax_set", "kexp_set"))
        cur_set, qk_turned, qT_set, kv_done = (sem(n) for n in ("cur_set", "qk_turned", "qT_set", "kv_done"))
        kv_set, kv_turned, kvT_set, ko_done, ko_set = (sem(n) for n in ("kv_set", "kv_turned", "kvT_set", "ko_done", "ko_set"))
        qTcur_set, attn_done, fx_set = sem("qTcur_set"), sem("attn_done"), sem("fx_set")
        fn_set, fn_turned, fnT_set = sem("fn_set"), sem("fn_turned"), sem("fnT_set")
        ff_done, g_set, m_done, mix_set, mix_out = (sem(n) for n in ("ff_done", "g_set", "m_done", "mix_set", "mix_out"))
        full = (P - 1) * EC
        loads = 18

        with nc.Block() as block:
            @block.sync
            def _(sp):
                sp.wait_ge(edges_pad, 2)
                for name, dst in (("dst", dst_raw), ("src", src_raw)):
                    sp.dma_start(dst[0:P - 1, :], a[name][0:full].rearrange("(p e) -> p e", e=EC)).then_inc(edges_in, 16)
                    sp.dma_start(dst[P - 1:P, 0:E - full],
                                 a[name][full:E].rearrange("(p e) -> p e", p=1)).then_inc(edges_in, 16)
                sp.wait_ge(zeroed, 1)
                sp.dma_start(xn[:, 0:NT - 1, :],
                             a["x"][0:(NT - 1) * P, :].rearrange("(t p) c -> p t c", p=P)).then_inc(x_in, 16)
                sp.dma_start(xn[0:LAST, NT - 1, :], a["x"][(NT - 1) * P:N, :]).then_inc(x_in, 16)
                sp.wait_ge(fill_set, 1)
                sp.dma_start(sorted_edges.rearrange("(p s) w -> p s w", p=P), fill[:]).then_inc(fill_out, 16)

                def chunks(w):
                    return w.rearrange("(c p) n -> p c n", p=P)
                n = 0
                for dst, src in ((gat_w[:, :, 0:C], chunks(a["L0_gnn_W1"])),
                                 (k["gat2_w"][:, :, 0:C], chunks(a["L0_gnn_W2"])),
                                 (wx[:], chunks(a["L0_mix_Wx"])), (wo[:], chunks(a["L0_mix_Wo"])),
                                 (w1[:], chunks(a["L0_mix_W1"])), (w2[:], chunks(a["L0_mix_W2"])),
                                 (bo_row[:], a["L0_mix_bo"].rearrange("(o n) -> o n", o=1)),
                                 (b2_row[:], a["L0_mix_b2"].rearrange("(o n) -> o n", o=1))):
                    sp.dma_start(dst, src).then_inc(w_in, 16)
                    n += 1
                for j, name in enumerate(("a1_src", "a1_dst", "a2_src", "a2_dst")):
                    sp.dma_start(a_row[:, j, :],
                                 a["L0_gnn_" + name].rearrange("h c -> (h c)").partition_broadcast(P)).then_inc(w_in, 16)
                    n += 1
                with nc.allow_non_contiguous_dma(reason="a bias of a few hundred values, one a partition"):
                    for j, name in enumerate(("ln1_g", "ln1_b", "bx", "ln2_g", "ln2_b")):
                        sp.dma_start(bias_cols[:, j, :], a["L0_mix_" + name].rearrange("(c p) -> p c", p=P)).then_inc(w_in, 16)
                        n += 1
                    sp.dma_start(b1_col[:], a["L0_mix_b1"].rearrange("(c p) -> p c", p=P)).then_inc(w_in, 16)
                assert n + 1 == loads
                sp.wait_ge(zeroed, 4)
                for h in range(MH):
                    c, r = h * DH // P, h * DH % P
                    for w, name, wide in ((wq, "Wq", KR), (wk, "Wk", KR), (wv, "Wv", DH)):
                        sp.dma_start(w[r:r + DH, c, h * wide:(h + 1) * wide], a["L0_mix_" + name]).then_inc(small_in, 16)
                sp.sem_inc(tab_out, 16)
                with sp.Fori(0, NT) as t:
                    sp.wait_ge(row_set, t + 1)
                    sp.dma_start(table1[bass.ds(t * P, P), :], tabrow[:]).then_inc(tab_out, 16)
                sp.sem_inc(mix_out, 16)
                with sp.Fori(0, NT) as t:
                    sp.wait_ge(mix_set, t + 1)
                    sp.dma_start(mixed[bass.ds(t * P, P), :], mixrow[:]).then_inc(mix_out, 16)
                sp.wait_ge(tab_out, 16 * (NT + 1))
                sp.wait_ge(mix_out, 16 * (NT + 1))

            @block.gpsimd
            def _(pool):
                own = Steps(pool, consts)
                pool.memset(dst_raw[:], PAD_DST).then_inc(edges_pad, 1)
                pool.memset(src_raw[:], 0).then_inc(edges_pad, 1)
                own.link(pool.memset(ones[:], 1.0))
                own.did(pool.affine_select(out=ident[:], in_=ones[:], compare_op=ALU.is_equal, fill=0.0, base=0,
                                           pattern=[[-1, P]], channel_multiplier=1))
                own.did(pool.affine_select(out=below[:], in_=ones[:], compare_op=ALU.is_gt, fill=0.0, base=0,
                                           pattern=[[1, P]], channel_multiplier=-1))
                for out_, pattern, step in ((k["iota_row"], [[1, P]], 0), (k["iota_col"], [[1, 1]], 1), (bnum, [[1, NT + 1]], 0)):
                    own.did(pool.iota(out_[:], pattern, base=0, channel_multiplier=step,
                                      allow_small_or_imprecise_dtypes=True))
                own.did(pool.memset(scratch[:], 0.0))
                own.did(pool.affine_select(out=k["loops"][:], in_=ones[:, 0:NT], compare_op=ALU.is_ge, fill=0.0,
                                           base=LOOPS - 1, pattern=[[-P, NT]], channel_multiplier=-1))
                own.link(pool.memset(headmask[:], 1.0))
                hm = headmask[:].rearrange("q (h d) -> q h d", d=DH)
                own.link(pool.affine_select(out=hm, in_=hm, compare_op=ALU.is_ge, fill=0.0, base=0,
                                            pattern=[[-KR, MH], [0, DH]], channel_multiplier=1))
                own.link(pool.affine_select(out=hm, in_=hm, compare_op=ALU.is_ge, fill=0.0, base=KR - 1,
                                            pattern=[[KR, MH], [0, DH]], channel_multiplier=-1))
                bound = pool.to_reg(SLOTS - 1)
                pool.wait_ge(slots_set, 1)
                pool.wait_ge(fill_out, 16)

                def half(i, y, again):
                    if again:
                        for j in range(HALF):
                            pool.wait_ge(scattered[y * HALF + j], 16 * i)
                    at = i * 2 * HALF + y * HALF
                    pool.tensor_copy(cur_slot[:, y, :], slot_i[:, bass.ds(at, HALF)]).then_inc(pool_copied, 1)
                    pool.tensor_copy(cur_pair[:, y], pair[:, bass.ds(at, HALF), :]).then_inc(pool_copied, 1)
                    pool.wait_ge(pool_copied, (i * 2 + y + 1) * 2)
                    pool.tensor_tensor(scratch[:], ones[0:1, 0:1], ones[0:1, 0:1], ALU.add).then_inc(consts, 1)
                    for j in range(HALF):
                        pool.indirect_dma_start(sorted_edges, bass.IndirectOffsetOnAxis(cur_slot[:, y, j:j + 1], 0),
                                                cur_pair[:, y, j, :], None, bounds_check=bound,
                                                oob_is_err=False).then_inc(scattered[y * HALF + j], 16)
                half(0, 0, False)
                half(0, 1, False)
                with pool.Fori(1, EC // (2 * HALF)) as i:
                    half(i, 0, True)
                    half(i, 1, True)
                for s in scattered:
                    pool.wait_ge(s, 16 * (EC // (2 * HALF)))

            @block.vector
            def _(dve):
                own = Steps(dve, v_own)
                link = own.link

                def copy(dst, src):
                    return dve.tensor_scalar(dst, src, 1.0, None, ALU.mult)
                dve.memset(xn[:, NT - 1, :], 0.0).then_inc(zeroed, 1)
                for w in (wq, wk, wv):
                    dve.memset(w[:], 0.0).then_inc(zeroed, 1)
                own.did(dve.memset(ones_e[:], 1.0))
                own.did(dve.memset(zrow[:], 0.0))
                own.did(dve.memset(v1[:, :, C:C + 1], 1.0))
                link(dve.memset(fill[:, :, 0], 0))
                dve.memset(fill[:, :, 1], PAD_DST).then_inc(fill_set, 1)
                dve.wait_ge(edges_in, 64)
                dve.wait_ge(consts, 11)
                own.did(dve.tensor_copy(pair[:, :, 0], src_raw[:]))
                own.did(dve.tensor_copy(pair[:, :, 1], dst_raw[:]))
                link(dve.tensor_scalar(blk_i[:], dst_raw[:], 7, None, ALU.arith_shift_right))
                link(dve.tensor_copy(blk[:], blk_i[:]))
                with own.loop(NT, 1) as b:
                    link(dve.tensor_scalar(mask[:], blk[:], bnum[:, bass.ds(b, 1)], None, ALU.is_equal, ALU.add,
                                           accum_out=cnt[:, bass.ds(b, 1)]))
                dve.tensor_copy(off[:], cnt[:]).then_inc(counted, 1)
                dve.wait_ge(prefixed, 2)
                link(dve.tensor_copy(tl_i[:], ps_a[:, 0:NT]))
                link(dve.tensor_scalar(tl[:], tl_i[:], float(P - 1), None, ALU.add))
                link(dve.tensor_copy(tl_i[:], tl[:]))
                link(dve.tensor_scalar(tl_i[:], tl_i[:], 7, None, ALU.arith_shift_right))
                link(dve.tensor_copy(tl[:], tl_i[:]))
                link(dve.tensor_tensor_scan(cnt[:], ones_e[:, 0:NT], tl[:], 0.0, ALU.mult, ALU.add))
                link(dve.tensor_tensor(cnt[:], cnt[:], tl[:], ALU.subtract))
                link(dve.scalar_tensor_tensor(off[:], cnt[:], float(P), ps_b[:, 0:NT], ALU.mult, ALU.add))
                link(dve.tensor_scalar(slot[:], blk[:], float(NT), FAR, ALU.is_equal, ALU.mult))
                with own.loop(NT, 4) as b:
                    link(dve.tensor_scalar(mask[:], blk[:], bnum[:, bass.ds(b, 1)], None, ALU.is_equal))
                    link(dve.tensor_tensor_scan(rank[:], ones_e[:], mask[:], off[:, bass.ds(b, 1)], ALU.mult, ALU.add))
                    link(dve.tensor_tensor(rank[:], rank[:], mask[:], ALU.mult))
                    link(dve.tensor_tensor(slot[:], slot[:], rank[:], ALU.add))
                link(dve.tensor_scalar(slot[:], slot[:], -1.0, None, ALU.add))
                dve.tensor_copy(slot_i[:], slot[:]).then_inc(slots_set, 1)

                dve.wait_ge(w_in, 16 * loads)
                for layer, w, heads in ((0, gat_w, HEADS1), (1, k["gat2_w"], 1)):
                    for side in range(2):
                        for c in range(CC):
                            link(dve.tensor_tensor(prod[:], w[:, c, 0:C], a_row[:, 2 * layer + side, :], ALU.mult))
                            link(dve.tensor_reduce(w[:, c, C + side * heads:C + (side + 1) * heads],
                                                   prod[:].rearrange("p (h d) -> p h d", h=heads), AX.X, ALU.add))
                dve.sem_inc(w_set, 1)

                def root(n):
                    dve.tensor_scalar(rstd[:], mv[:, :, 1], EPS, None, ALU.add).then_inc(var_set, 1)
                    dve.wait_ge(std_set, n)
                    link(dve.reciprocal(rstd[:], std[:]))

                def normed(dst, t):
                    return dve.tensor_scalar(dst, tile_of(xn, t), mv[:, bass.ds(t, 1), 0:1].rearrange("p o c -> p (o c)"),
                                             rstd[:, bass.ds(t, 1)], ALU.subtract, ALU.mult)

                def moments(t):
                    own.did(dve.memset(tick[:], 0.0))
                    link(dve.bn_stats(stats[:], tile_of(xn, t)))
                    own.did(dve.memset(tick[:], 0.0))
                    own.did(dve.bn_aggr(mv_t[:], stats[:]))
                    own.settle()
                    link(copy(tile_of(mv, t), mv_t[:]))
                dve.wait_ge(x_in, 32)
                dve.wait_ge(zeroed, 1)
                with own.loop(NT, 5) as t:
                    moments(t)
                root(1)
                with own.loop(NT, 6) as t:
                    link(normed(tile_of(xn, t), t))
                    moments(t)
                root(2)
                dve.sem_inc(qk_out, 2)
                with own.loop(NT, 0) as t:
                    dve.wait_ge(turned, t + 1)
                    normed(hn[:], t).then_inc(hn_set, 1)
                    dve.wait_ge(turned, t + 2)
                    for c in range(CC):
                        dve.tensor_scalar(hnT[:, c, :], ps_b[:, c * P:(c + 1) * P], bias_cols[:, 0, c:c + 1],
                                          bias_cols[:, 1, c:c + 1], ALU.mult, ALU.add).then_inc(hnT_set, 1)
                    dve.wait_ge(xm_done, t + 1)
                    for c in range(CC):
                        dve.tensor_scalar(xmT[:, c, :], ps_d[:, c * P:(c + 1) * P], bias_cols[:, 2, c:c + 1],
                                          None, ALU.add).then_inc(xmT_set, 1)
                    dve.wait_ge(qkv_done, t + 1)
                    copy(q[:, bass.ds(t, 1)].rearrange("p o h r -> p (o h r)"), ps_f[:, P:P + QK]).then_inc(qk_out, 1)
                    copy(kT[:, bass.ds(t * P, P)], ps_f[0:QK, 0:P]).then_inc(qk_out, 1)
                dve.wait_ge(qk_out, 2 * NT + 2)
                link(dve.tensor_reduce(qm[:], q[:], AX.X, ALU.max))
                dve.tensor_tensor(q[:], q[:], qm[:].unsqueeze(3).to_broadcast([P, NT, MH, KR]), ALU.subtract).then_inc(q_set, 1)
                link(dve.tensor_reduce(kmax[:], kT[:, 0:N], AX.X, ALU.max))
                dve.tensor_scalar(kmax[:], kmax[:], -1.0, None, ALU.mult).then_inc(kmax_set, 1)
                dve.wait_ge(qexp_set, 1)
                link(dve.tensor_reduce(qm[:], q[:], AX.X, ALU.add))
                link(dve.reciprocal(qm[:], qm[:]))
                link(dve.tensor_tensor(q[:], q[:], qm[:].unsqueeze(3).to_broadcast([P, NT, MH, KR]), ALU.mult))
                dve.wait_ge(kexp_set, 1)
                dve.memset(kT[:, N:NP], 0.0).then_inc(qsoft_set, 1)
                with own.loop(NT, 0) as t:
                    dve.wait_ge(qk_turned, t + 2)
                    dve.wait_ge(kv_done, t + 1)
                    copy(qT[:, bass.ds(t * P, P)], ps_a[0:QK, 0:P]).then_inc(qT_set, 1)
                    dve.tensor_copy(ek[:], ps_b[:, 0:QK]).then_inc(qT_set, 1)
                dve.wait_ge(kv_done, NT + 2)
                link(dve.reciprocal(kvr[:], ps_c[0:QK, C:C + 1]))
                dve.scalar_tensor_tensor(kv[:], ps_c[0:QK, 0:C], kvr[:, 0:1], headmask[:], ALU.mult, ALU.mult).then_inc(kv_set, 1)
                dve.wait_ge(kv_turned, 1)
                dve.tensor_copy(kvT[:].rearrange("p c q -> p (c q)"), ps_a[:, 0:CC * QK]).then_inc(kvT_set, 1)
                dve.wait_ge(ko_done, 1)
                dve.tensor_copy(ko[:], ps_b[0:QK, 0:C]).then_inc(ko_set, 1)
                with own.loop(NT, 5) as t:
                    dve.wait_ge(attn_done, t + 1)
                    dve.tensor_tensor(tile_of(xn, t), ps_d[:, 0:C], tile_of(xn, t), ALU.add).then_inc(fx_set, 1)
                    dve.wait_ge(fx_set, t + 2)
                    moments(t)
                root(3)
                with own.loop(NT, 0) as t:
                    dve.wait_ge(fn_turned, t + 1)
                    normed(hn[:], t).then_inc(fn_set, 1)
                    dve.wait_ge(fn_turned, t + 2)
                    for c in range(CC):
                        dve.tensor_scalar(hnT[:, c, :], ps_a[:, c * P:(c + 1) * P], bias_cols[:, 3, c:c + 1],
                                          bias_cols[:, 4, c:c + 1], ALU.mult, ALU.add).then_inc(fnT_set, 1)
                    dve.wait_ge(m_done, t + 1)
                    dve.wait_ge(mix_out, 16 * (t + 1))
                    dve.tensor_tensor(mixrow[:], ps_d[:, 0:C], tile_of(xn, t), ALU.add).then_inc(mix_set, 1)

            @block.scalar
            def _(act):
                for n in range(2):
                    act.wait_ge(var_set, n + 1)
                    act.activation(std[:], rstd[:], ACT.Sqrt).then_inc(std_set, 1)
                act.sem_inc(h_out, 3)
                act.sem_inc(v_out, 1)
                with act.Fori(0, NT) as t:
                    act.wait_ge(hn_set, t + 1)
                    act.wait_ge(turned, t + 1)
                    act.activation(xcur[:], tile_of(xn, t), ACT.Copy).then_inc(xcur_set, 1)
                    act.wait_ge(turned, t + 2)
                    act.activation(xnT[:].rearrange("p c n -> p (c n)"), ps_a[:, 0:C], ACT.Copy).then_inc(xnT_set, 1)
                    act.wait_ge(h_done, t + 1)
                    act.wait_ge(tab_out, 16 * (t + 1))
                    act.activation(tabrow[:], ps_c[:, 0:C + HEADS1], ACT.Copy).then_inc(row_set, 1)
                    act.activation(tile_of(h1, t), ps_c[:, 0:C], ACT.Copy).then_inc(h_out, 1)
                    act.activation(tile_of(es1, t), ps_c[:, C:C + HEADS1], ACT.Copy).then_inc(h_out, 1)
                    act.activation(tile_of(ed1, t), ps_c[:, C + HEADS1:C + 2 * HEADS1], ACT.Copy).then_inc(h_out, 1)
                    act.wait_ge(qkv_done, t + 1)
                    act.activation(v1[:, bass.ds(t, 1), 0:C].rearrange("p o c -> p (o c)"), ps_e[:, 0:C],
                                   ACT.Copy).then_inc(v_out, 1)
                act.wait_ge(q_set, 1)
                act.activation(q[:], q[:], ACT.Exp).then_inc(qexp_set, 1)
                act.wait_ge(kmax_set, 1)
                act.activation(kT[:, 0:N], kT[:, 0:N], ACT.Exp, bias=kmax[:, 0:1]).then_inc(kexp_set, 1)
                act.wait_ge(qsoft_set, 1)
                with act.Fori(0, NT) as t:
                    act.wait_ge(qk_turned, t + 1)
                    act.activation(qcur[:], q[:, bass.ds(t, 1)].rearrange("p o h r -> p (o h r)"), ACT.Copy).then_inc(cur_set, 1)
                    act.activation(kcur[:], kT[:, bass.ds(t * P, P)], ACT.Copy).then_inc(cur_set, 1)
                act.wait_ge(qT_set, 2 * NT)
                with act.Fori(0, NT) as t:
                    act.wait_ge(fx_set, t + 1)
                    act.activation(qTcur[:], qT[:, bass.ds(t * P, P)], ACT.Copy).then_inc(qTcur_set, 1)
                act.wait_ge(var_set, 3)
                act.activation(std[:], rstd[:], ACT.Sqrt).then_inc(std_set, 1)
                act.preload_act_table(ACT.Gelu)
                with act.Fori(0, NT) as t:
                    act.wait_ge(ff_done, t + 1)
                    for f in range(FM):
                        act.activation(gT[:, f, :], ps_g[:].rearrange("p b n -> p (b n)")[:, f * P:(f + 1) * P], ACT.Gelu,
                                       bias=b1_col[:, f:f + 1]).then_inc(g_set, 1)

            @block.tensor
            def _(pe):
                pe.wait_ge(counted, 1)
                pe.matmul(ps_a[:, 0:NT], ones[:], cnt[:], start=True, stop=True).then_inc(prefixed, 1)
                pe.matmul(ps_b[:, 0:NT], below[:], cnt[:], start=True, stop=True).then_inc(prefixed, 1)
                pe.wait_ge(small_in, 16 * 3 * MH)
                pe.wait_ge(w_set, 1)
                pe.wait_ge(w_in, 16 * loads)
                pe.wait_ge(slots_set, 1)
                pe.sem_inc(turned, 1)
                with pe.Fori(0, NT) as t:
                    pe.wait_ge(hn_set, t + 1)
                    pe.wait_ge(xcur_set, t + 1)
                    for c in range(CC):
                        pe.transpose(ps_a[:, c * P:(c + 1) * P], xcur[:, c * P:(c + 1) * P], ident[:])
                    for c in range(CC):
                        last = pe.transpose(ps_b[:, c * P:(c + 1) * P], hn[:, c * P:(c + 1) * P], ident[:])
                    last.then_inc(turned, 1)
                    pe.wait_ge(xnT_set, t + 1)
                    pe.wait_ge(h_out, 3 * t + 3)
                    for c in range(CC):
                        last = pe.matmul(ps_c[:, 0:C + 2 * HEADS1], xnT[:, c, :], gat_w[:, c, :], start=c == 0, stop=c == CC - 1)
                    last.then_inc(h_done, 1)
                    pe.wait_ge(hnT_set, 2 * t + 2)
                    for m in range(CC):
                        for c in range(CC):
                            last = pe.matmul(ps_d[:, m * P:(m + 1) * P], wx[:, c, m * P:(m + 1) * P], hnT[:, c, :],
                                             start=c == 0, stop=c == CC - 1)
                    last.then_inc(xm_done, 1)
                    pe.wait_ge(xmT_set, 2 * t + 2)
                    pe.wait_ge(v_out, t + 1)
                    pe.wait_ge(qk_out, 2 * t + 2)
                    for c in range(CC):
                        pe.matmul(ps_e[:, 0:C], xmT[:, c, :], wv[:, c, :], start=c == 0, stop=c == CC - 1)
                    for c in range(CC):
                        pe.matmul(ps_f[:, P:P + QK], xmT[:, c, :], wq[:, c, :], start=c == 0, stop=c == CC - 1)
                    for c in range(CC):
                        last = pe.matmul(ps_f[0:QK, 0:P], wk[:, c, :], xmT[:, c, :], start=c == 0, stop=c == CC - 1)
                    last.then_inc(qkv_done, 1)
                pe.sem_inc(qk_turned, 1)
                pe.wait_ge(h_out, 3 * NT + 3)
                pe.matmul(ps_c[0:QK, 0:C + 1], zrow[:, 0:QK], zrow[:], start=True, stop=False,
                          skip_group_check=True).then_inc(kv_done, 1)
                with pe.Fori(0, NT) as t:
                    pe.wait_ge(cur_set, 2 * t + 2)
                    pe.transpose(ps_a[0:QK, 0:P], qcur[:], ident[:])
                    pe.transpose(ps_b[:, 0:QK], kcur[:], ident[0:QK, 0:QK]).then_inc(qk_turned, 1)
                    pe.wait_ge(qT_set, 2 * t + 2)
                    pe.matmul(ps_c[0:QK, 0:C + 1], ek[:], tile_of(v1, t), start=False, stop=False,
                              skip_group_check=True).then_inc(kv_done, 1)
                pe.matmul(ps_c[0:QK, 0:C + 1], zrow[:, 0:QK], zrow[:], start=False, stop=True,
                          skip_group_check=True).then_inc(kv_done, 1)
                pe.wait_ge(kv_set, 1)
                for c in range(CC):
                    last = pe.transpose(ps_a[:, c * QK:(c + 1) * QK], kv[:, c * P:(c + 1) * P], ident[0:QK, 0:QK])
                last.then_inc(kv_turned, 1)
                pe.wait_ge(kvT_set, 1)
                for c in range(CC):
                    last = pe.matmul(ps_b[0:QK, 0:C], kvT[:, c, :], wo[:, c, :], start=c == 0, stop=c == CC - 1)
                last.then_inc(ko_done, 1)
                pe.wait_ge(ko_set, 1)
                pe.sem_inc(fx_set, 1)
                with pe.Fori(0, NT) as t:
                    pe.wait_ge(qTcur_set, t + 1)
                    pe.matmul(ps_d[:, 0:C], qTcur[:], ko[:], start=True, stop=False)
                    pe.matmul(ps_d[:, 0:C], ones[0:1, :], bo_row[:], start=False, stop=True).then_inc(attn_done, 1)
                pe.sem_inc(fn_turned, 1)
                with pe.Fori(0, NT) as t:
                    pe.wait_ge(fn_set, t + 1)
                    for c in range(CC):
                        last = pe.transpose(ps_a[:, c * P:(c + 1) * P], hn[:, c * P:(c + 1) * P], ident[:])
                    last.then_inc(fn_turned, 1)
                    pe.wait_ge(fnT_set, 2 * t + 2)
                    for f in range(FM):
                        for c in range(CC):
                            last = pe.matmul(ps_g[:].rearrange("p b n -> p (b n)")[:, f * P:(f + 1) * P],
                                             w1[:, c, f * P:(f + 1) * P], hnT[:, c, :], start=c == 0, stop=c == CC - 1)
                    last.then_inc(ff_done, 1)
                    pe.wait_ge(g_set, FM * (t + 1))
                    pe.matmul(ps_d[:, 0:C], ones[0:1, :], b2_row[:], start=True, stop=False)
                    for f in range(FM):
                        last = pe.matmul(ps_d[:, 0:C], gT[:, f, :], w2[:, f, :], start=False, stop=f == FM - 1)
                    last.then_inc(m_done, 1)


def edge_tables(nc, k, alloc, sems, sorted_edges, dst_row, src_row):
    with ExitStack() as st:
        sb, sem = alloc(st), sems(st)
        rows = sb("rows", [TR, 4, P, 2], I32)
        part = sb("part", [TR, 4, P], I32)
        names = ("src_f", "dst_lo", "src_hi", "block", "src_lo", "pad")
        src_f, dst_lo, src_hi, block_f, src_lo, pad = (sb(n, [TR, 4, P]) for n in names)
        ps = [st.enter_context(nc.psum_tensor(f"ps_t{j}", [P, 512], F32)) for j in range(4)]
        rows_in, own_s, rows_set, turned = sem("rows_in"), sem("tables_own"), sem("rows_set"), sem("tables_turned")
        rows_out = sem("rows_out")
        with nc.Block() as block:
            @block.sync
            def _(sp):
                sp.dma_start(rows[:].rearrange("t c p w -> t c (p w)"),
                             sorted_edges.rearrange("(c t p) w -> t c (p w)", c=4, p=P)).then_inc(rows_in, 16)
                sp.wait_ge(rows_set, 1)
                sp.dma_start(dst_row.rearrange("(c t p) -> t c p", c=4, p=P), dst_lo[:]).then_inc(rows_out, 16)
                sp.dma_start(src_row.rearrange("(c t p) -> t c p", c=4, p=P), src_lo[:]).then_inc(rows_out, 16)
                sp.wait_ge(rows_out, 32)

            @block.vector
            def _(dve):
                own = Steps(dve, own_s)
                link = own.link
                dve.wait_ge(rows_in, 16)
                src, dst = rows[:, :, :, 0], rows[:, :, :, 1]
                own.did(dve.tensor_copy(src_f[:], src))
                link(dve.tensor_copy(pad[:], dst))
                own.did(dve.tensor_scalar(pad[:], pad[:], float(NP), float(P), ALU.is_ge, ALU.mult))
                link(dve.tensor_scalar(part[:], dst, P - 1, None, ALU.bitwise_and))
                link(dve.tensor_copy(dst_lo[:], part[:]))
                link(dve.tensor_tensor(dst_lo[:], dst_lo[:], pad[:], ALU.add))
                link(dve.tensor_scalar(part[:], src, P - 1, None, ALU.bitwise_and))
                link(dve.tensor_copy(src_lo[:], part[:]))
                link(dve.tensor_scalar(part[:], src, 7, None, ALU.arith_shift_right))
                link(dve.tensor_copy(src_hi[:], part[:]))
                link(dve.tensor_scalar(part[:], dst, 7, None, ALU.arith_shift_right))
                link(dve.tensor_copy(block_f[:], part[:]))
                dve.tensor_scalar(block_f[:], block_f[:], float(NT - 1), None, ALU.min).then_inc(rows_set, 1)
                dve.wait_ge(turned, 4)
                for j, dst_t in enumerate((k["src_col"][:], k["dst_col"][:], k["hi_col"][:])):
                    dve.tensor_copy(dst_t, ps[j][:, 0:TT])
                own.did(dve.memset(k["block_row"][:, 0:BATCH], 0))
                own.did(dve.tensor_copy(k["block_row"][:, BATCH:], ps[3][0:1, 0:TT]))
                own.settle()

            @block.tensor
            def _(pe):
                pe.wait_ge(rows_set, 1)
                for j, t in enumerate((src_f, dst_lo, src_hi, block_f)):
                    for c in range(4):
                        last = pe.transpose(ps[j][:, c * TR:(c + 1) * TR], t[:, c, :], k["ident"][0:TR, 0:TR])
                    last.then_inc(turned, 1)


def segment_max(nc, layer, H, k, es, ed, top_e, em, alloc, sems, src_row):
    with ExitStack() as st:
        sb, sem = alloc(st), sems(st)

        def s(name):
            return sem(f"{name}_{layer}")
        low, low_row, floor_ = sb("low", [P, 1]), sb("low_row", [1, 1]), sb("floor", [P, 1])
        raised = sb("raised", [P, NT, H])
        zeros = sb("zeros", [1, H * P])
        src_b = sb("src_b", [P, 2, BATCH * P])
        pick_lo = sb("pick_lo", [P, 2, BATCH * P])
        pick_hi = sb("pick_hi", [P, 2, BATCH, NT])
        picked = sb("picked", [P, BATCH, NT, H])
        es_e = sb("es_e", [P, 2, BATCH, H])
        spread = sb("spread", [P, 2, BATCH, H, P])
        best = sb("best", [P, BATCH, H])
        is_dst = sb("is_dst", [P, 2, BATCH, P if H > 1 else 1])
        iota_row, iota_col = k["iota_row"], k["iota_col"]
        ps_f = [st.enter_context(nc.psum_tensor(f"ps_f{y}_{layer}", [P, 512], F32)) for y in range(2)]
        ps_v = st.enter_context(nc.psum_tensor(f"ps_v_{layer}", [P, BATCH, 512], F32))
        own_s, low_set, low_turned, low_spread = s("max_own"), s("low_set"), s("low_turned"), s("low_spread")
        src_in = [s(f"src_in{y}") for y in range(2)]
        picks_set, fetched, fetch_read = s("picks_set"), s("fetched"), s("fetch_read")
        es_set, dst_set, spread_set, turned, best_set = s("es_set"), s("dst_set"), s("spread_set"), s("spread_turned"), s("best_set")
        picks_free = s("picks_free")
        src_rows = src_row.rearrange("(b n) -> b n", n=BATCH * P)

        with nc.Block() as block:
            @block.sync
            def _(sp):
                def fetch(i, y):
                    b = i * 2 + y
                    sp.wait_ge(picks_free, b + 1)
                    sp.dma_start(src_b[:, y, :], src_rows[bass.ds(b, 1), :].to_broadcast([P, BATCH * P])).then_inc(src_in[y], 16)
                with sp.Fori(0, NB // 2) as i:
                    fetch(i, 0)
                    fetch(i, 1)
                fetch(NB // 2, 0)

            @block.vector
            def _(dve):
                own = Steps(dve, own_s)
                link = own.link
                own.did(dve.memset(zeros[:], 0.0))
                link(dve.tensor_reduce(low[:], es[:].rearrange("p t h -> p (t h)"), AX.X, ALU.min))
                dve.sem_inc(low_set, 1)
                dve.wait_ge(low_turned, 1)
                dve.tensor_reduce(low_row[:], ps_f[0][0:1, 0:P], AX.X, ALU.min).then_inc(low_set, 1)
                dve.wait_ge(low_spread, 1)
                link(dve.tensor_scalar(floor_[:], ps_f[1][:, 0:1], -1.0, None, ALU.add))
                link(dve.tensor_scalar(raised[:], es[:], floor_[:, 0:1], None, ALU.subtract))
                link(dve.tensor_tensor(top_e[:], raised[:], k["loops"][:].unsqueeze(2).to_broadcast([P, NT, H]), ALU.mult))
                dve.sem_inc(picks_free, 2)
                dve.sem_inc(fetch_read, 2)
                dve.sem_inc(best_set, BATCH)

                def picks(i, y):
                    b = i * 2 + y
                    dve.wait_ge(src_in[y], (i + 1) * 16)
                    dve.wait_ge(fetched, b + 1)
                    dve.tensor_scalar(pick_lo[:, y, :], src_b[:, y, :], iota_col[:, 0:1], None, ALU.is_equal).then_inc(picks_free, 1)
                    dve.tensor_tensor(pick_hi[:, y], iota_row[:, 0:NT].unsqueeze(1).to_broadcast([P, BATCH, NT]),
                                      k["hi_col"][:, bass.ds(b * BATCH, BATCH)].unsqueeze(2).to_broadcast([P, BATCH, NT]),
                                      ALU.is_equal).then_inc(picks_set, 1)

                def fold(b, between):
                    blocks = blocks_of(nc, mybir.EngineType.DVE, k, b)
                    for j in range(BATCH + 1):
                        if j < BATCH:
                            between(j)
                            dve.wait_ge(turned, BATCH * (b + 2) + j + 1)
                            dve.tensor_reduce(best[:, j, :], ps_v[:, j, 0:H * P].rearrange("p (h e) -> p h e", h=H), AX.X,
                                              ALU.max).then_inc(best_set, 1)
                        if j > 0:
                            at = top_e[:, bass.ds(blocks[j - 1], 1), :].rearrange("p o h -> p (o h)")
                            dve.wait_ge(best_set, BATCH * (b + 2) + j)
                            own.settle()
                            own.did(dve.tensor_tensor(at, at, best[:, j - 1, :], ALU.max))

                def step(i, y):
                    b = i * 2 + y
                    picks(*((i, 1) if y == 0 else (i + 1, 0)))
                    dve.wait_ge(fetched, b + 3)
                    dve.wait_ge(picks_set, b + 1)
                    dve.tensor_tensor(picked[:], ps_f[y][:, 0:BATCH * NT * H].rearrange("p (k t h) -> p k t h", k=BATCH, h=H),
                                      pick_hi[:, y].unsqueeze(3).to_broadcast([P, BATCH, NT, H]), ALU.mult).then_inc(fetch_read, 1)
                    dve.wait_ge(fetch_read, b + 3)
                    dve.tensor_reduce(es_e[:, y], picked[:].rearrange("p k t h -> p k h t"), AX.X, ALU.add).then_inc(es_set, 1)
                    dve.wait_ge(turned, BATCH * (b + 1))

                    def to_dst(j):
                        dst = k["dst_col"][:, bass.ds(b * BATCH + j, 1)]
                        if H == 1:
                            dve.wait_ge(es_set, b + 1)
                            last = dve.tensor_scalar(spread[:, y, j, 0, :], iota_row[:], dst, es_e[:, y, j, 0:1],
                                                     ALU.is_equal, ALU.mult)
                        else:
                            last = dve.tensor_scalar(is_dst[:, y, j, :], iota_row[:], dst, None, ALU.is_equal)
                        last.then_inc(dst_set, 1)
                    fold(b - 1, to_dst)

                picks(0, 0)
                with own.loop(NB // 2, 2 * BATCH) as i:
                    step(i, 0)
                    step(i, 1)
                fold(NB - 1, lambda j: None)
                own.settle()
                m = em[:, :, H:2 * H]
                link(dve.tensor_copy(em[:, :, 0:H], ed[:]))
                link(dve.scalar_tensor_tensor(top_e[:], top_e[:], floor_[:, 0:1], ed[:], ALU.add, ALU.add))
                link(dve.scalar_tensor_tensor(m, top_e[:], SLOPE, top_e[:], ALU.mult, ALU.max))

            if H > 1:
                @block.scalar
                def _(act):
                    with act.Fori(0, NB // 2) as i:
                        for y in range(2):
                            b = i * 2 + y
                            act.wait_ge(turned, BATCH * (b + 1))
                            act.wait_ge(es_set, b + 1)
                            for j in range(BATCH):
                                act.wait_ge(dst_set, BATCH * b + j + 1)
                                for h in range(H):
                                    act.activation(spread[:, y, j, h, :], is_dst[:, y, j, :], ACT.Copy,
                                                   scale=es_e[:, y, j, h:h + 1]).then_inc(spread_set, 1)

            @block.tensor
            def _(pe):
                pe.sem_inc(turned, BATCH)
                pe.wait_ge(low_set, 1)
                for j in range(BATCH):
                    pe.matmul(ps_v[:, j, 0:H * P], zeros[:, 0:P], zeros[:, 0:H * P], start=True, stop=True).then_inc(turned, 1)
                pe.transpose(ps_f[0][0:1, 0:P], low[:], k["ident"][:]).then_inc(low_turned, 1)
                pe.wait_ge(low_set, 2)
                pe.matmul(ps_f[1][:, 0:1], k["ones"][0:1, :], low_row[:], start=True, stop=True).then_inc(low_spread, 1)
                pe.sem_inc(fetched, 2)

                def fetch(i, y):
                    b = i * 2 + y
                    pe.wait_ge(picks_set, b + 1)
                    pe.wait_ge(fetch_read, b + 1)
                    for j in range(BATCH):
                        last = pe.matmul(ps_f[y][:, j * NT * H:(j + 1) * NT * H], pick_lo[:, y, j * P:(j + 1) * P],
                                         raised[:].rearrange("p t h -> p (t h)"), start=True, stop=True)
                    last.then_inc(fetched, 1)

                def step(i, y):
                    b = i * 2 + y
                    fetch(*((i, 1) if y == 0 else (i + 1, 0)))
                    if H == 1:
                        pe.wait_ge(dst_set, BATCH * (b + 1))
                    else:
                        pe.wait_ge(spread_set, BATCH * H * (b + 1))
                    for j in range(BATCH):
                        pe.wait_ge(best_set, BATCH * (b + 1) + j + 1)
                        for h in range(H):
                            last = pe.transpose(ps_v[:, j, h * P:(h + 1) * P], spread[:, y, j, h, :], k["ident"][:])
                        last.then_inc(turned, 1)

                fetch(0, 0)
                with pe.Fori(0, NB // 2) as i:
                    step(i, 0)
                    step(i, 1)


def weighted_sum(nc, layer, H, k, em, es, acc, wself, table, alloc, sems, dst_row):
    with ExitStack() as st:
        sb, sem = alloc(st), sems(st)

        def s(name):
            return sem(f"{name}_{layer}")
        W = C + H
        BY_ACT = 2 if H > 1 else BATCH
        zeros = sb("zeros", [1, W])
        dst_b = sb("dst_b", [P, 2, BATCH * P])
        to_edge = sb("to_edge", [P, 2, BATCH * P])
        to_dst = sb("to_dst", [P, DEPTH, BATCH, P])
        rows = sb("rows_h", [P, DEPTH, BATCH, W])
        logit, leaky = sb("logit", [P, 2, BATCH, H]), sb("leaky", [P, 2, BATCH, H])
        cur = sb("cur_src", [P, DEPTH, BATCH], I32)
        scratch = sb("pool_scratch_h", [1, 1])
        tself = sb("tself", [P, NT, H])
        ps_e = [st.enter_context(nc.psum_tensor(f"ps_e{y}_{layer}", [P, 512], F32)) for y in range(2)]
        ps_o = st.enter_context(nc.psum_tensor(f"ps_o_{layer}", [P, BATCH, 512], F32))
        own_s, self_set, self_exp = s("sum_own"), s("self_set"), s("self_exp")
        dst_in = [s(f"dst_in{y}") for y in range(2)]
        gathered = [[s(f"gathered{y}{j}") for j in range(BATCH)] for y in range(DEPTH)]
        copied, onehots, fetched, ed_read = s("copied"), s("onehots"), s("ed_fetched"), s("ed_read")
        zeros_set, act_msg, to_dst_set = s("zeros_set"), s("act_msg"), s("to_dst_set")
        logit_set, w_set, msg_set, summed, added = s("logit_set"), s("w_set"), s("msg_set"), s("summed"), s("added")
        dst_rows = dst_row.rearrange("(b n) -> b n", n=BATCH * P)

        with nc.Block() as block:
            @block.sync
            def _(sp):
                def fetch(i, y):
                    b = i * 2 + y
                    sp.wait_ge(onehots, b + 1)
                    sp.dma_start(dst_b[:, y, :], dst_rows[bass.ds(b, 1), :].to_broadcast([P, BATCH * P])).then_inc(dst_in[y], 16)
                with sp.Fori(0, NB // 2) as i:
                    fetch(i, 0)
                    fetch(i, 1)
                fetch(NB // 2, 0)

            @block.gpsimd
            def _(pool):
                pool.memset(scratch[:], 0.0)

                def gather(i, y):
                    b = i * DEPTH + y
                    pool.wait_ge(summed, BATCH * (b + 1))
                    pool.tensor_copy(cur[:, y, :], k["src_col"][:, bass.ds(b * BATCH, BATCH)]).then_inc(copied, 1)
                    pool.wait_ge(copied, b + 1)
                    pool.tensor_tensor(scratch[:], k["ones"][0:1, 0:1], k["ones"][0:1, 0:1], ALU.add)
                    for j in range(BATCH):
                        pool.indirect_dma_start(rows[:, y, j, :], None, table,
                                                bass.IndirectOffsetOnAxis(cur[:, y, j:j + 1], 0)).then_inc(gathered[y][j], 16)
                with pool.Fori(0, NB // DEPTH) as i:
                    for y in range(DEPTH):
                        gather(i, y)

            @block.vector
            def _(dve):
                own = Steps(dve, own_s)
                link = own.link
                m = em[:, :, H:2 * H]
                dve.memset(zeros[:], 0.0).then_inc(zeros_set, 1)
                own.did(dve.memset(acc[:], 0.0))
                link(dve.tensor_tensor(tself[:], es[:], em[:, :, 0:H], ALU.add))
                link(dve.scalar_tensor_tensor(tself[:], tself[:], SLOPE, tself[:], ALU.mult, ALU.max))
                link(dve.tensor_tensor(tself[:], tself[:], m, ALU.subtract))
                dve.tensor_scalar(tself[:], tself[:], 1.0, None, ALU.min).then_inc(self_set, 1)
                dve.sem_inc(onehots, 2)
                dve.sem_inc(ed_read, 2)
                dve.sem_inc(added, BATCH)

                def onehot(i, y4, j):
                    b = i * DEPTH + y4
                    if j == 0:
                        dve.wait_ge(summed, BATCH * (b + 1))
                    dve.tensor_scalar(to_dst[:, y4, j, :], k["iota_row"][:], k["dst_col"][:, bass.ds(b * BATCH + j, 1)],
                                      None, ALU.is_equal).then_inc(to_dst_set, 1)
                    if j == BATCH - 1:
                        y = y4 % 2
                        dve.wait_ge(dst_in[y], (i * (DEPTH // 2) + y4 // 2 + 1) * 16)
                        dve.wait_ge(fetched, b + 1)
                        dve.tensor_scalar(to_edge[:, y, :], dst_b[:, y, :], k["iota_col"][:, 0:1], None, ALU.is_equal).then_inc(onehots, 1)

                def add(b, between):
                    blocks = blocks_of(nc, mybir.EngineType.DVE, k, b)
                    for j in range(BATCH):
                        at = acc[:, bass.ds(blocks[j], 1), :].rearrange("p o c -> p (o c)")
                        dve.wait_ge(summed, BATCH * (b + DEPTH) + j + 1)
                        dve.wait_ge(added, BATCH * (b + 2) + j)
                        dve.tensor_tensor(at, at, ps_o[:, j, 0:W], ALU.add).then_inc(added, 1)
                        between(j)

                def step(i, y4):
                    b, y = i * DEPTH + y4, y4 % 2
                    after = (i, y4 + 1) if y4 + 1 < DEPTH else (i + 1, 0)
                    for j in range(BATCH):
                        dve.wait_ge(gathered[y4][j], (i + 1) * 16)
                    dve.wait_ge(fetched, b + 3)
                    edm = ps_e[y][:, 0:BATCH * 2 * H].rearrange("p (k w) -> p k w", w=2 * H)
                    own.did(dve.tensor_tensor(logit[:, y], rows[:, y4, :, C:W], edm[:, :, 0:H], ALU.add))
                    onehot(*after, 0)
                    own.settle()
                    own.did(dve.scalar_tensor_tensor(leaky[:, y], logit[:, y], SLOPE, logit[:, y], ALU.mult, ALU.max))
                    onehot(*after, 1)
                    own.settle()
                    dve.tensor_tensor(logit[:, y], leaky[:, y], edm[:, :, H:2 * H], ALU.subtract).then_inc(ed_read, 1)
                    onehot(*after, 2)
                    dve.wait_ge(ed_read, b + 3)
                    dve.tensor_scalar(leaky[:, y], logit[:, y], 1.0, None, ALU.min).then_inc(logit_set, 1)
                    onehot(*after, 3)

                    def message(j):
                        j += BY_ACT
                        if j < BATCH:
                            dve.wait_ge(w_set, b + 1)
                            msg = rows[:, y4, j, 0:C].rearrange("p (h d) -> p h d", h=H)
                            dve.tensor_tensor(msg, msg, rows[:, y4, j, C:W].unsqueeze(2).to_broadcast([P, H, C // H]),
                                              ALU.mult).then_inc(msg_set, 1)
                    add(b - 1, message)

                for j in range(BATCH):
                    onehot(0, 0, j)
                with own.loop(NB // DEPTH, DEPTH * 2) as i:
                    for y in range(DEPTH):
                        step(i, y)
                add(NB - 1, lambda j: None)
                dve.wait_ge(added, BATCH * (NB + 2))
                dve.wait_ge(self_exp, 1)
                link(dve.tensor_tensor(wself[:], wself[:], k["loops"][:].unsqueeze(2).to_broadcast([P, NT, H]), ALU.mult))

            @block.scalar
            def _(act):
                act.wait_ge(self_set, 1)
                act.activation(wself[:], tself[:], ACT.Exp).then_inc(self_exp, 1)
                with act.Fori(0, NB // DEPTH) as i:
                    for y in range(DEPTH):
                        b = i * DEPTH + y
                        act.wait_ge(logit_set, b + 1)
                        act.activation(rows[:, y, :, C:W], leaky[:, y % 2], ACT.Exp).then_inc(w_set, 1)
                        act.wait_ge(w_set, b + 1)
                        for j in range(BY_ACT):
                            for h in range(H):
                                msg = rows[:, y, j, h * (C // H):(h + 1) * (C // H)]
                                act.activation(msg, msg, ACT.Copy, scale=rows[:, y, j, C + h:C + h + 1]).then_inc(act_msg, 1)

            @block.tensor
            def _(pe):
                pe.sem_inc(fetched, 2)
                pe.sem_inc(summed, (DEPTH - 1) * BATCH)
                pe.wait_ge(zeros_set, 1)
                for j in range(BATCH):
                    pe.matmul(ps_o[:, j, 0:W], zeros[:, 0:P], zeros[:], start=True, stop=True).then_inc(summed, 1)

                def fetch(i, y4):
                    b, y = i * DEPTH + y4, y4 % 2
                    blocks = blocks_of(nc, mybir.EngineType.PE, k, b)
                    pe.wait_ge(onehots, b + 3)
                    pe.wait_ge(ed_read, b + 1)
                    for j in range(BATCH):
                        last = pe.matmul(ps_e[y][:, j * 2 * H:(j + 1) * 2 * H], to_edge[:, y, j * P:(j + 1) * P],
                                         em[:, bass.ds(blocks[j], 1), :].rearrange("p o w -> p (o w)"), start=True, stop=True)
                    last.then_inc(fetched, 1)

                def step(i, y4):
                    b, y = i * DEPTH + y4, y4 % 2
                    fetch(*((i, y4 + 1) if y4 + 1 < DEPTH else (i + 1, 0)))
                    pe.wait_ge(to_dst_set, BATCH * (b + 1))
                    for j in range(BATCH):
                        if j < BY_ACT:
                            pe.wait_ge(act_msg, H * (BY_ACT * b + j + 1))
                        else:
                            pe.wait_ge(msg_set, (BATCH - BY_ACT) * b + j - BY_ACT + 1)
                        pe.wait_ge(added, BATCH * (b + 1) + j + 1)
                        pe.matmul(ps_o[:, j, 0:W], to_dst[:, y4, j, :], rows[:, y4, j, :], start=True, stop=True).then_inc(summed, 1)

                fetch(0, 0)
                with pe.Fori(0, NB // DEPTH) as i:
                    for y in range(DEPTH):
                        step(i, y)

def tile_of(t3, t):
    return t3[:, bass.ds(t, 1), :].rearrange("p o c -> p (o c)")


def aggregate(dve, own, H, h1, acc, wself, bias_b, part, t):
    link = own.link
    heads = [P, H, C // H]

    def by_head(ap):
        return ap.rearrange("p (h d) -> p h d", h=H)
    wide = lambda w: tile_of(w, t).unsqueeze(2).to_broadcast(heads)
    link(dve.tensor_tensor(by_head(part[:]), by_head(tile_of(h1, t)), wide(wself[0]), ALU.mult))
    link(dve.tensor_tensor(part[:], part[:], acc[:, bass.ds(t, 1), 0:C].rearrange("p o c -> p (o c)"), ALU.add))
    link(dve.tensor_tensor(by_head(part[:]), by_head(part[:]), wide(wself[1]), ALU.mult))
    link(dve.tensor_tensor(tile_of(h1, t), part[:], bias_b[:], ALU.add))


def moments(dve, own, src, t, tick, stats, mv_t, mv):
    own.did(dve.memset(tick[:], 0.0))
    own.link(dve.bn_stats(stats[:], tile_of(src, t)))
    own.did(dve.memset(tick[:], 0.0))
    own.did(dve.bn_aggr(mv_t[:], stats[:]))
    own.settle()
    own.link(dve.tensor_scalar(tile_of(mv, t), mv_t[:], 1.0, None, ALU.mult))


def between_layers(nc, a, k, acc, wself, alloc, sems, table2):
    with ExitStack() as st:
        sb, sem = alloc(st), sems(st)
        h1, gat_w = k["h1"], k["gat2_w"]
        bias_b, part, hn = sb("gnn_b1_b", [P, C]), sb("part", [P, C]), sb("on", [P, C])
        g_col, b_col = sb("g_col", [P, CC]), sb("b_col", [P, CC])
        rden = sb("rden", [P, NT, HEADS1])
        stats, mv, mv_t, tick = sb("stats_o", [P, 6]), sb("mv_o", [P, NT, 2]), sb("mv_ot", [P, 2]), sb("tick_o", [1, 1])
        std, rstd = sb("std_o", [P, NT]), sb("rstd_o", [P, NT])
        rT = sb("rT", [P, CC, P])
        tabrow = sb("tabrow2", [P, C + 1])
        ps_t = st.enter_context(nc.psum_tensor("ps_t", [P, 512], F32))
        ps_h = st.enter_context(nc.psum_tensor("ps_h", [P, 512], F32))
        b_in, own_s, var_set, std_set, on_set = (sem(n) for n in ("mid_in", "mid_own", "mid_var", "mid_std", "on_set"))
        turned, rT_set, h_done, row_set, h_out, row_out = (sem(n) for n in ("mid_turned", "rT_set", "mid_h", "row2_set", "h2_out", "row2_out"))
        with nc.Block() as block:
            @block.sync
            def _(sp):
                sp.dma_start(bias_b[:], a["L0_gnn_b1"].partition_broadcast(P)).then_inc(b_in, 16)
                with nc.allow_non_contiguous_dma(reason="a bias of a few hundred values, one a partition"):
                    sp.dma_start(g_col[:], a["L0_gnn_ln_g"].rearrange("(c p) -> p c", p=P)).then_inc(b_in, 16)
                    sp.dma_start(b_col[:], a["L0_gnn_ln_b"].rearrange("(c p) -> p c", p=P)).then_inc(b_in, 16)
                sp.sem_inc(row_out, 16)
                with sp.Fori(0, NT) as t:
                    sp.wait_ge(row_set, t + 1)
                    sp.dma_start(table2[bass.ds(t * P, P), :], tabrow[:]).then_inc(row_out, 16)
                sp.wait_ge(row_out, 16 * (NT + 1))

            @block.vector
            def _(dve):
                own = Steps(dve, own_s)
                link = own.link
                link(dve.tensor_tensor(rden[:], acc[:, :, C:C + HEADS1], wself[:], ALU.add))
                link(dve.tensor_scalar(rden[:], rden[:], 1e-30, None, ALU.max))
                link(dve.reciprocal(rden[:], rden[:]))
                dve.wait_ge(b_in, 48)
                with own.loop(NT, 9) as t:
                    aggregate(dve, own, HEADS1, h1, acc, (wself, rden), bias_b, part, t)
                    moments(dve, own, h1, t, tick, stats, mv_t, mv)
                dve.tensor_scalar(rstd[:], mv[:, :, 1], EPS, None, ALU.add).then_inc(var_set, 1)
                dve.wait_ge(std_set, 1)
                link(dve.reciprocal(rstd[:], std[:]))
                with own.loop(NT, 0) as t:
                    dve.wait_ge(turned, t + 1)
                    dve.tensor_scalar(hn[:], tile_of(h1, t), mv[:, bass.ds(t, 1), 0:1].rearrange("p o c -> p (o c)"),
                                      rstd[:, bass.ds(t, 1)], ALU.subtract, ALU.mult).then_inc(on_set, 1)

            @block.scalar
            def _(act):
                act.wait_ge(var_set, 1)
                act.activation(std[:], rstd[:], ACT.Sqrt).then_inc(std_set, 1)
                act.wait_ge(b_in, 48)
                act.sem_inc(h_out, 3)
                with act.Fori(0, NT) as t:
                    act.wait_ge(turned, t + 2)
                    for c in range(CC):
                        act.activation(rT[:, c, :], ps_t[:, c * P:(c + 1) * P], ACT.Relu, bias=b_col[:, c:c + 1],
                                       scale=g_col[:, c:c + 1]).then_inc(rT_set, 1)
                    act.wait_ge(h_done, t + 1)
                    act.wait_ge(row_out, 16 * (t + 1))
                    act.activation(tabrow[:], ps_h[:, 0:C + 1], ACT.Copy).then_inc(row_set, 1)
                    act.activation(tile_of(h1, t), ps_h[:, 0:C], ACT.Copy).then_inc(h_out, 1)
                    act.activation(k["es2"][:, bass.ds(t, 1), 0], ps_h[:, C:C + 1], ACT.Copy).then_inc(h_out, 1)
                    act.activation(k["ed2"][:, bass.ds(t, 1), 0], ps_h[:, C + 1:C + 2], ACT.Copy).then_inc(h_out, 1)

            @block.tensor
            def _(pe):
                pe.sem_inc(turned, 1)
                with pe.Fori(0, NT) as t:
                    pe.wait_ge(on_set, t + 1)
                    for c in range(CC):
                        last = pe.transpose(ps_t[:, c * P:(c + 1) * P], hn[:, c * P:(c + 1) * P], k["ident"][:])
                    last.then_inc(turned, 1)
                    pe.wait_ge(rT_set, 2 * t + 2)
                    pe.wait_ge(h_out, 3 * t + 3)
                    for c in range(CC):
                        last = pe.matmul(ps_h[:, 0:C + 2], rT[:, c, :], gat_w[:, c, :], start=c == 0, stop=c == CC - 1)
                    last.then_inc(h_done, 1)


def experts(nc, a, k, acc, wself, alloc, sems, mixed, out):
    with ExitStack() as st:
        sb, sem = alloc(st), sems(st)
        r = k["h1"]
        bias_b, part, hn = sb("gnn_b2_b", [P, C]), sb("part_r", [P, C]), sb("rn", [P, C])
        rden = sb("rden_r", [P, NT, 1])
        stats, mv, mv_t, tick = sb("stats_r", [P, 6]), sb("mv_r", [P, NT, 2]), sb("mv_rt", [P, 2]), sb("tick_r", [1, 1])
        std, rstd = sb("std_r", [P, NT]), sb("rstd_r", [P, NT])
        add = sb("add", [P, 2, 5, C])
        w1, w2 = sb("ffn_w1", [P, EX * CC, ED]), sb("ffn_w2", [P, EX * FE, C])
        b1_col, b2 = sb("ffn_b1_col", [P, EX * FE]), sb("ffn_b2", [EX, C])
        wg = sb("wg", [P, CC, EX])
        gate_rows = sb("gate_rows", [1, 2, EX])
        xT_cur = sb("xT_cur", [P, CC, P])
        lg, lg2 = sb("lg", [P, NT, EX]), sb("lg2", [P, NT, EX])
        eq, first, second, place = (sb(n, [P, NT, EX]) for n in ("eq", "first", "second", "place"))
        v0, v1, w0, w1_ = (sb(n, [P, NT]) for n in ("v0", "v1", "w0", "w1_"))
        c_cur, cT = sb("c_cur", [P, EX]), sb("cT", [EX, P])
        hT = sb("hT", [P, 2, FE, P])
        xT = acc[:].rearrange("p t c -> p (t c)")[:, 0:CC * NP].rearrange("p (c n) -> p c n", c=CC)
        ps_t = st.enter_context(nc.psum_tensor("ps_xt", [P, 512], F32))
        ps_c = st.enter_context(nc.psum_tensor("ps_cb", [P, 512], F32))
        ps_h = [st.enter_context(nc.psum_tensor(f"ps_eh{y}", [P, 512], F32)) for y in range(2)]
        ps_y = [st.enter_context(nc.psum_tensor(f"ps_ey{y}", [P, 512], F32)) for y in range(2)]
        names = ("small_in", "w_in", "add_in", "own", "var", "std", "rn_set", "turned", "xT_set", "lg_done", "lg_set",
                 "gap_set", "gap_exp", "comb_set", "c_set", "c_turned", "cT_set", "bias_done", "w1_done", "h_set",
                 "w2_done", "added", "stored", "used", "xT_all", "zeroed")
        S = {n: sem("ffn_" + n) for n in names}
        GROUP = 5
        assert NT % GROUP == 0
        comb = lg2

        with nc.Block() as block:
            @block.sync
            def _(sp):
                sp.dma_start(bias_b[:], a["L0_gnn_b2"].partition_broadcast(P)).then_inc(S["small_in"], 16)
                sp.dma_start(wg[:], a["L0_ffn_Wg"].rearrange("(c p) n -> p c n", p=P)).then_inc(S["small_in"], 16)
                sp.dma_start(gate_rows[:, 0, :], a["L0_ffn_bg"].rearrange("(o n) -> o n", o=1)).then_inc(S["small_in"], 16)
                sp.dma_start(gate_rows[:, 1, :], a["L0_ffn_bias"].rearrange("(o n) -> o n", o=1)).then_inc(S["small_in"], 16)
                sp.dma_start(b2[:], a["L0_ffn_b2"]).then_inc(S["small_in"], 16)
                with nc.allow_non_contiguous_dma(reason="biases, one a partition"):
                    for e in range(EX):
                        sp.dma_start(b1_col[:, e * FE:(e + 1) * FE], a["L0_ffn_b1"][e].rearrange("(f p) -> p f", p=P)).then_inc(S["small_in"], 16)
                sp.wait_ge(S["zeroed"], 1)
                for gr in range(NT // GROUP):
                    if gr > 0:
                        sp.wait_ge(S["used"], gr)
                    lo, n = gr * GROUP, GROUP if gr < NT // GROUP - 1 else GROUP - 1
                    sp.dma_start(add[:, 0, 0:n, :], a["x"][lo * P:(lo + n) * P, :].rearrange("(t p) c -> p t c", p=P)).then_inc(S["add_in"], 16)
                    sp.dma_start(add[:, 1, :, :], mixed[lo * P:(lo + GROUP) * P, :].rearrange("(t p) c -> p t c", p=P)).then_inc(S["add_in"], 16)
                    if n < GROUP:
                        sp.dma_start(add[0:LAST, 0, n, :], a["x"][(NT - 1) * P:N, :]).then_inc(S["add_in"], 16)
                sp.dma_start(w1[:], a["L0_ffn_W1"].rearrange("e (c p) n -> p (e c) n", p=P)).then_inc(S["w_in"], 16)
                sp.dma_start(w2[:], a["L0_ffn_W2"].rearrange("e (f p) n -> p (e f) n", p=P)).then_inc(S["w_in"], 16)
                with sp.Fori(0, NT - 1) as t:
                    sp.wait_ge(S["added"], (EX + 1) * (t + 1) + 2)
                    sp.dma_start(out[bass.ds(t * P, P), :], tile_of(r, t)).then_inc(S["stored"], 16)
                sp.wait_ge(S["added"], (EX + 1) * NT + 2)
                sp.dma_start(out[(NT - 1) * P:N, :], r[0:LAST, NT - 1, :]).then_inc(S["stored"], 16)
                sp.wait_ge(S["stored"], 16 * NT)

            @block.vector
            def _(dve):
                own = Steps(dve, S["own"])
                link = own.link
                link(dve.memset(add[:, 0, GROUP - 1, :], 0.0))
                dve.sem_inc(S["zeroed"], 1)
                link(dve.tensor_tensor(rden[:], acc[:, :, C:C + 1], wself[:], ALU.add))
                link(dve.tensor_scalar(rden[:], rden[:], 1e-30, None, ALU.max))
                link(dve.reciprocal(rden[:], rden[:]))
                dve.wait_ge(S["small_in"], 16 * (5 + EX))
                with own.loop(NT, 4) as t:
                    aggregate(dve, own, 1, r, acc, (wself, rden), bias_b, part, t)
                for gr in range(NT // GROUP):
                    dve.wait_ge(S["add_in"], 32 * (gr + 1) + (16 if gr == NT // GROUP - 1 else 0))
                    at = r[:, gr * GROUP:(gr + 1) * GROUP, :]
                    link(dve.tensor_tensor(at, at, add[:, 0], ALU.add))
                    link(dve.tensor_tensor(at, at, add[:, 1], ALU.add))
                    dve.sem_inc(S["used"], 1)
                with own.loop(NT, 5) as t:
                    moments(dve, own, r, t, tick, stats, mv_t, mv)
                dve.tensor_scalar(rstd[:], mv[:, :, 1], EPS, None, ALU.add).then_inc(S["var"], 1)
                dve.wait_ge(S["std"], 1)
                link(dve.reciprocal(rstd[:], std[:]))
                with own.loop(NT, 0) as t:
                    dve.wait_ge(S["turned"], t + 1)
                    dve.tensor_scalar(hn[:], tile_of(r, t), mv[:, bass.ds(t, 1), 0:1].rearrange("p o c -> p (o c)"),
                                      rstd[:, bass.ds(t, 1)], ALU.subtract, ALU.mult).then_inc(S["rn_set"], 1)
                    dve.wait_ge(S["lg_done"], t + 1)
                    dve.tensor_scalar(tile_of(lg, t), ps_c[:, 0:EX], 1.0, None, ALU.mult).then_inc(S["lg_set"], 1)
                dve.wait_ge(S["lg_set"], NT)

                def wide(v):
                    return v[:].unsqueeze(2).to_broadcast([P, NT, EX])
                number = k["iota_row"][:, 0:EX].unsqueeze(1).to_broadcast([P, NT, EX])

                def largest(src, value, onehot):
                    link(dve.tensor_reduce(value[:], src[:], AX.X, ALU.max))
                    link(dve.tensor_tensor(eq[:], src[:], wide(value), ALU.is_equal))
                    link(dve.tensor_scalar(eq[:], eq[:], -float(EX), float(EX), ALU.mult, ALU.add))
                    link(dve.tensor_tensor(eq[:], eq[:], number, ALU.add))
                    link(dve.tensor_reduce(w0[:], eq[:], AX.X, ALU.min))
                    link(dve.tensor_tensor(onehot[:], number, wide(w0), ALU.is_equal))
                largest(lg, v0, first)
                link(dve.scalar_tensor_tensor(lg2[:], first[:], -3e38, lg[:], ALU.mult, ALU.add))
                largest(lg2, v1, second)
                dve.tensor_tensor(v1[:], v1[:], v0[:], ALU.subtract).then_inc(S["gap_set"], 1)
                dve.wait_ge(S["gap_exp"], 1)
                link(dve.tensor_scalar(w0[:], w1_[:], 1.0, None, ALU.add))
                link(dve.reciprocal(w0[:], w0[:]))
                link(dve.tensor_tensor(w1_[:], w1_[:], w0[:], ALU.mult))
                link(dve.tensor_tensor(first[:], first[:], wide(w0), ALU.mult))
                link(dve.tensor_tensor(second[:], second[:], wide(w1_), ALU.mult))
                link(dve.tensor_tensor(comb[:], first[:], second[:], ALU.add))
                dve.sem_inc(S["comb_set"], 1)
                dve.sem_inc(S["added"], 2)
                with own.loop(NT, 0) as t:
                    def add_to(pos):
                        dve.wait_ge(S["added"], (EX + 1) * t + pos + 2)
                    at = tile_of(r, t)
                    dve.wait_ge(S["c_turned"], t + 1)
                    dve.tensor_scalar(c_cur[:], tile_of(comb, t), 1.0, None, ALU.mult).then_inc(S["c_set"], 1)
                    for e in range(EX):
                        if e == 3:
                            dve.wait_ge(S["c_turned"], t + 2)
                            dve.tensor_copy(cT[:], ps_c[0:EX, 0:P]).then_inc(S["cT_set"], 1)
                        if e == 5:
                            dve.wait_ge(S["bias_done"], t + 1)
                            add_to(e)
                            dve.tensor_tensor(at, at, ps_t[:, 0:C], ALU.add).then_inc(S["added"], 1)
                        dve.wait_ge(S["w2_done"], EX * t + e + 3)
                        add_to(e + (e >= 5))
                        dve.scalar_tensor_tensor(at, ps_y[e % 2][:, 0:C], comb[:, bass.ds(t, 1), e:e + 1].rearrange("p o c -> p (o c)"),
                                                 at, ALU.mult, ALU.add).then_inc(S["added"], 1)

            @block.scalar
            def _(act):
                act.wait_ge(S["var"], 1)
                act.activation(std[:], rstd[:], ACT.Sqrt).then_inc(S["std"], 1)
                act.sem_inc(S["xT_all"], 1)
                with act.Fori(0, NT) as t:
                    act.wait_ge(S["turned"], t + 2)
                    act.activation(xT_cur[:].rearrange("p c n -> p (c n)"), ps_t[:, 0:C], ACT.Copy).then_inc(S["xT_set"], 1)
                    act.activation(xT[:, :, bass.ds(t * P, P)], ps_t[:, 0:C].rearrange("p (c n) -> p c n", c=CC),
                                   ACT.Copy).then_inc(S["xT_all"], 1)
                act.wait_ge(S["gap_set"], 1)
                act.activation(w1_[:], v1[:], ACT.Exp).then_inc(S["gap_exp"], 1)
                act.sem_inc(S["h_set"], 2 * FE)
                act.wait_ge(S["small_in"], 16 * (5 + EX))
                with act.Fori(0, NT) as t:
                    for e in range(EX):
                        act.wait_ge(S["w1_done"], EX * t + e + 1)
                        act.wait_ge(S["w2_done"], EX * t + e + 1)
                        for f in range(FE):
                            act.activation(hT[:, e % 2, f, :], ps_h[e % 2][:, f * P:(f + 1) * P], ACT.Relu,
                                           bias=b1_col[:, e * FE + f:e * FE + f + 1]).then_inc(S["h_set"], 1)

            @block.tensor
            def _(pe):
                pe.wait_ge(S["small_in"], 16 * (5 + EX))
                pe.sem_inc(S["turned"], 1)
                with pe.Fori(0, NT) as t:
                    pe.wait_ge(S["rn_set"], t + 1)
                    pe.wait_ge(S["xT_all"], t + 1)
                    for c in range(CC):
                        last = pe.transpose(ps_t[:, c * P:(c + 1) * P], hn[:, c * P:(c + 1) * P], k["ident"][:])
                    last.then_inc(S["turned"], 1)
                    pe.wait_ge(S["xT_set"], t + 1)
                    for c in range(CC):
                        pe.matmul(ps_c[:, 0:EX], xT_cur[:, c, :], wg[:, c, :], start=c == 0, stop=False)
                    for j in range(2):
                        last = pe.matmul(ps_c[:, 0:EX], k["ones"][0:1, :], gate_rows[:, j, :], start=False, stop=j == 1)
                    last.then_inc(S["lg_done"], 1)
                pe.wait_ge(S["comb_set"], 1)
                pe.wait_ge(S["xT_all"], NT + 1)
                pe.wait_ge(S["w_in"], 32)
                pe.sem_inc(S["c_turned"], 1)
                pe.sem_inc(S["w2_done"], 2)
                with pe.Fori(0, NT) as t:
                    def up(e):
                        pe.wait_ge(S["h_set"], FE * (EX * t + e) + FE)
                        for f in range(FE):
                            for c in range(CC):
                                last = pe.matmul(ps_h[e % 2][:, f * P:(f + 1) * P], w1[:, e * CC + c, f * P:(f + 1) * P],
                                                 xT[:, c, bass.ds(t * P, P)], start=c == 0, stop=c == CC - 1)
                        last.then_inc(S["w1_done"], 1)

                    def read_by(e):
                        e2 = e - 2
                        return (EX + 1) * t + (e2 + (e2 >= 5) + 3 if e2 >= 0 else e2 + 3)
                    up(0)
                    for e in range(EX):
                        if e + 1 < EX:
                            up(e + 1)
                        if e == 1:
                            pe.wait_ge(S["c_set"], t + 1)
                            pe.transpose(ps_c[0:EX, 0:P], c_cur[:], k["ident"][:]).then_inc(S["c_turned"], 1)
                        if e == 3:
                            pe.wait_ge(S["cT_set"], t + 1)
                            pe.matmul(ps_t[:, 0:C], cT[:], b2[:], start=True, stop=True).then_inc(S["bias_done"], 1)
                        pe.wait_ge(S["h_set"], FE * (EX * t + e) + 3 * FE)
                        pe.wait_ge(S["added"], read_by(e))
                        for f in range(FE):
                            last = pe.matmul(ps_y[e % 2][:, 0:C], hT[:, e % 2, f, :], w2[:, e * FE + f, :], start=f == 0, stop=f == FE - 1)
                        last.then_inc(S["w2_done"], 1)


_INS = ["x", "src", "dst"] + ["L0_gnn_" + n for n in ("W1", "a1_src", "a1_dst", "b1", "ln_g", "ln_b", "W2", "a2_src", "a2_dst", "b2")] \
    + ["L0_mix_" + n for n in ("ln1_g", "ln1_b", "Wx", "bx", "Wq", "Wk", "Wv", "Wo", "bo", "ln2_g", "ln2_b", "W1", "b1", "W2", "b2")] \
    + ["L0_ffn_" + n for n in ("Wg", "bg", "bias", "W1", "b1", "W2", "b2")]


def kernel(**inputs):
    import numpy as _np
    import concourse.bacc as _bacc
    from concourse import mybir as _mybir
    from concourse.bass_utils import run_bass_kernel_spmd as _run

    nc = _bacc.Bacc("TRN2", target_bir_lowering=False, num_devices=1)
    arrays, args = {}, {}
    for name in _INS:
        array = _np.ascontiguousarray(inputs[name])
        arrays[f"in_{name}"] = array
        args[name] = nc.dram_tensor(f"in_{name}", array.shape, _mybir.dt.from_np(array.dtype), kind="ExternalInput").ap()
    out = nc.dram_tensor("out", [N, C], F32, kind="ExternalOutput").ap()
    build(nc, args, out)
    r = _run(nc, [arrays], core_ids=[0])
    return r.results[0]["out"]
```

```python
from contextlib import ExitStack, contextmanager

import concourse.bass as bass
from concourse import mybir

F32 = mybir.dt.float32
I32 = mybir.dt.int32
U32 = mybir.dt.uint32
ALU = mybir.AluOpType
ACT = mybir.ActivationFunctionType
AX = mybir.AxisListType

P = 128
N, C, E = 3125, 256, 50000
NT = -(-N // P)
NP = NT * P
LAST = N - (NT - 1) * P
LOOPS = 625
CC = C // P
HEADS1, HID = 4, C // 4
MH, DH, KR = 8, 32, 4
FF = 4 * C
FM = FF // P
EX, ED = 8, 512
FE = ED // P
EPS = 1e-5
SLOPE = 0.2

HALF = 4
EC = -(-E // (P * 2 * HALF)) * 2 * HALF
BATCH = 4
TILES = -(-(E // P + NT) // (2 * BATCH)) * 2 * BATCH
NB = TILES // BATCH
DEPTH = 4
assert NB % DEPTH == 0
TT = TILES + BATCH
TR = TT // 4
SLOTS = TT * P
PAD_DST = NP + P - 1
FAR = float(1 << 22)


def blocks_of(nc, engine, k, b):
    _, found = nc.values_load_multi_w_load_instructions(
        k["block_row"][0:1, bass.ds((b + 1) * BATCH, BATCH)], engines=(engine,), min_val=0, max_val=NT - 1,
        skip_runtime_bounds_check_because="edge_tables bounds them")
    return found


class Steps:

    def __init__(self, eng, sem):
        self.eng, self.sem, self.n, self.turn = eng, sem, 0, None

    def did(self, ins):
        ins.then_inc(self.sem, 1)
        self.n += 1

    def settle(self):
        self.eng.wait_ge(self.sem, self.n if self.turn is None else self.turn * self.per + self.n)

    def link(self, ins):
        self.did(ins)
        self.settle()

    @contextmanager
    def loop(self, count, per):
        n0 = self.n
        with self.eng.Fori(0, count) as i:
            self.turn, self.per = i, per
            yield i
            assert self.n - n0 == per, (self.n - n0, per)
        self.n, self.turn = n0 + per * count, None


def build(nc, a, out):
    with ExitStack() as top:
        phases = iter(range(99))

        def alloc(stack):
            n = next(phases)
            return lambda name, shape, dt=F32: stack.enter_context(nc.sbuf_tensor(f"{name}_{n}", shape, dt))

        def sems(stack):
            taken = []

            def sem(name):
                taken.append(nc.alloc_semaphore(name=name))
                return taken[-1]

            def clear():
                nc.clear_and_free_semaphores(taken)
                nc.all_engine_barrier()
            stack.callback(clear)
            return sem

        sorted_edges = nc.dram_tensor("sorted_edges", [SLOTS, 2], I32).ap()
        dst_row = nc.dram_tensor("dst_row", [SLOTS], F32).ap()
        src_row = nc.dram_tensor("src_row", [SLOTS], F32).ap()
        table1 = nc.dram_tensor("table1", [NP, C + HEADS1], F32).ap()
        table2 = nc.dram_tensor("table2", [NP, C + 1], F32).ap()
        mixed = nc.dram_tensor("mixed", [NP, C], F32).ap()

        g = alloc(top)
        k = {
            "ident": g("ident", [P, P]), "ones": g("ones", [P, P]), "below": g("below", [P, P]),
            "iota_row": g("iota_row", [P, P]), "iota_col": g("iota_col", [P, 1]),
            "h1": g("h1", [P, NT, C]),
            "es1": g("es1", [P, NT, HEADS1]), "ed1": g("ed1", [P, NT, HEADS1]),
            "loops": g("loops", [P, NT]),
            "es2": g("es2", [P, NT, 1]), "ed2": g("ed2", [P, NT, 1]),
            "gat2_w": g("gat2_w", [P, CC, C + 2]),
            "src_col": g("src_col", [P, TT], I32), "dst_col": g("dst_col", [P, TT]),
            "hi_col": g("hi_col", [P, TT]), "block_row": g("block_row", [1, BATCH + TT], I32),
        }
        node_phase(nc, a, k, alloc, sems, sorted_edges, table1, mixed)
        edge_tables(nc, k, alloc, sems, sorted_edges, dst_row, src_row)
        with ExitStack() as layer:
            acc = alloc(layer)("acc1", [P, NT, C + HEADS1])
            wself = alloc(layer)("wself1", [P, NT, HEADS1])
            with ExitStack() as st:
                top_e = alloc(st)("top1", [P, NT, HEADS1])
                em = alloc(st)("em1", [P, NT, 2 * HEADS1])
                segment_max(nc, 1, HEADS1, k, k["es1"], k["ed1"], top_e, em, alloc, sems, src_row)
                weighted_sum(nc, 1, HEADS1, k, em, k["es1"], acc, wself, table1, alloc, sems, dst_row)
            between_layers(nc, a, k, acc, wself, alloc, sems, table2)
        with ExitStack() as layer:
            acc = alloc(layer)("acc2", [P, NT, C + 1])
            wself = alloc(layer)("wself2", [P, NT, 1])
            with ExitStack() as st:
                top_e = alloc(st)("top2", [P, NT, 1])
                em = alloc(st)("em2", [P, NT, 2])
                segment_max(nc, 2, 1, k, k["es2"], k["ed2"], top_e, em, alloc, sems, src_row)
                weighted_sum(nc, 2, 1, k, em, k["es2"], acc, wself, table2, alloc, sems, dst_row)
            experts(nc, a, k, acc, wself, alloc, sems, mixed, out)


def node_phase(nc, a, k, alloc, sems, sorted_edges, table1, mixed):
    with ExitStack() as st:
        sb, sem = alloc(st), sems(st)
        ident, ones, below = k["ident"], k["ones"], k["below"]
        dst_raw, src_raw = sb("dst_raw", [P, EC], I32), sb("src_raw", [P, EC], I32)
        fill = sb("fill", [P, TT, 2], I32)
        pair = sb("pair", [P, EC, 2], I32)
        blk_i = sb("blk_i", [P, EC], I32)
        blk, mask, rank, slot = (sb(n, [P, EC]) for n in ("blk", "mask", "rank", "slot"))
        slot_i = sb("slot_i", [P, EC], I32)
        ones_e = sb("ones_e", [P, EC])
        bnum = sb("bnum", [P, NT + 1])
        cnt, off, tl = sb("cnt", [P, NT]), sb("off", [P, NT]), sb("tl", [P, NT])
        tl_i = sb("tl_i", [P, NT], I32)
        cur_slot = sb("cur_slot", [P, 2, HALF], I32)
        cur_pair = sb("cur_pair", [P, 2, HALF, 2], I32)
        scratch = sb("pool_scratch", [1, 1])

        xn = sb("xn", [P, NT, C])
        halves, gap, mv = sb("halves", [P, NT, 6]), sb("gap", [P, NT]), sb("mv", [P, NT, 2])
        std, rstd = sb("std", [P, NT]), sb("rstd", [P, NT])
        hn, xcur = sb("hn", [P, C]), sb("xcur", [P, C])
        gat_w = sb("gat1_w", [P, CC, C + 2 * HEADS1])
        a_row = sb("a_row", [P, 4, C])
        prod = sb("prod", [P, C])
        xnT, hnT, xmT = (sb(n, [P, CC, P]) for n in ("xnT", "hnT", "xmT"))
        wx, wo = sb("wx", [P, CC, C]), sb("wo", [P, CC, C])
        wq, wk, wv = sb("wq", [P, CC, MH * KR]), sb("wk", [P, CC, MH * KR]), sb("wv", [P, CC, C])
        bias_cols = sb("bias_cols", [P, 5, CC])
        b1_col = sb("mix_b1_col", [P, FM])
        bo_row, b2_row = sb("bo_row", [1, C]), sb("mix_b2_row", [1, C])
        w1, w2 = sb("mix_w1", [P, CC, FF]), sb("mix_w2", [P, FM, C])
        v1 = sb("v1", [P, NT, C + 1])
        q = sb("q", [P, NT, MH, KR])
        qm = sb("qm", [P, NT, MH])
        QK = MH * KR
        kT, qT = sb("kT", [QK, NP]), sb("qT", [QK, NP])
        kmax = sb("kmax", [QK, 1])
        qcur, kcur, qTcur = sb("qcur", [P, QK]), sb("kcur", [QK, P]), sb("qTcur", [QK, P])
        zrow = sb("zrow", [1, C + 1])
        ek = sb("ek", [P, QK])
        kv, kvr = sb("kv", [QK, C]), sb("kvr", [QK, 1])
        headmask = sb("headmask", [QK, C])
        kvT = sb("kvT", [P, CC, QK])
        ko = sb("ko", [QK, C])
        gT = sb("gT", [P, 2, FM, P])
        mixrow = sb("mixrow", [P, C])
        es1, ed1, h1 = k["es1"], k["ed1"], k["h1"]
        tabrow = sb("tabrow", [P, C + HEADS1])

        def pt(name, shape):
            return st.enter_context(nc.psum_tensor(name, shape, F32))
        ps_a, ps_b, ps_c, ps_d = (pt(f"ps_{n}", [P, 512]) for n in "abcd")
        ps_e, ps_f = pt("ps_e", [P, 512]), pt("ps_f", [P, 512])
        ps_g, ps_g2 = pt("ps_g", [P, 512]), pt("ps_g2", [P, 512])
        FB = 512 // P
        ps_ff = ((ps_g, ps_g2), (ps_e, ps_f))
        assert FM == 2 * FB and NT % 2 == 1

        edges_pad, consts, fill_set, fill_out = (sem(n) for n in ("edges_pad", "consts", "fill_set", "fill_out"))
        edges_in, x_in, w_in, small_in = (sem(n) for n in ("edges_in", "x_in", "w_in", "small_in"))
        zeroed, v_own = sem("zeroed"), sem("node_dve_own")
        counted, prefixed, slots_set = sem("counted"), sem("prefixed"), sem("slots_set")
        pool_copied, scattered = sem("pool_copied"), [sem(f"scattered{j}") for j in range(2 * HALF)]
        w_set, var_set, std_set = sem("w_set"), sem("var_set"), sem("std_set")
        hn_set, xcur_set, turned = sem("hn_set"), sem("xcur_set"), sem("turned")
        xnT_set, hnT_set, xmT_set = sem("xnT_set"), sem("hnT_set"), sem("xmT_set")
        h_done, xm_done, qkv_done = sem("h_done"), sem("xm_done"), sem("qkv_done")
        row_set, h_out, v_out, qk_out, tab_out = (sem(n) for n in ("row_set", "h_out", "v_out", "qk_out", "tab_out"))
        q_set, qexp_set, qsoft_set, kmax_set, kexp_set = (sem(n) for n in ("q_set", "qexp_set", "qsoft_set", "kmax_set", "kexp_set"))
        cur_set, qk_turned, qT_set, kv_done = (sem(n) for n in ("cur_set", "qk_turned", "qT_set", "kv_done"))
        kv_set, kv_turned, kvT_set, ko_done, ko_set = (sem(n) for n in ("kv_set", "kv_turned", "kvT_set", "ko_done", "ko_set"))
        qTcur_set, attn_done, fx_set = sem("qTcur_set"), sem("attn_done"), sem("fx_set")
        fn_set, fn_turned, fnT_set = sem("fn_set"), sem("fn_turned"), sem("fnT_set")
        ff_done, g_set, m_done, mix_set, mix_out = (sem(n) for n in ("ff_done", "g_set", "m_done", "mix_set", "mix_out"))
        full = (P - 1) * EC
        loads = 18

        with nc.Block() as block:
            @block.sync
            def _(sp):
                sp.wait_ge(edges_pad, 2)
                for name, dst in (("dst", dst_raw), ("src", src_raw)):
                    sp.dma_start(dst[0:P - 1, :], a[name][0:full].rearrange("(p e) -> p e", e=EC)).then_inc(edges_in, 16)
                    sp.dma_start(dst[P - 1:P, 0:E - full],
                                 a[name][full:E].rearrange("(p e) -> p e", p=1)).then_inc(edges_in, 16)
                sp.wait_ge(zeroed, 1)
                sp.dma_start(xn[:, 0:NT - 1, :],
                             a["x"][0:(NT - 1) * P, :].rearrange("(t p) c -> p t c", p=P)).then_inc(x_in, 16)
                sp.dma_start(xn[0:LAST, NT - 1, :], a["x"][(NT - 1) * P:N, :]).then_inc(x_in, 16)
                sp.wait_ge(fill_set, 1)
                sp.dma_start(sorted_edges.rearrange("(p s) w -> p s w", p=P), fill[:]).then_inc(fill_out, 16)

                def chunks(w):
                    return w.rearrange("(c p) n -> p c n", p=P)
                n = 0
                for dst, src in ((gat_w[:, :, 0:C], chunks(a["L0_gnn_W1"])),
                                 (k["gat2_w"][:, :, 0:C], chunks(a["L0_gnn_W2"])),
                                 (wx[:], chunks(a["L0_mix_Wx"])), (wo[:], chunks(a["L0_mix_Wo"])),
                                 (w1[:], chunks(a["L0_mix_W1"])), (w2[:], chunks(a["L0_mix_W2"])),
                                 (bo_row[:], a["L0_mix_bo"].rearrange("(o n) -> o n", o=1)),
                                 (b2_row[:], a["L0_mix_b2"].rearrange("(o n) -> o n", o=1))):
                    sp.dma_start(dst, src).then_inc(w_in, 16)
                    n += 1
                for j, name in enumerate(("a1_src", "a1_dst", "a2_src", "a2_dst")):
                    sp.dma_start(a_row[:, j, :],
                                 a["L0_gnn_" + name].rearrange("h c -> (h c)").partition_broadcast(P)).then_inc(w_in, 16)
                    n += 1
                with nc.allow_non_contiguous_dma(reason="a bias of a few hundred values, one a partition"):
                    for j, name in enumerate(("ln1_g", "ln1_b", "bx", "ln2_g", "ln2_b")):
                        sp.dma_start(bias_cols[:, j, :], a["L0_mix_" + name].rearrange("(c p) -> p c", p=P)).then_inc(w_in, 16)
                        n += 1
                    sp.dma_start(b1_col[:], a["L0_mix_b1"].rearrange("(c p) -> p c", p=P)).then_inc(w_in, 16)
                assert n + 1 == loads
                sp.wait_ge(zeroed, 4)
                for h in range(MH):
                    c, r = h * DH // P, h * DH % P
                    for w, name, wide in ((wq, "Wq", KR), (wk, "Wk", KR), (wv, "Wv", DH)):
                        sp.dma_start(w[r:r + DH, c, h * wide:(h + 1) * wide], a["L0_mix_" + name]).then_inc(small_in, 16)
                sp.sem_inc(tab_out, 16)
                with sp.Fori(0, NT) as t:
                    sp.wait_ge(row_set, t + 1)
                    sp.dma_start(table1[bass.ds(t * P, P), :], tabrow[:]).then_inc(tab_out, 16)
                sp.sem_inc(mix_out, 16)
                with sp.Fori(0, NT) as t:
                    sp.wait_ge(mix_set, t + 2)
                    sp.dma_start(mixed[bass.ds(t * P, P), :], mixrow[:]).then_inc(mix_out, 16)
                sp.wait_ge(tab_out, 16 * (NT + 1))
                sp.wait_ge(mix_out, 16 * (NT + 1))

            @block.gpsimd
            def _(pool):
                own = Steps(pool, consts)
                pool.memset(dst_raw[:], PAD_DST).then_inc(edges_pad, 1)
                pool.memset(src_raw[:], 0).then_inc(edges_pad, 1)
                own.link(pool.memset(ones[:], 1.0))
                own.did(pool.affine_select(out=ident[:], in_=ones[:], compare_op=ALU.is_equal, fill=0.0, base=0,
                                           pattern=[[-1, P]], channel_multiplier=1))
                own.did(pool.affine_select(out=below[:], in_=ones[:], compare_op=ALU.is_gt, fill=0.0, base=0,
                                           pattern=[[1, P]], channel_multiplier=-1))
                for out_, pattern, step in ((k["iota_row"], [[1, P]], 0), (k["iota_col"], [[1, 1]], 1), (bnum, [[1, NT + 1]], 0)):
                    own.did(pool.iota(out_[:], pattern, base=0, channel_multiplier=step,
                                      allow_small_or_imprecise_dtypes=True))
                own.did(pool.memset(scratch[:], 0.0))
                own.did(pool.affine_select(out=k["loops"][:], in_=ones[:, 0:NT], compare_op=ALU.is_ge, fill=0.0,
                                           base=LOOPS - 1, pattern=[[-P, NT]], channel_multiplier=-1))
                own.link(pool.memset(headmask[:], 1.0))
                hm = headmask[:].rearrange("q (h d) -> q h d", d=DH)
                own.link(pool.affine_select(out=hm, in_=hm, compare_op=ALU.is_ge, fill=0.0, base=0,
                                            pattern=[[-KR, MH], [0, DH]], channel_multiplier=1))
                own.link(pool.affine_select(out=hm, in_=hm, compare_op=ALU.is_ge, fill=0.0, base=KR - 1,
                                            pattern=[[KR, MH], [0, DH]], channel_multiplier=-1))
                bound = pool.to_reg(SLOTS - 1)
                pool.wait_ge(slots_set, 1)
                pool.wait_ge(fill_out, 16)

                def half(i, y, again):
                    if again:
                        for j in range(HALF):
                            pool.wait_ge(scattered[y * HALF + j], 16 * i)
                    at = i * 2 * HALF + y * HALF
                    pool.tensor_copy(cur_slot[:, y, :], slot_i[:, bass.ds(at, HALF)]).then_inc(pool_copied, 1)
                    pool.tensor_copy(cur_pair[:, y], pair[:, bass.ds(at, HALF), :]).then_inc(pool_copied, 1)
                    pool.wait_ge(pool_copied, (i * 2 + y + 1) * 2)
                    pool.tensor_tensor(scratch[:], ones[0:1, 0:1], ones[0:1, 0:1], ALU.add).then_inc(consts, 1)
                    for j in range(HALF):
                        pool.indirect_dma_start(sorted_edges, bass.IndirectOffsetOnAxis(cur_slot[:, y, j:j + 1], 0),
                                                cur_pair[:, y, j, :], None, bounds_check=bound,
                                                oob_is_err=False).then_inc(scattered[y * HALF + j], 16)
                half(0, 0, False)
                half(0, 1, False)
                with pool.Fori(1, EC // (2 * HALF)) as i:
                    half(i, 0, True)
                    half(i, 1, True)
                for s in scattered:
                    pool.wait_ge(s, 16 * (EC // (2 * HALF)))

            @block.vector
            def _(dve):
                own = Steps(dve, v_own)
                link = own.link

                def copy(dst, src):
                    return dve.tensor_scalar(dst, src, 1.0, None, ALU.mult)
                dve.memset(xn[:, NT - 1, :], 0.0).then_inc(zeroed, 1)
                for w in (wq, wk, wv):
                    dve.memset(w[:], 0.0).then_inc(zeroed, 1)
                own.did(dve.memset(ones_e[:], 1.0))
                own.did(dve.memset(zrow[:], 0.0))
                own.did(dve.memset(v1[:, :, C:C + 1], 1.0))
                link(dve.memset(fill[:, :, 0], 0))
                dve.memset(fill[:, :, 1], PAD_DST).then_inc(fill_set, 1)
                dve.wait_ge(edges_in, 64)
                dve.wait_ge(consts, 11)
                own.did(dve.tensor_copy(pair[:, :, 0], src_raw[:]))
                own.did(dve.tensor_copy(pair[:, :, 1], dst_raw[:]))
                link(dve.tensor_scalar(blk_i[:], dst_raw[:], 7, None, ALU.arith_shift_right))
                link(dve.tensor_copy(blk[:], blk_i[:]))
                with own.loop(NT, 1) as b:
                    link(dve.tensor_scalar(mask[:], blk[:], bnum[:, bass.ds(b, 1)], None, ALU.is_equal, ALU.add,
                                           accum_out=cnt[:, bass.ds(b, 1)]))
                dve.tensor_copy(off[:], cnt[:]).then_inc(counted, 1)
                dve.wait_ge(prefixed, 2)
                link(dve.tensor_copy(tl_i[:], ps_a[:, 0:NT]))
                link(dve.tensor_scalar(tl[:], tl_i[:], float(P - 1), None, ALU.add))
                link(dve.tensor_copy(tl_i[:], tl[:]))
                link(dve.tensor_scalar(tl_i[:], tl_i[:], 7, None, ALU.arith_shift_right))
                link(dve.tensor_copy(tl[:], tl_i[:]))
                link(dve.tensor_tensor_scan(cnt[:], ones_e[:, 0:NT], tl[:], 0.0, ALU.mult, ALU.add))
                link(dve.tensor_tensor(cnt[:], cnt[:], tl[:], ALU.subtract))
                link(dve.scalar_tensor_tensor(off[:], cnt[:], float(P), ps_b[:, 0:NT], ALU.mult, ALU.add))
                link(dve.tensor_scalar(slot[:], blk[:], float(NT), FAR, ALU.is_equal, ALU.mult))
                with own.loop(NT, 4) as b:
                    link(dve.tensor_scalar(mask[:], blk[:], bnum[:, bass.ds(b, 1)], None, ALU.is_equal))
                    link(dve.tensor_tensor_scan(rank[:], ones_e[:], mask[:], off[:, bass.ds(b, 1)], ALU.mult, ALU.add))
                    link(dve.tensor_tensor(rank[:], rank[:], mask[:], ALU.mult))
                    link(dve.tensor_tensor(slot[:], slot[:], rank[:], ALU.add))
                link(dve.tensor_scalar(slot[:], slot[:], -1.0, None, ALU.add))
                dve.tensor_copy(slot_i[:], slot[:]).then_inc(slots_set, 1)

                dve.wait_ge(w_in, 16 * loads)
                for layer, w, heads in ((0, gat_w, HEADS1), (1, k["gat2_w"], 1)):
                    for side in range(2):
                        for c in range(CC):
                            link(dve.tensor_tensor(prod[:], w[:, c, 0:C], a_row[:, 2 * layer + side, :], ALU.mult))
                            link(dve.tensor_reduce(w[:, c, C + side * heads:C + (side + 1) * heads],
                                                   prod[:].rearrange("p (h d) -> p h d", h=heads), AX.X, ALU.add))
                dve.sem_inc(w_set, 1)

                def root(n):
                    dve.tensor_scalar(rstd[:], mv[:, :, 1], EPS, None, ALU.add).then_inc(var_set, 1)
                    dve.wait_ge(std_set, n)
                    link(dve.reciprocal(rstd[:], std[:]))

                def normed(dst, t):
                    return dve.tensor_scalar(dst, tile_of(xn, t), mv[:, bass.ds(t, 1), 0:1].rearrange("p o c -> p (o c)"),
                                             rstd[:, bass.ds(t, 1)], ALU.subtract, ALU.mult)

                dve.wait_ge(x_in, 32)
                dve.wait_ge(zeroed, 1)
                moments(dve, own, xn, halves, gap, mv)
                root(1)
                with own.loop(NT, 1) as t:
                    own.did(normed(tile_of(xn, t), t))
                own.settle()
                moments(dve, own, xn, halves, gap, mv)
                root(2)
                dve.sem_inc(qk_out, 2)

                def hn_of(t):
                    dve.wait_ge(turned, t + 1)
                    normed(hn[:], t).then_inc(hn_set, 1)

                def hnT_of(t):
                    dve.wait_ge(turned, t + 2)
                    for c in range(CC):
                        dve.tensor_scalar(hnT[:, c, :], ps_b[:, c * P:(c + 1) * P], bias_cols[:, 0, c:c + 1],
                                          bias_cols[:, 1, c:c + 1], ALU.mult, ALU.add).then_inc(hnT_set, 1)

                def xmT_of(t):
                    dve.wait_ge(xm_done, t + 1)
                    for c in range(CC):
                        dve.tensor_scalar(xmT[:, c, :], ps_d[:, c * P:(c + 1) * P], bias_cols[:, 2, c:c + 1],
                                          None, ALU.add).then_inc(xmT_set, 1)

                def qk_of(t):
                    dve.wait_ge(qkv_done, t + 1)
                    copy(q[:, bass.ds(t, 1)].rearrange("p o h r -> p (o h r)"), ps_f[:, P:P + QK]).then_inc(qk_out, 1)
                    copy(kT[:, bass.ds(t * P, P)], ps_f[0:QK, 0:P]).then_inc(qk_out, 1)
                hn_of(0)
                hnT_of(0)
                hn_of(1)
                with dve.Fori(0, NT - 2) as t:
                    xmT_of(t)
                    hnT_of(t + 1)
                    hn_of(t + 2)
                    qk_of(t)
                xmT_of(NT - 2)
                hnT_of(NT - 1)
                qk_of(NT - 2)
                xmT_of(NT - 1)
                qk_of(NT - 1)
                dve.wait_ge(qk_out, 2 * NT + 2)
                link(dve.tensor_reduce(qm[:], q[:], AX.X, ALU.max))
                dve.tensor_tensor(q[:], q[:], qm[:].unsqueeze(3).to_broadcast([P, NT, MH, KR]), ALU.subtract).then_inc(q_set, 1)
                link(dve.tensor_reduce(kmax[:], kT[:, 0:N], AX.X, ALU.max))
                dve.tensor_scalar(kmax[:], kmax[:], -1.0, None, ALU.mult).then_inc(kmax_set, 1)
                dve.wait_ge(qexp_set, 1)
                link(dve.tensor_reduce(qm[:], q[:], AX.X, ALU.add))
                link(dve.reciprocal(qm[:], qm[:]))
                link(dve.tensor_tensor(q[:], q[:], qm[:].unsqueeze(3).to_broadcast([P, NT, MH, KR]), ALU.mult))
                dve.wait_ge(kexp_set, 1)
                dve.memset(kT[:, N:NP], 0.0).then_inc(qsoft_set, 1)
                with own.loop(NT, 0) as t:
                    dve.wait_ge(qk_turned, t + 2)
                    dve.wait_ge(kv_done, t + 1)
                    copy(qT[:, bass.ds(t * P, P)], ps_a[0:QK, 0:P]).then_inc(qT_set, 1)
                    dve.tensor_copy(ek[:], ps_b[:, 0:QK]).then_inc(qT_set, 1)
                dve.wait_ge(kv_done, NT + 2)
                link(dve.reciprocal(kvr[:], ps_c[0:QK, C:C + 1]))
                dve.scalar_tensor_tensor(kv[:], ps_c[0:QK, 0:C], kvr[:, 0:1], headmask[:], ALU.mult, ALU.mult).then_inc(kv_set, 1)
                dve.wait_ge(kv_turned, 1)
                dve.tensor_copy(kvT[:].rearrange("p c q -> p (c q)"), ps_a[:, 0:CC * QK]).then_inc(kvT_set, 1)
                dve.wait_ge(ko_done, 1)
                dve.tensor_copy(ko[:], ps_b[0:QK, 0:C]).then_inc(ko_set, 1)
                with dve.Fori(0, NT) as t:
                    dve.wait_ge(attn_done, t + 2)
                    dve.tensor_tensor(tile_of(xn, t), ps_d[:, 0:C], tile_of(xn, t), ALU.add).then_inc(fx_set, 1)
                dve.wait_ge(fx_set, NT + 1)
                moments(dve, own, xn, halves, gap, mv)
                root(3)

                def fn_of(t):
                    dve.wait_ge(fn_turned, t + 1)
                    normed(hn[:], t).then_inc(fn_set, 1)

                def fnT_of(t):
                    dve.wait_ge(fn_turned, t + 2)
                    for c in range(CC):
                        dve.tensor_scalar(hnT[:, c, :], ps_a[:, c * P:(c + 1) * P], bias_cols[:, 3, c:c + 1],
                                          bias_cols[:, 4, c:c + 1], ALU.mult, ALU.add).then_inc(fnT_set, 1)

                def mix_of(t):
                    dve.wait_ge(m_done, t + 3)
                    dve.wait_ge(mix_out, 16 * (t + 1))
                    dve.tensor_tensor(mixrow[:], ps_d[:, 0:C], tile_of(xn, t), ALU.add).then_inc(mix_set, 1)
                fn_of(0)
                for t in range(2):
                    fnT_of(t)
                    fn_of(t + 1)
                with dve.Fori(0, NT - 3) as t:
                    fnT_of(t + 2)
                    fn_of(t + 3)
                    mix_of(t)
                fnT_of(NT - 1)
                for t in range(NT - 3, NT):
                    mix_of(t)

            @block.scalar
            def _(act):
                for n in range(2):
                    act.wait_ge(var_set, n + 1)
                    act.activation(std[:], rstd[:], ACT.Sqrt).then_inc(std_set, 1)
                act.sem_inc(h_out, 3)
                act.sem_inc(v_out, 1)

                def xcur_of(t):
                    act.wait_ge(hn_set, t + 1)
                    act.wait_ge(turned, t + 1)
                    act.activation(xcur[:], tile_of(xn, t), ACT.Copy).then_inc(xcur_set, 1)

                def xnT_of():
                    act.activation(xnT[:].rearrange("p c n -> p (c n)"), ps_a[:, 0:C], ACT.Copy).then_inc(xnT_set, 1)

                def outputs(t):
                    act.wait_ge(h_done, t + 1)
                    act.wait_ge(tab_out, 16 * (t + 1))
                    act.activation(tabrow[:], ps_c[:, 0:C + HEADS1], ACT.Copy).then_inc(row_set, 1)
                    act.activation(tile_of(h1, t), ps_c[:, 0:C], ACT.Copy).then_inc(h_out, 1)
                    act.activation(tile_of(es1, t), ps_c[:, C:C + HEADS1], ACT.Copy).then_inc(h_out, 1)
                    act.activation(tile_of(ed1, t), ps_c[:, C + HEADS1:C + 2 * HEADS1], ACT.Copy).then_inc(h_out, 1)
                    act.wait_ge(qkv_done, t + 1)
                    act.activation(v1[:, bass.ds(t, 1), 0:C].rearrange("p o c -> p (o c)"), ps_e[:, 0:C],
                                   ACT.Copy).then_inc(v_out, 1)
                xcur_of(0)
                act.wait_ge(turned, 2)
                xnT_of()
                xcur_of(1)
                with act.Fori(0, NT - 2) as t:
                    act.wait_ge(turned, t + 3)
                    xnT_of()
                    xcur_of(t + 2)
                    outputs(t)
                act.wait_ge(turned, NT + 1)
                xnT_of()
                outputs(NT - 2)
                outputs(NT - 1)
                act.wait_ge(q_set, 1)
                act.activation(q[:], q[:], ACT.Exp).then_inc(qexp_set, 1)
                act.wait_ge(kmax_set, 1)
                act.activation(kT[:, 0:N], kT[:, 0:N], ACT.Exp, bias=kmax[:, 0:1]).then_inc(kexp_set, 1)
                act.wait_ge(qsoft_set, 1)
                with act.Fori(0, NT) as t:
                    act.wait_ge(qk_turned, t + 1)
                    act.activation(qcur[:], q[:, bass.ds(t, 1)].rearrange("p o h r -> p (o h r)"), ACT.Copy).then_inc(cur_set, 1)
                    act.activation(kcur[:], kT[:, bass.ds(t * P, P)], ACT.Copy).then_inc(cur_set, 1)
                act.wait_ge(qT_set, 2 * NT)
                with act.Fori(0, NT) as t:
                    act.wait_ge(attn_done, t + 1)
                    act.activation(qTcur[:], qT[:, bass.ds(t * P, P)], ACT.Copy).then_inc(qTcur_set, 1)
                act.wait_ge(var_set, 3)
                act.activation(std[:], rstd[:], ACT.Sqrt).then_inc(std_set, 1)
                act.preload_act_table(ACT.Gelu)

                def gelu(t, y):
                    act.wait_ge(ff_done, t + 1)
                    act.wait_ge(m_done, t + 1)
                    for f in range(FM):
                        act.activation(gT[:, y, f, :], ps_ff[y][f // FB][:, f % FB * P:(f % FB + 1) * P], ACT.Gelu,
                                       bias=b1_col[:, f:f + 1]).then_inc(g_set, 1)
                with act.Fori(0, NT // 2) as i:
                    for y in range(2):
                        gelu(i * 2 + y, y)
                gelu(NT - 1, 0)

            @block.tensor
            def _(pe):
                pe.wait_ge(counted, 1)
                pe.matmul(ps_a[:, 0:NT], ones[:], cnt[:], start=True, stop=True).then_inc(prefixed, 1)
                pe.matmul(ps_b[:, 0:NT], below[:], cnt[:], start=True, stop=True).then_inc(prefixed, 1)
                pe.wait_ge(small_in, 16 * 3 * MH)
                pe.wait_ge(w_set, 1)
                pe.wait_ge(w_in, 16 * loads)
                pe.wait_ge(slots_set, 1)
                pe.sem_inc(turned, 1)

                def turn(t):
                    pe.wait_ge(hn_set, t + 1)
                    pe.wait_ge(xcur_set, t + 1)
                    for c in range(CC):
                        pe.transpose(ps_a[:, c * P:(c + 1) * P], xcur[:, c * P:(c + 1) * P], ident[:])
                    for c in range(CC):
                        last = pe.transpose(ps_b[:, c * P:(c + 1) * P], hn[:, c * P:(c + 1) * P], ident[:])
                    last.then_inc(turned, 1)

                def h_and_xm(t):
                    pe.wait_ge(xnT_set, t + 1)
                    pe.wait_ge(h_out, 3 * t + 3)
                    for c in range(CC):
                        last = pe.matmul(ps_c[:, 0:C + 2 * HEADS1], xnT[:, c, :], gat_w[:, c, :], start=c == 0, stop=c == CC - 1)
                    last.then_inc(h_done, 1)
                    pe.wait_ge(hnT_set, 2 * t + 2)
                    for m in range(CC):
                        for c in range(CC):
                            last = pe.matmul(ps_d[:, m * P:(m + 1) * P], wx[:, c, m * P:(m + 1) * P], hnT[:, c, :],
                                             start=c == 0, stop=c == CC - 1)
                    last.then_inc(xm_done, 1)

                def qkv(t):
                    pe.wait_ge(xmT_set, 2 * t + 2)
                    pe.wait_ge(v_out, t + 1)
                    pe.wait_ge(qk_out, 2 * t + 2)
                    for c in range(CC):
                        pe.matmul(ps_e[:, 0:C], xmT[:, c, :], wv[:, c, :], start=c == 0, stop=c == CC - 1)
                    for c in range(CC):
                        pe.matmul(ps_f[:, P:P + QK], xmT[:, c, :], wq[:, c, :], start=c == 0, stop=c == CC - 1)
                    for c in range(CC):
                        last = pe.matmul(ps_f[0:QK, 0:P], wk[:, c, :], xmT[:, c, :], start=c == 0, stop=c == CC - 1)
                    last.then_inc(qkv_done, 1)
                turn(0)
                with pe.Fori(0, NT - 1) as t:
                    h_and_xm(t)
                    turn(t + 1)
                    qkv(t)
                h_and_xm(NT - 1)
                qkv(NT - 1)
                pe.sem_inc(qk_turned, 1)
                pe.wait_ge(h_out, 3 * NT + 3)
                pe.matmul(ps_c[0:QK, 0:C + 1], zrow[:, 0:QK], zrow[:], start=True, stop=False,
                          skip_group_check=True).then_inc(kv_done, 1)
                with pe.Fori(0, NT) as t:
                    pe.wait_ge(cur_set, 2 * t + 2)
                    pe.transpose(ps_a[0:QK, 0:P], qcur[:], ident[:])
                    pe.transpose(ps_b[:, 0:QK], kcur[:], ident[0:QK, 0:QK]).then_inc(qk_turned, 1)
                    pe.wait_ge(qT_set, 2 * t + 2)
                    pe.matmul(ps_c[0:QK, 0:C + 1], ek[:], tile_of(v1, t), start=False, stop=False,
                              skip_group_check=True).then_inc(kv_done, 1)
                pe.matmul(ps_c[0:QK, 0:C + 1], zrow[:, 0:QK], zrow[:], start=False, stop=True,
                          skip_group_check=True).then_inc(kv_done, 1)
                pe.wait_ge(kv_set, 1)
                for c in range(CC):
                    last = pe.transpose(ps_a[:, c * QK:(c + 1) * QK], kv[:, c * P:(c + 1) * P], ident[0:QK, 0:QK])
                last.then_inc(kv_turned, 1)
                pe.wait_ge(kvT_set, 1)
                for c in range(CC):
                    last = pe.matmul(ps_b[0:QK, 0:C], kvT[:, c, :], wo[:, c, :], start=c == 0, stop=c == CC - 1)
                last.then_inc(ko_done, 1)
                pe.wait_ge(ko_set, 1)
                pe.sem_inc(fx_set, 1)
                pe.sem_inc(attn_done, 1)
                with pe.Fori(0, NT) as t:
                    pe.wait_ge(qTcur_set, t + 1)
                    pe.wait_ge(fx_set, t + 1)
                    pe.matmul(ps_d[:, 0:C], qTcur[:], ko[:], start=True, stop=False)
                    pe.matmul(ps_d[:, 0:C], ones[0:1, :], bo_row[:], start=False, stop=True).then_inc(attn_done, 1)
                pe.wait_ge(fx_set, NT + 1)

                def turn_fn(t):
                    pe.wait_ge(fn_set, t + 1)
                    pe.wait_ge(fnT_set, 2 * t + 2)
                    for c in range(CC):
                        last = pe.transpose(ps_a[:, c * P:(c + 1) * P], hn[:, c * P:(c + 1) * P], ident[:])
                    last.then_inc(fn_turned, 1)

                def up(t, y):
                    pe.wait_ge(fnT_set, 2 * t + 4)
                    pe.wait_ge(g_set, FM * (t + 1))
                    for f in range(FM):
                        for c in range(CC):
                            last = pe.matmul(ps_ff[y][f // FB][:, f % FB * P:(f % FB + 1) * P],
                                             w1[:, c, f * P:(f + 1) * P], hnT[:, c, :], start=c == 0, stop=c == CC - 1)
                    last.then_inc(ff_done, 1)

                def down(t, y):
                    pe.wait_ge(g_set, FM * (t + 3))
                    pe.wait_ge(mix_set, t + 1)
                    pe.matmul(ps_d[:, 0:C], ones[0:1, :], b2_row[:], start=True, stop=False)
                    for f in range(FM):
                        last = pe.matmul(ps_d[:, 0:C], gT[:, y, f, :], w2[:, f, :], start=False, stop=f == FM - 1)
                    last.then_inc(m_done, 1)
                pe.sem_inc(fn_turned, 1)
                pe.sem_inc(fnT_set, 2)
                pe.sem_inc(g_set, 2 * FM)
                pe.sem_inc(mix_set, 1)
                pe.sem_inc(m_done, 2)
                turn_fn(0)
                up(0, 0)
                turn_fn(1)
                with pe.Fori(0, (NT - 3) // 2) as i:
                    for y in range(2):
                        up(i * 2 + y + 1, 1 - y)
                        turn_fn(i * 2 + y + 2)
                        down(i * 2 + y, y)
                up(NT - 2, 1)
                turn_fn(NT - 1)
                down(NT - 3, 0)
                up(NT - 1, 0)
                down(NT - 2, 1)
                down(NT - 1, 0)


def edge_tables(nc, k, alloc, sems, sorted_edges, dst_row, src_row):
    with ExitStack() as st:
        sb, sem = alloc(st), sems(st)
        rows = sb("rows", [TR, 4, P, 2], I32)
        part = sb("part", [TR, 4, P], I32)
        names = ("src_f", "dst_lo", "src_hi", "block", "src_lo", "pad")
        src_f, dst_lo, src_hi, block_f, src_lo, pad = (sb(n, [TR, 4, P]) for n in names)
        ps = [st.enter_context(nc.psum_tensor(f"ps_t{j}", [P, 512], F32)) for j in range(4)]
        rows_in, own_s, rows_set, turned = sem("rows_in"), sem("tables_own"), sem("rows_set"), sem("tables_turned")
        rows_out = sem("rows_out")
        with nc.Block() as block:
            @block.sync
            def _(sp):
                sp.dma_start(rows[:].rearrange("t c p w -> t c (p w)"),
                             sorted_edges.rearrange("(c t p) w -> t c (p w)", c=4, p=P)).then_inc(rows_in, 16)
                sp.wait_ge(rows_set, 1)
                sp.dma_start(dst_row.rearrange("(c t p) -> t c p", c=4, p=P), dst_lo[:]).then_inc(rows_out, 16)
                sp.dma_start(src_row.rearrange("(c t p) -> t c p", c=4, p=P), src_lo[:]).then_inc(rows_out, 16)
                sp.wait_ge(rows_out, 32)

            @block.vector
            def _(dve):
                own = Steps(dve, own_s)
                link = own.link
                dve.wait_ge(rows_in, 16)
                src, dst = rows[:, :, :, 0], rows[:, :, :, 1]
                own.did(dve.tensor_copy(src_f[:], src))
                link(dve.tensor_copy(pad[:], dst))
                own.did(dve.tensor_scalar(pad[:], pad[:], float(NP), float(P), ALU.is_ge, ALU.mult))
                link(dve.tensor_scalar(part[:], dst, P - 1, None, ALU.bitwise_and))
                link(dve.tensor_copy(dst_lo[:], part[:]))
                link(dve.tensor_tensor(dst_lo[:], dst_lo[:], pad[:], ALU.add))
                link(dve.tensor_scalar(part[:], src, P - 1, None, ALU.bitwise_and))
                link(dve.tensor_copy(src_lo[:], part[:]))
                link(dve.tensor_scalar(part[:], src, 7, None, ALU.arith_shift_right))
                link(dve.tensor_copy(src_hi[:], part[:]))
                link(dve.tensor_scalar(part[:], dst, 7, None, ALU.arith_shift_right))
                link(dve.tensor_copy(block_f[:], part[:]))
                dve.tensor_scalar(block_f[:], block_f[:], float(NT - 1), None, ALU.min).then_inc(rows_set, 1)
                dve.wait_ge(turned, 4)
                for j, dst_t in enumerate((k["src_col"][:], k["dst_col"][:], k["hi_col"][:])):
                    dve.tensor_copy(dst_t, ps[j][:, 0:TT])
                own.did(dve.memset(k["block_row"][:, 0:BATCH], 0))
                own.did(dve.tensor_copy(k["block_row"][:, BATCH:], ps[3][0:1, 0:TT]))
                own.settle()

            @block.tensor
            def _(pe):
                pe.wait_ge(rows_set, 1)
                for j, t in enumerate((src_f, dst_lo, src_hi, block_f)):
                    for c in range(4):
                        last = pe.transpose(ps[j][:, c * TR:(c + 1) * TR], t[:, c, :], k["ident"][0:TR, 0:TR])
                    last.then_inc(turned, 1)


def segment_max(nc, layer, H, k, es, ed, top_e, em, alloc, sems, src_row):
    with ExitStack() as st:
        sb, sem = alloc(st), sems(st)

        def s(name):
            return sem(f"{name}_{layer}")
        low, low_row, floor_ = sb("low", [P, 1]), sb("low_row", [1, 1]), sb("floor", [P, 1])
        raised = sb("raised", [P, NT, H])
        zeros = sb("zeros", [1, H * P])
        src_b = sb("src_b", [P, 2, BATCH * P])
        pick_lo = sb("pick_lo", [P, 2, BATCH * P])
        pick_hi = sb("pick_hi", [P, 2, BATCH, NT])
        picked = sb("picked", [P, BATCH, NT, H])
        es_e = sb("es_e", [P, 2, BATCH, H])
        spread = sb("spread", [P, 2, BATCH, H, P])
        best = sb("best", [P, BATCH, H])
        is_dst = sb("is_dst", [P, 2, BATCH, P if H > 1 else 1])
        iota_row, iota_col = k["iota_row"], k["iota_col"]
        ps_f = [st.enter_context(nc.psum_tensor(f"ps_f{y}_{layer}", [P, 512], F32)) for y in range(2)]
        ps_v = st.enter_context(nc.psum_tensor(f"ps_v_{layer}", [P, BATCH, 512], F32))
        own_s, low_set, low_turned, low_spread = s("max_own"), s("low_set"), s("low_turned"), s("low_spread")
        src_in = [s(f"src_in{y}") for y in range(2)]
        picks_set, fetched, fetch_read = s("picks_set"), s("fetched"), s("fetch_read")
        es_set, dst_set, spread_set, turned, best_set = s("es_set"), s("dst_set"), s("spread_set"), s("spread_turned"), s("best_set")
        picks_free = s("picks_free")
        src_rows = src_row.rearrange("(b n) -> b n", n=BATCH * P)

        with nc.Block() as block:
            @block.sync
            def _(sp):
                def fetch(i, y):
                    b = i * 2 + y
                    sp.wait_ge(picks_free, b + 1)
                    sp.dma_start(src_b[:, y, :], src_rows[bass.ds(b, 1), :].to_broadcast([P, BATCH * P])).then_inc(src_in[y], 16)
                with sp.Fori(0, NB // 2) as i:
                    fetch(i, 0)
                    fetch(i, 1)
                fetch(NB // 2, 0)

            @block.vector
            def _(dve):
                own = Steps(dve, own_s)
                link = own.link
                own.did(dve.memset(zeros[:], 0.0))
                link(dve.tensor_reduce(low[:], es[:].rearrange("p t h -> p (t h)"), AX.X, ALU.min))
                dve.sem_inc(low_set, 1)
                dve.wait_ge(low_turned, 1)
                dve.tensor_reduce(low_row[:], ps_f[0][0:1, 0:P], AX.X, ALU.min).then_inc(low_set, 1)
                dve.wait_ge(low_spread, 1)
                link(dve.tensor_scalar(floor_[:], ps_f[1][:, 0:1], -1.0, None, ALU.add))
                link(dve.tensor_scalar(raised[:], es[:], floor_[:, 0:1], None, ALU.subtract))
                link(dve.tensor_tensor(top_e[:], raised[:], k["loops"][:].unsqueeze(2).to_broadcast([P, NT, H]), ALU.mult))
                dve.sem_inc(picks_free, 2)
                dve.sem_inc(fetch_read, 2)
                dve.sem_inc(best_set, BATCH)

                def picks(i, y):
                    b = i * 2 + y
                    dve.wait_ge(src_in[y], (i + 1) * 16)
                    dve.wait_ge(fetched, b + 1)
                    dve.tensor_scalar(pick_lo[:, y, :], src_b[:, y, :], iota_col[:, 0:1], None, ALU.is_equal).then_inc(picks_free, 1)
                    dve.tensor_tensor(pick_hi[:, y], iota_row[:, 0:NT].unsqueeze(1).to_broadcast([P, BATCH, NT]),
                                      k["hi_col"][:, bass.ds(b * BATCH, BATCH)].unsqueeze(2).to_broadcast([P, BATCH, NT]),
                                      ALU.is_equal).then_inc(picks_set, 1)

                def fold(b, between):
                    blocks = blocks_of(nc, mybir.EngineType.DVE, k, b)
                    for j in range(BATCH + 1):
                        if j < BATCH:
                            between(j)
                            dve.wait_ge(turned, BATCH * (b + 2) + j + 1)
                            dve.tensor_reduce(best[:, j, :], ps_v[:, j, 0:H * P].rearrange("p (h e) -> p h e", h=H), AX.X,
                                              ALU.max).then_inc(best_set, 1)
                        if j > 0:
                            at = top_e[:, bass.ds(blocks[j - 1], 1), :].rearrange("p o h -> p (o h)")
                            dve.wait_ge(best_set, BATCH * (b + 2) + j)
                            own.settle()
                            own.did(dve.tensor_tensor(at, at, best[:, j - 1, :], ALU.max))

                def step(i, y):
                    b = i * 2 + y
                    picks(*((i, 1) if y == 0 else (i + 1, 0)))
                    dve.wait_ge(fetched, b + 3)
                    dve.wait_ge(picks_set, b + 1)
                    dve.tensor_tensor(picked[:], ps_f[y][:, 0:BATCH * NT * H].rearrange("p (k t h) -> p k t h", k=BATCH, h=H),
                                      pick_hi[:, y].unsqueeze(3).to_broadcast([P, BATCH, NT, H]), ALU.mult).then_inc(fetch_read, 1)
                    dve.wait_ge(fetch_read, b + 3)
                    dve.tensor_reduce(es_e[:, y], picked[:].rearrange("p k t h -> p k h t"), AX.X, ALU.add).then_inc(es_set, 1)
                    dve.wait_ge(turned, BATCH * (b + 1))

                    def to_dst(j):
                        dst = k["dst_col"][:, bass.ds(b * BATCH + j, 1)]
                        if H == 1:
                            dve.wait_ge(es_set, b + 1)
                            last = dve.tensor_scalar(spread[:, y, j, 0, :], iota_row[:], dst, es_e[:, y, j, 0:1],
                                                     ALU.is_equal, ALU.mult)
                        else:
                            last = dve.tensor_scalar(is_dst[:, y, j, :], iota_row[:], dst, None, ALU.is_equal)
                        last.then_inc(dst_set, 1)
                    fold(b - 1, to_dst)

                picks(0, 0)
                with own.loop(NB // 2, 2 * BATCH) as i:
                    step(i, 0)
                    step(i, 1)
                fold(NB - 1, lambda j: None)
                own.settle()
                m = em[:, :, H:2 * H]
                link(dve.tensor_copy(em[:, :, 0:H], ed[:]))
                link(dve.scalar_tensor_tensor(top_e[:], top_e[:], floor_[:, 0:1], ed[:], ALU.add, ALU.add))
                link(dve.scalar_tensor_tensor(m, top_e[:], SLOPE, top_e[:], ALU.mult, ALU.max))

            if H > 1:
                @block.scalar
                def _(act):
                    with act.Fori(0, NB // 2) as i:
                        for y in range(2):
                            b = i * 2 + y
                            act.wait_ge(turned, BATCH * (b + 1))
                            act.wait_ge(es_set, b + 1)
                            for j in range(BATCH):
                                act.wait_ge(dst_set, BATCH * b + j + 1)
                                for h in range(H):
                                    act.activation(spread[:, y, j, h, :], is_dst[:, y, j, :], ACT.Copy,
                                                   scale=es_e[:, y, j, h:h + 1]).then_inc(spread_set, 1)

            @block.tensor
            def _(pe):
                pe.sem_inc(turned, BATCH)
                pe.wait_ge(low_set, 1)
                for j in range(BATCH):
                    pe.matmul(ps_v[:, j, 0:H * P], zeros[:, 0:P], zeros[:, 0:H * P], start=True, stop=True).then_inc(turned, 1)
                pe.transpose(ps_f[0][0:1, 0:P], low[:], k["ident"][:]).then_inc(low_turned, 1)
                pe.wait_ge(low_set, 2)
                pe.matmul(ps_f[1][:, 0:1], k["ones"][0:1, :], low_row[:], start=True, stop=True).then_inc(low_spread, 1)
                pe.sem_inc(fetched, 2)

                def fetch(i, y):
                    b = i * 2 + y
                    pe.wait_ge(picks_set, b + 1)
                    pe.wait_ge(fetch_read, b + 1)
                    for j in range(BATCH):
                        last = pe.matmul(ps_f[y][:, j * NT * H:(j + 1) * NT * H], pick_lo[:, y, j * P:(j + 1) * P],
                                         raised[:].rearrange("p t h -> p (t h)"), start=True, stop=True)
                    last.then_inc(fetched, 1)

                def step(i, y):
                    b = i * 2 + y
                    fetch(*((i, 1) if y == 0 else (i + 1, 0)))
                    if H == 1:
                        pe.wait_ge(dst_set, BATCH * (b + 1))
                    else:
                        pe.wait_ge(spread_set, BATCH * H * (b + 1))
                    for j in range(BATCH):
                        pe.wait_ge(best_set, BATCH * (b + 1) + j + 1)
                        for h in range(H):
                            last = pe.transpose(ps_v[:, j, h * P:(h + 1) * P], spread[:, y, j, h, :], k["ident"][:])
                        last.then_inc(turned, 1)

                fetch(0, 0)
                with pe.Fori(0, NB // 2) as i:
                    step(i, 0)
                    step(i, 1)


def weighted_sum(nc, layer, H, k, em, es, acc, wself, table, alloc, sems, dst_row):
    with ExitStack() as st:
        sb, sem = alloc(st), sems(st)

        def s(name):
            return sem(f"{name}_{layer}")
        W = C + H
        BY_ACT = 2 if H > 1 else BATCH
        zeros = sb("zeros", [1, W])
        dst_b = sb("dst_b", [P, 2, BATCH * P])
        to_edge = sb("to_edge", [P, 2, BATCH * P])
        to_dst = sb("to_dst", [P, DEPTH, BATCH, P])
        rows = sb("rows_h", [P, DEPTH, BATCH, W])
        logit, leaky = sb("logit", [P, 2, BATCH, H]), sb("leaky", [P, 2, BATCH, H])
        cur = sb("cur_src", [P, DEPTH, BATCH], I32)
        scratch = sb("pool_scratch_h", [1, 1])
        tself = sb("tself", [P, NT, H])
        ps_e = [st.enter_context(nc.psum_tensor(f"ps_e{y}_{layer}", [P, 512], F32)) for y in range(2)]
        ps_o = st.enter_context(nc.psum_tensor(f"ps_o_{layer}", [P, BATCH, 512], F32))
        own_s, self_set, self_exp = s("sum_own"), s("self_set"), s("self_exp")
        dst_in = [s(f"dst_in{y}") for y in range(2)]
        gathered = [[s(f"gathered{y}{j}") for j in range(BATCH)] for y in range(DEPTH)]
        copied, onehots, fetched, ed_read = s("copied"), s("onehots"), s("ed_fetched"), s("ed_read")
        zeros_set, act_msg, to_dst_set = s("zeros_set"), s("act_msg"), s("to_dst_set")
        logit_set, w_set, msg_set, summed, added = s("logit_set"), s("w_set"), s("msg_set"), s("summed"), s("added")
        dst_rows = dst_row.rearrange("(b n) -> b n", n=BATCH * P)

        with nc.Block() as block:
            @block.sync
            def _(sp):
                def fetch(i, y):
                    b = i * 2 + y
                    sp.wait_ge(onehots, b + 1)
                    sp.dma_start(dst_b[:, y, :], dst_rows[bass.ds(b, 1), :].to_broadcast([P, BATCH * P])).then_inc(dst_in[y], 16)
                with sp.Fori(0, NB // 2) as i:
                    fetch(i, 0)
                    fetch(i, 1)
                fetch(NB // 2, 0)

            @block.gpsimd
            def _(pool):
                pool.memset(scratch[:], 0.0)

                def gather(i, y):
                    b = i * DEPTH + y
                    pool.wait_ge(summed, BATCH * (b + 1))
                    pool.tensor_copy(cur[:, y, :], k["src_col"][:, bass.ds(b * BATCH, BATCH)]).then_inc(copied, 1)
                    pool.wait_ge(copied, b + 1)
                    pool.tensor_tensor(scratch[:], k["ones"][0:1, 0:1], k["ones"][0:1, 0:1], ALU.add)
                    for j in range(BATCH):
                        pool.indirect_dma_start(rows[:, y, j, :], None, table,
                                                bass.IndirectOffsetOnAxis(cur[:, y, j:j + 1], 0)).then_inc(gathered[y][j], 16)
                with pool.Fori(0, NB // DEPTH) as i:
                    for y in range(DEPTH):
                        gather(i, y)

            @block.vector
            def _(dve):
                own = Steps(dve, own_s)
                link = own.link
                m = em[:, :, H:2 * H]
                dve.memset(zeros[:], 0.0).then_inc(zeros_set, 1)
                own.did(dve.memset(acc[:], 0.0))
                link(dve.tensor_tensor(tself[:], es[:], em[:, :, 0:H], ALU.add))
                link(dve.scalar_tensor_tensor(tself[:], tself[:], SLOPE, tself[:], ALU.mult, ALU.max))
                link(dve.tensor_tensor(tself[:], tself[:], m, ALU.subtract))
                dve.tensor_scalar(tself[:], tself[:], 1.0, None, ALU.min).then_inc(self_set, 1)
                dve.sem_inc(onehots, 2)
                dve.sem_inc(ed_read, 2)
                dve.sem_inc(added, BATCH)

                def onehot(i, y4, j):
                    b = i * DEPTH + y4
                    if j == 0:
                        dve.wait_ge(summed, BATCH * (b + 1))
                    dve.tensor_scalar(to_dst[:, y4, j, :], k["iota_row"][:], k["dst_col"][:, bass.ds(b * BATCH + j, 1)],
                                      None, ALU.is_equal).then_inc(to_dst_set, 1)
                    if j == BATCH - 1:
                        y = y4 % 2
                        dve.wait_ge(dst_in[y], (i * (DEPTH // 2) + y4 // 2 + 1) * 16)
                        dve.wait_ge(fetched, b + 1)
                        dve.tensor_scalar(to_edge[:, y, :], dst_b[:, y, :], k["iota_col"][:, 0:1], None, ALU.is_equal).then_inc(onehots, 1)

                def add(b, between):
                    blocks = blocks_of(nc, mybir.EngineType.DVE, k, b)
                    for j in range(BATCH):
                        at = acc[:, bass.ds(blocks[j], 1), :].rearrange("p o c -> p (o c)")
                        dve.wait_ge(summed, BATCH * (b + DEPTH) + j + 1)
                        dve.wait_ge(added, BATCH * (b + 2) + j)
                        dve.tensor_tensor(at, at, ps_o[:, j, 0:W], ALU.add).then_inc(added, 1)
                        between(j)

                def step(i, y4):
                    b, y = i * DEPTH + y4, y4 % 2
                    after = (i, y4 + 1) if y4 + 1 < DEPTH else (i + 1, 0)
                    for j in range(BATCH):
                        dve.wait_ge(gathered[y4][j], (i + 1) * 16)
                    dve.wait_ge(fetched, b + 3)
                    edm = ps_e[y][:, 0:BATCH * 2 * H].rearrange("p (k w) -> p k w", w=2 * H)
                    own.did(dve.tensor_tensor(logit[:, y], rows[:, y4, :, C:W], edm[:, :, 0:H], ALU.add))
                    onehot(*after, 0)
                    own.settle()
                    own.did(dve.scalar_tensor_tensor(leaky[:, y], logit[:, y], SLOPE, logit[:, y], ALU.mult, ALU.max))
                    onehot(*after, 1)
                    own.settle()
                    dve.tensor_tensor(logit[:, y], leaky[:, y], edm[:, :, H:2 * H], ALU.subtract).then_inc(ed_read, 1)
                    onehot(*after, 2)
                    dve.wait_ge(ed_read, b + 3)
                    dve.tensor_scalar(leaky[:, y], logit[:, y], 1.0, None, ALU.min).then_inc(logit_set, 1)
                    onehot(*after, 3)

                    def message(j):
                        j += BY_ACT
                        if j < BATCH:
                            dve.wait_ge(w_set, b + 1)
                            msg = rows[:, y4, j, 0:C].rearrange("p (h d) -> p h d", h=H)
                            dve.tensor_tensor(msg, msg, rows[:, y4, j, C:W].unsqueeze(2).to_broadcast([P, H, C // H]),
                                              ALU.mult).then_inc(msg_set, 1)
                    add(b - 1, message)

                for j in range(BATCH):
                    onehot(0, 0, j)
                with own.loop(NB // DEPTH, DEPTH * 2) as i:
                    for y in range(DEPTH):
                        step(i, y)
                add(NB - 1, lambda j: None)
                dve.wait_ge(added, BATCH * (NB + 2))
                dve.wait_ge(self_exp, 1)
                link(dve.tensor_tensor(wself[:], wself[:], k["loops"][:].unsqueeze(2).to_broadcast([P, NT, H]), ALU.mult))

            @block.scalar
            def _(act):
                act.wait_ge(self_set, 1)
                act.activation(wself[:], tself[:], ACT.Exp).then_inc(self_exp, 1)
                with act.Fori(0, NB // DEPTH) as i:
                    for y in range(DEPTH):
                        b = i * DEPTH + y
                        act.wait_ge(logit_set, b + 1)
                        act.activation(rows[:, y, :, C:W], leaky[:, y % 2], ACT.Exp).then_inc(w_set, 1)
                        act.wait_ge(w_set, b + 1)
                        for j in range(BY_ACT):
                            for h in range(H):
                                msg = rows[:, y, j, h * (C // H):(h + 1) * (C // H)]
                                act.activation(msg, msg, ACT.Copy, scale=rows[:, y, j, C + h:C + h + 1]).then_inc(act_msg, 1)

            @block.tensor
            def _(pe):
                pe.sem_inc(fetched, 2)
                pe.sem_inc(summed, (DEPTH - 1) * BATCH)
                pe.wait_ge(zeros_set, 1)
                for j in range(BATCH):
                    pe.matmul(ps_o[:, j, 0:W], zeros[:, 0:P], zeros[:], start=True, stop=True).then_inc(summed, 1)

                def fetch(i, y4):
                    b, y = i * DEPTH + y4, y4 % 2
                    blocks = blocks_of(nc, mybir.EngineType.PE, k, b)
                    pe.wait_ge(onehots, b + 3)
                    pe.wait_ge(ed_read, b + 1)
                    for j in range(BATCH):
                        last = pe.matmul(ps_e[y][:, j * 2 * H:(j + 1) * 2 * H], to_edge[:, y, j * P:(j + 1) * P],
                                         em[:, bass.ds(blocks[j], 1), :].rearrange("p o w -> p (o w)"), start=True, stop=True)
                    last.then_inc(fetched, 1)

                def step(i, y4):
                    b, y = i * DEPTH + y4, y4 % 2
                    fetch(*((i, y4 + 1) if y4 + 1 < DEPTH else (i + 1, 0)))
                    pe.wait_ge(to_dst_set, BATCH * (b + 1))
                    for j in range(BATCH):
                        if j < BY_ACT:
                            pe.wait_ge(act_msg, H * (BY_ACT * b + j + 1))
                        else:
                            pe.wait_ge(msg_set, (BATCH - BY_ACT) * b + j - BY_ACT + 1)
                        pe.wait_ge(added, BATCH * (b + 1) + j + 1)
                        pe.matmul(ps_o[:, j, 0:W], to_dst[:, y4, j, :], rows[:, y4, j, :], start=True, stop=True).then_inc(summed, 1)

                fetch(0, 0)
                with pe.Fori(0, NB // DEPTH) as i:
                    for y in range(DEPTH):
                        step(i, y)

def tile_of(t3, t):
    return t3[:, bass.ds(t, 1), :].rearrange("p o c -> p (o c)")


def aggregate(dve, own, H, h1, acc, wself, bias_b):
    link = own.link

    def by_head(ap):
        return ap.rearrange("p t (h d) -> p t h d", h=H)

    def wide(w):
        return w[:].unsqueeze(3).to_broadcast([P, NT, H, C // H])
    link(dve.tensor_tensor(by_head(h1[:]), by_head(h1[:]), wide(wself[0]), ALU.mult))
    link(dve.tensor_tensor(h1[:], h1[:], acc[:, :, 0:C], ALU.add))
    link(dve.tensor_tensor(by_head(h1[:]), by_head(h1[:]), wide(wself[1]), ALU.mult))
    link(dve.tensor_tensor(h1[:], h1[:], bias_b[:].unsqueeze(1).to_broadcast([P, NT, C]), ALU.add))


def moments(dve, own, src, halves, gap, mv):
    with own.loop(NT, 1) as t:
        own.did(dve.bn_stats(tile_of(halves, t), tile_of(src, t)))
    own.settle()
    mean, var = mv[:, :, 0], mv[:, :, 1]
    own.did(dve.tensor_tensor(gap[:], halves[:, :, 1], halves[:, :, 4], ALU.subtract))
    own.did(dve.tensor_tensor(mean, halves[:, :, 1], halves[:, :, 4], ALU.add))
    own.link(dve.tensor_tensor(var, halves[:, :, 2], halves[:, :, 5], ALU.add))
    own.did(dve.tensor_scalar(mean, mean, 0.5, None, ALU.mult))
    own.did(dve.tensor_scalar(var, var, 1.0 / C, None, ALU.mult))
    own.link(dve.tensor_tensor(gap[:], gap[:], gap[:], ALU.mult))
    own.link(dve.scalar_tensor_tensor(var, gap[:], 0.25, var, ALU.mult, ALU.add))


def between_layers(nc, a, k, acc, wself, alloc, sems, table2):
    with ExitStack() as st:
        sb, sem = alloc(st), sems(st)
        h1, gat_w = k["h1"], k["gat2_w"]
        bias_b, hn = sb("gnn_b1_b", [P, C]), sb("on", [P, C])
        g_col, b_col = sb("g_col", [P, CC]), sb("b_col", [P, CC])
        rden = sb("rden", [P, NT, HEADS1])
        halves, gap, mv = sb("halves_o", [P, NT, 6]), sb("gap_o", [P, NT]), sb("mv_o", [P, NT, 2])
        std, rstd = sb("std_o", [P, NT]), sb("rstd_o", [P, NT])
        rT = sb("rT", [P, CC, P])
        tabrow = sb("tabrow2", [P, C + 1])
        ps_t = st.enter_context(nc.psum_tensor("ps_t", [P, 512], F32))
        ps_h = st.enter_context(nc.psum_tensor("ps_h", [P, 512], F32))
        b_in, own_s, var_set, std_set, on_set = (sem(n) for n in ("mid_in", "mid_own", "mid_var", "mid_std", "on_set"))
        turned, rT_set, h_done, row_set, h_out, row_out = (sem(n) for n in ("mid_turned", "rT_set", "mid_h", "row2_set", "h2_out", "row2_out"))
        with nc.Block() as block:
            @block.sync
            def _(sp):
                sp.dma_start(bias_b[:], a["L0_gnn_b1"].partition_broadcast(P)).then_inc(b_in, 16)
                with nc.allow_non_contiguous_dma(reason="a bias of a few hundred values, one a partition"):
                    sp.dma_start(g_col[:], a["L0_gnn_ln_g"].rearrange("(c p) -> p c", p=P)).then_inc(b_in, 16)
                    sp.dma_start(b_col[:], a["L0_gnn_ln_b"].rearrange("(c p) -> p c", p=P)).then_inc(b_in, 16)
                sp.sem_inc(row_out, 16)
                with sp.Fori(0, NT) as t:
                    sp.wait_ge(row_set, t + 1)
                    sp.dma_start(table2[bass.ds(t * P, P), :], tabrow[:]).then_inc(row_out, 16)
                sp.wait_ge(row_out, 16 * (NT + 1))

            @block.vector
            def _(dve):
                own = Steps(dve, own_s)
                link = own.link
                link(dve.tensor_tensor(rden[:], acc[:, :, C:C + HEADS1], wself[:], ALU.add))
                link(dve.tensor_scalar(rden[:], rden[:], 1e-30, None, ALU.max))
                link(dve.reciprocal(rden[:], rden[:]))
                dve.wait_ge(b_in, 48)
                aggregate(dve, own, HEADS1, h1, acc, (wself, rden), bias_b)
                moments(dve, own, h1, halves, gap, mv)
                dve.tensor_scalar(rstd[:], mv[:, :, 1], EPS, None, ALU.add).then_inc(var_set, 1)
                dve.wait_ge(std_set, 1)
                link(dve.reciprocal(rstd[:], std[:]))
                with own.loop(NT, 0) as t:
                    dve.wait_ge(turned, t + 1)
                    dve.tensor_scalar(hn[:], tile_of(h1, t), mv[:, bass.ds(t, 1), 0:1].rearrange("p o c -> p (o c)"),
                                      rstd[:, bass.ds(t, 1)], ALU.subtract, ALU.mult).then_inc(on_set, 1)

            @block.scalar
            def _(act):
                act.wait_ge(var_set, 1)
                act.activation(std[:], rstd[:], ACT.Sqrt).then_inc(std_set, 1)
                act.wait_ge(b_in, 48)
                act.sem_inc(h_out, 3)
                with act.Fori(0, NT) as t:
                    act.wait_ge(turned, t + 2)
                    for c in range(CC):
                        act.activation(rT[:, c, :], ps_t[:, c * P:(c + 1) * P], ACT.Relu, bias=b_col[:, c:c + 1],
                                       scale=g_col[:, c:c + 1]).then_inc(rT_set, 1)
                    act.wait_ge(h_done, t + 1)
                    act.wait_ge(row_out, 16 * (t + 1))
                    act.activation(tabrow[:], ps_h[:, 0:C + 1], ACT.Copy).then_inc(row_set, 1)
                    act.activation(tile_of(h1, t), ps_h[:, 0:C], ACT.Copy).then_inc(h_out, 1)
                    act.activation(k["es2"][:, bass.ds(t, 1), 0], ps_h[:, C:C + 1], ACT.Copy).then_inc(h_out, 1)
                    act.activation(k["ed2"][:, bass.ds(t, 1), 0], ps_h[:, C + 1:C + 2], ACT.Copy).then_inc(h_out, 1)

            @block.tensor
            def _(pe):
                pe.sem_inc(turned, 1)
                with pe.Fori(0, NT) as t:
                    pe.wait_ge(on_set, t + 1)
                    for c in range(CC):
                        last = pe.transpose(ps_t[:, c * P:(c + 1) * P], hn[:, c * P:(c + 1) * P], k["ident"][:])
                    last.then_inc(turned, 1)
                    pe.wait_ge(rT_set, 2 * t + 2)
                    pe.wait_ge(h_out, 3 * t + 3)
                    for c in range(CC):
                        last = pe.matmul(ps_h[:, 0:C + 2], rT[:, c, :], gat_w[:, c, :], start=c == 0, stop=c == CC - 1)
                    last.then_inc(h_done, 1)


def experts(nc, a, k, acc, wself, alloc, sems, mixed, out):
    with ExitStack() as st:
        sb, sem = alloc(st), sems(st)
        r = k["h1"]
        bias_b, hn = sb("gnn_b2_b", [P, C]), sb("rn", [P, C])
        rden = sb("rden_r", [P, NT, 1])
        halves, gap, mv = sb("halves_r", [P, NT, 6]), sb("gap_r", [P, NT]), sb("mv_r", [P, NT, 2])
        std, rstd = sb("std_r", [P, NT]), sb("rstd_r", [P, NT])
        GROUP = 5
        assert NT % GROUP == 0 and NT // GROUP % 2 == 1
        add = sb("add", [P, 2, 2, GROUP, C])
        w1, w2 = sb("ffn_w1", [P, EX * CC, ED]), sb("ffn_w2", [P, EX * FE, C])
        b1_col, b2 = sb("ffn_b1_col", [P, EX * FE]), sb("ffn_b2", [EX, C])
        wg = sb("wg", [P, CC, EX])
        gate_rows = sb("gate_rows", [1, 2, EX])
        xT_cur = sb("xT_cur", [P, CC, P])
        lg, lg2 = sb("lg", [P, NT, EX]), sb("lg2", [P, NT, EX])
        eq, first, second, place = (sb(n, [P, NT, EX]) for n in ("eq", "first", "second", "place"))
        v0, v1, w0, w1_ = (sb(n, [P, NT]) for n in ("v0", "v1", "w0", "w1_"))
        c_cur, cT = sb("c_cur", [P, EX]), sb("cT", [EX, P])
        hT = sb("hT", [P, 2, FE, P])
        xT = acc[:].rearrange("p t c -> p (t c)")[:, 0:CC * NP].rearrange("p (c n) -> p c n", c=CC)
        ps_t = st.enter_context(nc.psum_tensor("ps_xt", [P, 512], F32))
        ps_c = st.enter_context(nc.psum_tensor("ps_cb", [P, 512], F32))
        ps_h = [st.enter_context(nc.psum_tensor(f"ps_eh{y}", [P, 512], F32)) for y in range(2)]
        ps_y = [st.enter_context(nc.psum_tensor(f"ps_ey{y}", [P, 512], F32)) for y in range(2)]
        names = ("small_in", "w_in", "own", "var", "std", "rn_set", "turned", "xT_set", "lg_done", "lg_set",
                 "gap_set", "gap_exp", "comb_set", "c_set", "c_turned", "cT_set", "bias_done", "w1_done", "h_set",
                 "w2_done", "added", "stored", "used", "xT_all")
        S = {n: sem("ffn_" + n) for n in names}
        add_in = [sem(f"ffn_add_in{y}") for y in range(2)]
        comb = lg2

        with nc.Block() as block:
            @block.sync
            def _(sp):
                sp.dma_start(bias_b[:], a["L0_gnn_b2"].partition_broadcast(P)).then_inc(S["small_in"], 16)
                sp.dma_start(wg[:], a["L0_ffn_Wg"].rearrange("(c p) n -> p c n", p=P)).then_inc(S["small_in"], 16)
                sp.dma_start(gate_rows[:, 0, :], a["L0_ffn_bg"].rearrange("(o n) -> o n", o=1)).then_inc(S["small_in"], 16)
                sp.dma_start(gate_rows[:, 1, :], a["L0_ffn_bias"].rearrange("(o n) -> o n", o=1)).then_inc(S["small_in"], 16)
                sp.dma_start(b2[:], a["L0_ffn_b2"]).then_inc(S["small_in"], 16)
                with nc.allow_non_contiguous_dma(reason="biases, one a partition"):
                    for e in range(EX):
                        sp.dma_start(b1_col[:, e * FE:(e + 1) * FE], a["L0_ffn_b1"][e].rearrange("(f p) -> p f", p=P)).then_inc(S["small_in"], 16)
                for gr in range(NT // GROUP):
                    if gr > 1:
                        sp.wait_ge(S["used"], gr - 1)
                    lo, n, y = gr * GROUP, GROUP if gr < NT // GROUP - 1 else GROUP - 1, gr % 2
                    sp.dma_start(add[:, y, 0, 0:n, :], a["x"][lo * P:(lo + n) * P, :].rearrange("(t p) c -> p t c", p=P)).then_inc(add_in[y], 16)
                    sp.dma_start(add[:, y, 1, :, :], mixed[lo * P:(lo + GROUP) * P, :].rearrange("(t p) c -> p t c", p=P)).then_inc(add_in[y], 16)
                    if n < GROUP:
                        sp.dma_start(add[0:LAST, y, 0, n, :], a["x"][(NT - 1) * P:N, :]).then_inc(add_in[y], 16)
                with sp.Fori(0, NT - 1) as t:
                    sp.wait_ge(S["added"], (EX + 1) * (t + 1) + 2)
                    sp.dma_start(out[bass.ds(t * P, P), :], tile_of(r, t)).then_inc(S["stored"], 16)
                sp.wait_ge(S["added"], (EX + 1) * NT + 2)
                sp.dma_start(out[(NT - 1) * P:N, :], r[0:LAST, NT - 1, :]).then_inc(S["stored"], 16)
                sp.wait_ge(S["stored"], 16 * NT)

            @block.vector
            def _(dve):
                own = Steps(dve, S["own"])
                link = own.link
                link(dve.tensor_tensor(rden[:], acc[:, :, C:C + 1], wself[:], ALU.add))
                link(dve.tensor_scalar(rden[:], rden[:], 1e-30, None, ALU.max))
                link(dve.reciprocal(rden[:], rden[:]))
                dve.wait_ge(S["small_in"], 16 * (5 + EX))
                aggregate(dve, own, 1, r, acc, (wself, rden), bias_b)
                for gr in range(NT // GROUP):
                    last = gr == NT // GROUP - 1
                    dve.wait_ge(add_in[gr % 2], 32 * (gr // 2 + 1) + (16 if last else 0))
                    at = r[:, gr * GROUP:(gr + 1) * GROUP, :]
                    n = GROUP - 1 if last else GROUP
                    own.did(dve.tensor_tensor(at[:, 0:n], at[:, 0:n], add[:, gr % 2, 0, 0:n], ALU.add))
                    if last:
                        own.did(dve.tensor_tensor(at[0:LAST, n], at[0:LAST, n], add[0:LAST, gr % 2, 0, n], ALU.add))
                    own.settle()
                    link(dve.tensor_tensor(at, at, add[:, gr % 2, 1], ALU.add))
                    dve.sem_inc(S["used"], 1)
                moments(dve, own, r, halves, gap, mv)
                dve.tensor_scalar(rstd[:], mv[:, :, 1], EPS, None, ALU.add).then_inc(S["var"], 1)
                dve.wait_ge(S["std"], 1)
                link(dve.reciprocal(rstd[:], std[:]))

                def normed(t):
                    dve.wait_ge(S["turned"], t + 1)
                    dve.tensor_scalar(hn[:], tile_of(r, t), mv[:, bass.ds(t, 1), 0:1].rearrange("p o c -> p (o c)"),
                                      rstd[:, bass.ds(t, 1)], ALU.subtract, ALU.mult).then_inc(S["rn_set"], 1)

                def logits(t):
                    dve.wait_ge(S["lg_done"], t + 1)
                    dve.tensor_scalar(tile_of(lg, t), ps_c[:, 0:EX], 1.0, None, ALU.mult).then_inc(S["lg_set"], 1)
                normed(0)
                with dve.Fori(0, NT - 1) as t:
                    normed(t + 1)
                    logits(t)
                logits(NT - 1)
                dve.wait_ge(S["lg_set"], NT + 1)

                def wide(v):
                    return v[:].unsqueeze(2).to_broadcast([P, NT, EX])
                number = k["iota_row"][:, 0:EX].unsqueeze(1).to_broadcast([P, NT, EX])

                def largest(src, value, onehot):
                    link(dve.tensor_reduce(value[:], src[:], AX.X, ALU.max))
                    link(dve.tensor_tensor(eq[:], src[:], wide(value), ALU.is_equal))
                    link(dve.tensor_scalar(eq[:], eq[:], -float(EX), float(EX), ALU.mult, ALU.add))
                    link(dve.tensor_tensor(eq[:], eq[:], number, ALU.add))
                    link(dve.tensor_reduce(w0[:], eq[:], AX.X, ALU.min))
                    link(dve.tensor_tensor(onehot[:], number, wide(w0), ALU.is_equal))
                largest(lg, v0, first)
                link(dve.scalar_tensor_tensor(lg2[:], first[:], -3e38, lg[:], ALU.mult, ALU.add))
                largest(lg2, v1, second)
                dve.tensor_tensor(v1[:], v1[:], v0[:], ALU.subtract).then_inc(S["gap_set"], 1)
                dve.wait_ge(S["gap_exp"], 1)
                link(dve.tensor_scalar(w0[:], w1_[:], 1.0, None, ALU.add))
                link(dve.reciprocal(w0[:], w0[:]))
                link(dve.tensor_tensor(w1_[:], w1_[:], w0[:], ALU.mult))
                link(dve.tensor_tensor(first[:], first[:], wide(w0), ALU.mult))
                link(dve.tensor_tensor(second[:], second[:], wide(w1_), ALU.mult))
                link(dve.tensor_tensor(comb[:], first[:], second[:], ALU.add))
                dve.sem_inc(S["comb_set"], 1)
                dve.sem_inc(S["added"], 2)
                with own.loop(NT, 0) as t:
                    def add_to(pos):
                        dve.wait_ge(S["added"], (EX + 1) * t + pos + 2)
                    at = tile_of(r, t)
                    dve.wait_ge(S["c_turned"], t + 1)
                    dve.tensor_scalar(c_cur[:], tile_of(comb, t), 1.0, None, ALU.mult).then_inc(S["c_set"], 1)
                    for e in range(EX):
                        if e == 3:
                            dve.wait_ge(S["c_turned"], t + 2)
                            dve.tensor_copy(cT[:], ps_c[0:EX, 0:P]).then_inc(S["cT_set"], 1)
                        if e == 5:
                            dve.wait_ge(S["bias_done"], t + 1)
                            add_to(e)
                            dve.tensor_tensor(at, at, ps_t[:, 0:C], ALU.add).then_inc(S["added"], 1)
                        dve.wait_ge(S["w2_done"], EX * t + e + 3)
                        add_to(e + (e >= 5))
                        dve.scalar_tensor_tensor(at, ps_y[e % 2][:, 0:C], comb[:, bass.ds(t, 1), e:e + 1].rearrange("p o c -> p (o c)"),
                                                 at, ALU.mult, ALU.add).then_inc(S["added"], 1)

            @block.scalar
            def _(act):
                act.dma_start(w1[:], a["L0_ffn_W1"].rearrange("e (c p) n -> p (e c) n", p=P)).then_inc(S["w_in"], 16)
                act.dma_start(w2[:], a["L0_ffn_W2"].rearrange("e (f p) n -> p (e f) n", p=P)).then_inc(S["w_in"], 16)
                act.wait_ge(S["var"], 1)
                act.activation(std[:], rstd[:], ACT.Sqrt).then_inc(S["std"], 1)
                act.sem_inc(S["xT_all"], 1)
                with act.Fori(0, NT) as t:
                    act.wait_ge(S["turned"], t + 2)
                    act.activation(xT_cur[:].rearrange("p c n -> p (c n)"), ps_t[:, 0:C], ACT.Copy).then_inc(S["xT_set"], 1)
                    act.activation(xT[:, :, bass.ds(t * P, P)], ps_t[:, 0:C].rearrange("p (c n) -> p c n", c=CC),
                                   ACT.Copy).then_inc(S["xT_all"], 1)
                act.wait_ge(S["gap_set"], 1)
                act.activation(w1_[:], v1[:], ACT.Exp).then_inc(S["gap_exp"], 1)
                act.sem_inc(S["h_set"], 2 * FE)
                act.wait_ge(S["small_in"], 16 * (5 + EX))
                with act.Fori(0, NT) as t:
                    for e in range(EX):
                        act.wait_ge(S["w1_done"], EX * t + e + 1)
                        act.wait_ge(S["w2_done"], EX * t + e + 1)
                        for f in range(FE):
                            act.activation(hT[:, e % 2, f, :], ps_h[e % 2][:, f * P:(f + 1) * P], ACT.Relu,
                                           bias=b1_col[:, e * FE + f:e * FE + f + 1]).then_inc(S["h_set"], 1)

            @block.tensor
            def _(pe):
                pe.wait_ge(S["small_in"], 16 * (5 + EX))
                pe.sem_inc(S["turned"], 1)
                pe.sem_inc(S["lg_set"], 1)
                with pe.Fori(0, NT) as t:
                    pe.wait_ge(S["rn_set"], t + 1)
                    pe.wait_ge(S["xT_all"], t + 1)
                    for c in range(CC):
                        last = pe.transpose(ps_t[:, c * P:(c + 1) * P], hn[:, c * P:(c + 1) * P], k["ident"][:])
                    last.then_inc(S["turned"], 1)
                    pe.wait_ge(S["xT_set"], t + 1)
                    pe.wait_ge(S["lg_set"], t + 1)
                    for c in range(CC):
                        pe.matmul(ps_c[:, 0:EX], xT_cur[:, c, :], wg[:, c, :], start=c == 0, stop=False)
                    for j in range(2):
                        last = pe.matmul(ps_c[:, 0:EX], k["ones"][0:1, :], gate_rows[:, j, :], start=False, stop=j == 1)
                    last.then_inc(S["lg_done"], 1)
                pe.wait_ge(S["comb_set"], 1)
                pe.wait_ge(S["xT_all"], NT + 1)
                pe.wait_ge(S["w_in"], 32)
                pe.sem_inc(S["c_turned"], 1)
                pe.sem_inc(S["w2_done"], 2)

                def up(t, e):
                    pe.wait_ge(S["h_set"], FE * (EX * t + e) + FE)
                    for f in range(FE):
                        for c in range(CC):
                            last = pe.matmul(ps_h[e % 2][:, f * P:(f + 1) * P], w1[:, e * CC + c, f * P:(f + 1) * P],
                                             xT[:, c, bass.ds(t * P, P)], start=c == 0, stop=c == CC - 1)
                    last.then_inc(S["w1_done"], 1)

                def tile(t, ends):
                    for e in range(EX):
                        if e + 1 < EX:
                            up(t, e + 1)
                        elif not ends:
                            up(t + 1, 0)
                        if e == 1:
                            pe.wait_ge(S["c_set"], t + 1)
                            pe.transpose(ps_c[0:EX, 0:P], c_cur[:], k["ident"][:]).then_inc(S["c_turned"], 1)
                        if e == 3:
                            pe.wait_ge(S["cT_set"], t + 1)
                            pe.matmul(ps_t[:, 0:C], cT[:], b2[:], start=True, stop=True).then_inc(S["bias_done"], 1)
                        pe.wait_ge(S["h_set"], FE * (EX * t + e) + 3 * FE)
                        before = e - 2
                        pe.wait_ge(S["added"], (EX + 1) * t + before + (before >= 5) + 3)
                        for f in range(FE):
                            last = pe.matmul(ps_y[e % 2][:, 0:C], hT[:, e % 2, f, :], w2[:, e * FE + f, :], start=f == 0, stop=f == FE - 1)
                        last.then_inc(S["w2_done"], 1)
                up(0, 0)
                with pe.Fori(0, NT - 1) as t:
                    tile(t, False)
                tile(NT - 1, True)


_INS = ["x", "src", "dst"] + ["L0_gnn_" + n for n in ("W1", "a1_src", "a1_dst", "b1", "ln_g", "ln_b", "W2", "a2_src", "a2_dst", "b2")] \
    + ["L0_mix_" + n for n in ("ln1_g", "ln1_b", "Wx", "bx", "Wq", "Wk", "Wv", "Wo", "bo", "ln2_g", "ln2_b", "W1", "b1", "W2", "b2")] \
    + ["L0_ffn_" + n for n in ("Wg", "bg", "bias", "W1", "b1", "W2", "b2")]


def kernel(**inputs):
    import numpy as _np
    import concourse.bacc as _bacc
    from concourse import mybir as _mybir
    from concourse.bass_utils import run_bass_kernel_spmd as _run

    nc = _bacc.Bacc("TRN2", target_bir_lowering=False, num_devices=1)
    arrays, args = {}, {}
    for name in _INS:
        array = _np.ascontiguousarray(inputs[name])
        arrays[f"in_{name}"] = array
        args[name] = nc.dram_tensor(f"in_{name}", array.shape, _mybir.dt.from_np(array.dtype), kind="ExternalInput").ap()
    out = nc.dram_tensor("out", [N, C], F32, kind="ExternalOutput").ap()
    build(nc, args, out)
    r = _run(nc, [arrays], core_ids=[0])
    return r.results[0]["out"]
```

```python
from contextlib import ExitStack, contextmanager

import concourse.bass as bass
from concourse import mybir

F32 = mybir.dt.float32
I32 = mybir.dt.int32
U32 = mybir.dt.uint32
ALU = mybir.AluOpType
ACT = mybir.ActivationFunctionType
AX = mybir.AxisListType

P = 128
N, C, E = 3125, 256, 50000
NT = -(-N // P)
NP = NT * P
LAST = N - (NT - 1) * P
LOOPS = 625
CC = C // P
HEADS1, HID = 4, C // 4
MH, DH, KR = 8, 32, 4
FF = 4 * C
FM = FF // P
EX, ED = 8, 512
FE = ED // P
EPS = 1e-5
SLOPE = 0.2

HALF = 4
GROUP = 5
assert NT % GROUP == 0
EC = -(-E // (P * 2 * HALF)) * 2 * HALF
BATCH = 4
TILES = -(-(E // P + NT) // (2 * BATCH)) * 2 * BATCH
NB = TILES // BATCH
DEPTH = 8
assert NB % DEPTH == 0
TT = TILES + 2 * BATCH
TR = TT // 4
SLOTS = TT * P
PAD_DST = NP + P - 1
FAR = float(1 << 22)


def blocks_of(nc, engine, k, b):
    _, found = nc.values_load_multi_w_load_instructions(
        k["block_row"][0:1, bass.ds((b + 1) * BATCH, BATCH)], engines=(engine,), min_val=0, max_val=NT - 1,
        skip_runtime_bounds_check_because="edge_tables bounds them")
    return found


class Steps:

    def __init__(self, eng, sem):
        self.eng, self.sem, self.n, self.turn = eng, sem, 0, None

    def did(self, ins):
        ins.then_inc(self.sem, 1)
        self.n += 1

    def settle(self):
        self.eng.wait_ge(self.sem, self.n if self.turn is None else self.turn * self.per + self.n)

    def settle_but(self, last):
        n = self.n - last
        self.eng.wait_ge(self.sem, n if self.turn is None else self.turn * self.per + n)

    def link(self, ins):
        self.did(ins)
        self.settle()

    @contextmanager
    def loop(self, count, per):
        n0 = self.n
        with self.eng.Fori(0, count) as i:
            self.turn, self.per = i, per
            yield i
            assert self.n - n0 == per, (self.n - n0, per)
        self.n, self.turn = n0 + per * count, None


def build(nc, a, out):
    with ExitStack() as top:
        phases = iter(range(99))

        def alloc(stack):
            n = next(phases)
            return lambda name, shape, dt=F32: stack.enter_context(nc.sbuf_tensor(f"{name}_{n}", shape, dt))

        def sems(stack):
            taken = []

            def sem(name):
                taken.append(nc.alloc_semaphore(name=name))
                return taken[-1]

            def clear():
                nc.clear_and_free_semaphores(taken)
                nc.all_engine_barrier()
            stack.callback(clear)
            return sem

        sorted_edges = nc.dram_tensor("sorted_edges", [SLOTS, 2], I32).ap()
        dst_row = nc.dram_tensor("dst_row", [SLOTS], F32).ap()
        src_row = nc.dram_tensor("src_row", [SLOTS], F32).ap()
        table1 = nc.dram_tensor("table1", [NP, C + HEADS1], F32).ap()
        table2 = nc.dram_tensor("table2", [NP, C + 1], F32).ap()
        mixed = nc.dram_tensor("mixed", [NP, C], F32).ap()

        g = alloc(top)
        k = {
            "ident": g("ident", [P, P]), "ones": g("ones", [P, P]), "below": g("below", [P, P]),
            "iota_row": g("iota_row", [P, P]), "iota_col": g("iota_col", [P, 1]),
            "h1": g("h1", [P, NT, C]),
            "es1": g("es1", [P, NT, HEADS1]), "ed1": g("ed1", [P, NT, HEADS1]),
            "loops": g("loops", [P, NT]),
            "es2": g("es2", [P, NT, 1]), "ed2": g("ed2", [P, NT, 1]),
            "gat2_w": g("gat2_w", [P, CC, C + 2]),
            "src_col": g("src_col", [P, TT], I32), "dst_col": g("dst_col", [P, TT]),
            "hi_col": g("hi_col", [P, TT]), "block_row": g("block_row", [1, BATCH + TT], I32),
        }
        node_phase(nc, a, k, alloc, sems, sorted_edges, table1, mixed)
        edge_tables(nc, k, alloc, sems, sorted_edges, dst_row, src_row)
        with ExitStack() as layer:
            acc = alloc(layer)("acc1", [P, NT, C + HEADS1])
            wself = alloc(layer)("wself1", [P, NT, HEADS1])
            with ExitStack() as st:
                top_e = alloc(st)("top1", [P, NT, HEADS1])
                em = alloc(st)("em1", [P, NT, 2 * HEADS1])
                segment_max(nc, 1, HEADS1, k, k["es1"], k["ed1"], top_e, em, alloc, sems, src_row)
                weighted_sum(nc, 1, HEADS1, k, em, k["es1"], acc, wself, table1, alloc, sems, dst_row)
            between_layers(nc, a, k, acc, wself, alloc, sems, table2)
        with ExitStack() as layer:
            acc = alloc(layer)("acc2", [P, NT, C + 1])
            wself = alloc(layer)("wself2", [P, NT, 1])
            with ExitStack() as st:
                top_e = alloc(st)("top2", [P, NT, 1])
                em = alloc(st)("em2", [P, NT, 2])
                segment_max(nc, 2, 1, k, k["es2"], k["ed2"], top_e, em, alloc, sems, src_row)
                weighted_sum(nc, 2, 1, k, em, k["es2"], acc, wself, table2, alloc, sems, dst_row)
            experts(nc, a, k, acc, wself, alloc, sems, mixed, out)


def node_phase(nc, a, k, alloc, sems, sorted_edges, table1, mixed):
    with ExitStack() as st:
        sb, sem = alloc(st), sems(st)
        ident, ones, below = k["ident"], k["ones"], k["below"]
        dst_raw, src_raw = sb("dst_raw", [P, EC], I32), sb("src_raw", [P, EC], I32)
        fill = sb("fill", [P, TT, 2], I32)
        pair = sb("pair", [P, EC, 2], I32)
        blk_i = sb("blk_i", [P, EC], I32)
        SORTED = 5
        assert NT % SORTED == 0
        blk, slot = sb("blk", [P, EC]), sb("slot", [P, EC])
        mask, rank = sb("mask", [P, SORTED, EC]), sb("rank", [P, SORTED, EC])
        slot_i = sb("slot_i", [P, EC], I32)
        ones_e = sb("ones_e", [P, EC])
        bnum = sb("bnum", [P, NT + 3])
        cnt, off, tl = sb("cnt", [P, NT]), sb("off", [P, NT + 3]), sb("tl", [P, NT])
        tl_i = sb("tl_i", [P, NT], I32)
        cur_slot = sb("cur_slot", [P, 2, HALF], I32)
        cur_pair = sb("cur_pair", [P, 2, HALF, 2], I32)
        scratch = sb("pool_scratch", [1, 1])

        xn = sb("xn", [P, NT, C])
        halves, gap, mv = sb("halves", [P, NT, 6]), sb("gap", [P, NT]), sb("mv", [P, NT, 2])
        std, rstd = sb("std", [P, NT]), sb("rstd", [P, NT])
        hn, xcur = sb("hn", [P, C]), sb("xcur", [P, C])
        gat_w = sb("gat1_w", [P, CC, C + 2 * HEADS1])
        a_row = sb("a_row", [P, 4, C])
        xnT, hnT, xmT = (sb(n, [P, CC, P]) for n in ("xnT", "hnT", "xmT"))
        wx, wo = sb("wx", [P, CC, C]), sb("wo", [P, CC, C])
        wq, wk, wv = sb("wq", [P, CC, MH * KR]), sb("wk", [P, CC, MH * KR]), sb("wv", [P, CC, C])
        bias_cols = sb("bias_cols", [P, 5, CC])
        b1_col = sb("mix_b1_col", [P, FM])
        bo_b, b2_row = sb("bo_b", [P, C]), sb("mix_b2_row", [1, C])
        w1, w2 = sb("mix_w1", [P, CC, FF]), sb("mix_w2", [P, FM, C])
        v1 = sb("v1", [P, NT, C + 1])
        q = sb("q", [P, NT, MH, KR])
        qm = sb("qm", [P, NT, MH])
        QK = MH * KR
        kT, qT = sb("kT", [QK, NP]), sb("qT", [QK, NP])
        kmax = sb("kmax", [QK, 1])
        qcur, kcur, qTcur = sb("qcur", [P, QK]), sb("kcur", [QK, P]), sb("qTcur", [QK, 2, P])
        zrow = sb("zrow", [1, C + 1])
        ek = sb("ek", [P, 2, QK])
        kv, kvr = sb("kv", [QK, C]), sb("kvr", [QK, 1])
        headmask = sb("headmask", [QK, C])
        kvT = sb("kvT", [P, CC, QK])
        ko = sb("ko", [QK, C])
        gT = sb("gT", [P, 2, FM, P])
        prod = gT[:].rearrange("p y f n -> p (y f n)")[:, 0:4 * CC * C].rearrange("p (s c n) -> p s c n", s=4, c=CC)
        mixrow, xrow = sb("mixrow", [P, C]), sb("xrow", [P, C])
        es1, ed1, h1 = k["es1"], k["ed1"], k["h1"]
        tabrow = sb("tabrow", [P, C + HEADS1])

        def pt(name, shape):
            return st.enter_context(nc.psum_tensor(name, shape, F32))
        ps_a, ps_b, ps_c, ps_d = (pt(f"ps_{n}", [P, 512]) for n in "abcd")
        ps_e, ps_f = pt("ps_e", [P, 512]), pt("ps_f", [P, 512])
        ps_g, ps_g2 = pt("ps_g", [P, 512]), pt("ps_g2", [P, 512])
        FB = 512 // P
        ps_at = (ps_d, ps_e)
        ps_ff = ((ps_g, ps_g2), (ps_e, ps_f))
        assert FM == 2 * FB and NT % 2 == 1

        edges_pad, consts, fill_set, fill_out = (sem(n) for n in ("edges_pad", "consts", "fill_set", "fill_out"))
        edges_in, x_in, w_in, small_in = (sem(n) for n in ("edges_in", "x_in", "w_in", "small_in"))
        zeroed, v_own = sem("zeroed"), sem("node_dve_own")
        counted, prefixed, slots_set = sem("counted"), sem("prefixed"), sem("slots_set")
        pool_copied, scattered = sem("pool_copied"), [sem(f"scattered{j}") for j in range(2 * HALF)]
        w_set, var_set, std_set = sem("w_set"), sem("var_set"), sem("std_set")
        hn_set, xcur_set, turned = sem("hn_set"), sem("xcur_set"), sem("turned")
        xnT_set, hnT_set, xmT_set = sem("xnT_set"), sem("hnT_set"), sem("xmT_set")
        h_done, xm_done, qkv_done = sem("h_done"), sem("xm_done"), sem("qkv_done")
        row_set, h_out, v_out, qk_out, tab_out = (sem(n) for n in ("row_set", "h_out", "v_out", "qk_out", "tab_out"))
        q_set, qexp_set, qsoft_set, kmax_set, kexp_set = (sem(n) for n in ("q_set", "qexp_set", "qsoft_set", "kmax_set", "kexp_set"))
        cur_set, qk_turned, qT_set, kv_done = (sem(n) for n in ("cur_set", "qk_turned", "qT_set", "kv_done"))
        kv_set, kv_turned, kvT_set, ko_done, ko_set = (sem(n) for n in ("kv_set", "kv_turned", "kvT_set", "ko_done", "ko_set"))
        qTcur_set, attn_done, fx_set = sem("qTcur_set"), sem("attn_done"), sem("fx_set")
        fn_set, fn_turned, fnT_set = sem("fn_set"), sem("fn_turned"), sem("fnT_set")
        xrow_in, sum_set = sem("xrow_in"), sem("sum_set")
        ff_done, g_set, m_done, mix_set, mix_out = (sem(n) for n in ("ff_done", "g_set", "m_done", "mix_set", "mix_out"))
        full = (P - 1) * EC
        loads = 18

        with nc.Block() as block:
            @block.sync
            def _(sp):
                sp.wait_ge(edges_pad, 2)
                for name, dst in (("dst", dst_raw), ("src", src_raw)):
                    sp.dma_start(dst[0:P - 1, :], a[name][0:full].rearrange("(p e) -> p e", e=EC)).then_inc(edges_in, 16)
                    sp.dma_start(dst[P - 1:P, 0:E - full],
                                 a[name][full:E].rearrange("(p e) -> p e", p=1)).then_inc(edges_in, 16)
                sp.wait_ge(zeroed, 1)
                sp.dma_start(xn[:, 0:NT - 1, :],
                             a["x"][0:(NT - 1) * P, :].rearrange("(t p) c -> p t c", p=P)).then_inc(x_in, 16)
                sp.dma_start(xn[0:LAST, NT - 1, :], a["x"][(NT - 1) * P:N, :]).then_inc(x_in, 16)
                sp.wait_ge(fill_set, 1)
                sp.dma_start(sorted_edges.rearrange("(p s) w -> p s w", p=P), fill[:]).then_inc(fill_out, 16)

                def chunks(w):
                    return w.rearrange("(c p) n -> p c n", p=P)
                n = 0
                for dst, src in ((gat_w[:, :, 0:C], chunks(a["L0_gnn_W1"])),
                                 (k["gat2_w"][:, :, 0:C], chunks(a["L0_gnn_W2"])),
                                 (wx[:], chunks(a["L0_mix_Wx"])), (wo[:], chunks(a["L0_mix_Wo"])),
                                 (w1[:], chunks(a["L0_mix_W1"])), (w2[:], chunks(a["L0_mix_W2"])),
                                 (bo_b[:], a["L0_mix_bo"].partition_broadcast(P)),
                                 (b2_row[:], a["L0_mix_b2"].rearrange("(o n) -> o n", o=1))):
                    sp.dma_start(dst, src).then_inc(w_in, 16)
                    n += 1
                for j, name in enumerate(("a1_src", "a1_dst", "a2_src", "a2_dst")):
                    sp.dma_start(a_row[:, j, :],
                                 a["L0_gnn_" + name].rearrange("h c -> (h c)").partition_broadcast(P)).then_inc(w_in, 16)
                    n += 1
                with nc.allow_non_contiguous_dma(reason="a bias of a few hundred values, one a partition"):
                    for j, name in enumerate(("ln1_g", "ln1_b", "bx", "ln2_g", "ln2_b")):
                        sp.dma_start(bias_cols[:, j, :], a["L0_mix_" + name].rearrange("(c p) -> p c", p=P)).then_inc(w_in, 16)
                        n += 1
                    sp.dma_start(b1_col[:], a["L0_mix_b1"].rearrange("(c p) -> p c", p=P)).then_inc(w_in, 16)
                assert n + 1 == loads
                sp.wait_ge(zeroed, 4)
                for h in range(MH):
                    c, r = h * DH // P, h * DH % P
                    for w, name, wide in ((wq, "Wq", KR), (wk, "Wk", KR), (wv, "Wv", DH)):
                        sp.dma_start(w[r:r + DH, c, h * wide:(h + 1) * wide], a["L0_mix_" + name]).then_inc(small_in, 16)
                sp.sem_inc(tab_out, 16)
                with sp.Fori(0, NT) as t:
                    sp.wait_ge(row_set, t + 1)
                    sp.dma_start(table1[bass.ds(t * P, P), :], tabrow[:]).then_inc(tab_out, 16)
                sp.sem_inc(mix_out, 16)

                def load_x(t, rows=P):
                    sp.dma_start(xrow[0:rows, :], a["x"][bass.ds(t * P, rows), :]).then_inc(xrow_in, 16)
                with sp.Fori(0, NT - 1) as t:
                    load_x(t)
                    sp.wait_ge(mix_set, t + 2)
                    sp.dma_start(mixed[bass.ds(t * P, P), :], mixrow[:]).then_inc(mix_out, 16)
                load_x(NT - 1, LAST)
                sp.wait_ge(mix_set, NT + 1)
                sp.dma_start(mixed[(NT - 1) * P:, :], mixrow[:]).then_inc(mix_out, 16)
                sp.wait_ge(tab_out, 16 * (NT + 1))
                sp.wait_ge(mix_out, 16 * (NT + 1))

            @block.gpsimd
            def _(pool):
                own = Steps(pool, consts)
                pool.memset(dst_raw[:], PAD_DST).then_inc(edges_pad, 1)
                pool.memset(src_raw[:], 0).then_inc(edges_pad, 1)
                own.link(pool.memset(ones[:], 1.0))
                own.did(pool.affine_select(out=ident[:], in_=ones[:], compare_op=ALU.is_equal, fill=0.0, base=0,
                                           pattern=[[-1, P]], channel_multiplier=1))
                own.did(pool.affine_select(out=below[:], in_=ones[:], compare_op=ALU.is_gt, fill=0.0, base=0,
                                           pattern=[[1, P]], channel_multiplier=-1))
                for out_, pattern, step in ((k["iota_row"], [[1, P]], 0), (k["iota_col"], [[1, 1]], 1), (bnum, [[1, NT + 3]], 0)):
                    own.did(pool.iota(out_[:], pattern, base=0, channel_multiplier=step,
                                      allow_small_or_imprecise_dtypes=True))
                own.did(pool.memset(scratch[:], 0.0))
                own.did(pool.affine_select(out=k["loops"][:], in_=ones[:, 0:NT], compare_op=ALU.is_ge, fill=0.0,
                                           base=LOOPS - 1, pattern=[[-P, NT]], channel_multiplier=-1))
                own.link(pool.memset(headmask[:], 1.0))
                hm = headmask[:].rearrange("q (h d) -> q h d", d=DH)
                own.link(pool.affine_select(out=hm, in_=hm, compare_op=ALU.is_ge, fill=0.0, base=0,
                                            pattern=[[-KR, MH], [0, DH]], channel_multiplier=1))
                own.link(pool.affine_select(out=hm, in_=hm, compare_op=ALU.is_ge, fill=0.0, base=KR - 1,
                                            pattern=[[KR, MH], [0, DH]], channel_multiplier=-1))
                bound = pool.to_reg(SLOTS - 1)
                pool.wait_ge(slots_set, 1)
                pool.wait_ge(fill_out, 16)

                def half(i, y, again):
                    if again:
                        for j in range(HALF):
                            pool.wait_ge(scattered[y * HALF + j], 16 * i)
                    at = i * 2 * HALF + y * HALF
                    pool.tensor_copy(cur_slot[:, y, :], slot_i[:, bass.ds(at, HALF)]).then_inc(pool_copied, 1)
                    pool.tensor_copy(cur_pair[:, y], pair[:, bass.ds(at, HALF), :]).then_inc(pool_copied, 1)
                    pool.wait_ge(pool_copied, (i * 2 + y + 1) * 2)
                    pool.tensor_tensor(scratch[:], ones[0:1, 0:1], ones[0:1, 0:1], ALU.add).then_inc(consts, 1)
                    for j in range(HALF):
                        pool.indirect_dma_start(sorted_edges, bass.IndirectOffsetOnAxis(cur_slot[:, y, j:j + 1], 0),
                                                cur_pair[:, y, j, :], None, bounds_check=bound,
                                                oob_is_err=False).then_inc(scattered[y * HALF + j], 16)
                half(0, 0, False)
                half(0, 1, False)
                with pool.Fori(1, EC // (2 * HALF)) as i:
                    half(i, 0, True)
                    half(i, 1, True)
                for s in scattered:
                    pool.wait_ge(s, 16 * (EC // (2 * HALF)))

            @block.vector
            def _(dve):
                own = Steps(dve, v_own)
                link = own.link

                def copy(dst, src):
                    return dve.tensor_scalar(dst, src, 1.0, None, ALU.mult)
                dve.memset(xn[:, NT - 1, :], 0.0).then_inc(zeroed, 1)
                for w in (wq, wk, wv):
                    dve.memset(w[:], 0.0).then_inc(zeroed, 1)
                own.did(dve.memset(ones_e[:], 1.0))
                own.did(dve.memset(zrow[:], 0.0))
                own.did(dve.memset(v1[:, :, C:C + 1], 1.0))
                link(dve.memset(fill[:, :, 0], 0))
                dve.memset(fill[:, :, 1], PAD_DST).then_inc(fill_set, 1)
                dve.wait_ge(edges_in, 64)
                dve.wait_ge(consts, 11)
                own.did(dve.tensor_copy(pair[:, :, 0], src_raw[:]))
                own.did(dve.tensor_copy(pair[:, :, 1], dst_raw[:]))
                link(dve.tensor_scalar(blk_i[:], dst_raw[:], 7, None, ALU.arith_shift_right))
                link(dve.tensor_copy(blk[:], blk_i[:]))
                for y in range(SORTED):
                    own.did(dve.memset(mask[:, y, :], 0.0))
                with own.loop(NT // SORTED, SORTED) as i:
                    for y in range(SORTED):
                        b = i * SORTED + y
                        own.settle_but(SORTED - 1)
                        own.did(dve.tensor_scalar(mask[:, y, :], blk[:], bnum[:, bass.ds(b, 1)], None, ALU.is_equal, ALU.add,
                                                  accum_out=cnt[:, bass.ds(b, 1)]))
                own.settle()
                link(dve.memset(off[:], 0.0))
                dve.sem_inc(counted, 1)
                dve.wait_ge(prefixed, 2)
                link(dve.tensor_copy(tl_i[:], ps_a[:, 0:NT]))
                link(dve.tensor_scalar(tl[:], tl_i[:], float(P - 1), None, ALU.add))
                link(dve.tensor_copy(tl_i[:], tl[:]))
                link(dve.tensor_scalar(tl_i[:], tl_i[:], 7, None, ALU.arith_shift_right))
                link(dve.tensor_copy(tl[:], tl_i[:]))
                link(dve.tensor_tensor_scan(cnt[:], ones_e[:, 0:NT], tl[:], 0.0, ALU.mult, ALU.add))
                link(dve.tensor_tensor(cnt[:], cnt[:], tl[:], ALU.subtract))
                link(dve.scalar_tensor_tensor(off[:, 0:NT], cnt[:], float(P), ps_b[:, 0:NT], ALU.mult, ALU.add))
                link(dve.tensor_scalar(slot[:], blk[:], float(NT), FAR, ALU.is_equal, ALU.mult))

                def mark(b, y):
                    own.did(dve.tensor_scalar(mask[:, y, :], blk[:], bnum[:, bass.ds(b, 1)], None, ALU.is_equal))

                def count(b, y):
                    own.did(dve.tensor_tensor_scan(rank[:, y, :], ones_e[:], mask[:, y, :], off[:, bass.ds(b, 1)], ALU.mult, ALU.add))

                def keep(y):
                    own.did(dve.tensor_tensor(rank[:, y, :], rank[:, y, :], mask[:, y, :], ALU.mult))
                for b in range(3):
                    mark(b, b)
                own.settle()
                for b in range(2):
                    count(b, b)
                own.settle()
                keep(0)
                own.settle()
                with own.loop(NT // SORTED, 4 * SORTED) as i:
                    for y in range(SORTED):
                        b = i * SORTED + y
                        own.settle_but(2)
                        own.did(dve.tensor_tensor(slot[:], slot[:], rank[:, y, :], ALU.add))
                        own.settle_but(2)
                        keep((y + 1) % SORTED)
                        own.settle_but(2)
                        count(b + 2, (y + 2) % SORTED)
                        own.settle_but(2)
                        mark(b + 3, (y + 3) % SORTED)
                own.settle()
                link(dve.tensor_scalar(slot[:], slot[:], -1.0, None, ALU.add))
                dve.tensor_copy(slot_i[:], slot[:]).then_inc(slots_set, 1)

                dve.wait_ge(w_in, 16 * loads)
                sides = [(layer, side, w, heads) for layer, (w, heads) in enumerate(((gat_w, HEADS1), (k["gat2_w"], 1)))
                         for side in range(2)]
                for n, (layer, side, w, heads) in enumerate(sides):
                    own.did(dve.tensor_tensor(prod[:, n], w[:, :, 0:C],
                                              a_row[:, n:n + 1, :].to_broadcast([P, CC, C]), ALU.mult))
                own.settle()
                for n, (layer, side, w, heads) in enumerate(sides):
                    own.did(dve.tensor_reduce(w[:, :, C + side * heads:C + (side + 1) * heads],
                                              prod[:, n].rearrange("p c (h d) -> p c h d", h=heads), AX.X, ALU.add))
                own.settle()
                dve.sem_inc(w_set, 1)

                def root(n):
                    dve.tensor_scalar(rstd[:], mv[:, :, 1], EPS, None, ALU.add).then_inc(var_set, 1)
                    dve.wait_ge(std_set, n)
                    link(dve.reciprocal(rstd[:], std[:]))

                def normed(dst, t):
                    return dve.tensor_scalar(dst, tile_of(xn, t), mv[:, bass.ds(t, 1), 0:1].rearrange("p o c -> p (o c)"),
                                             rstd[:, bass.ds(t, 1)], ALU.subtract, ALU.mult)

                dve.wait_ge(x_in, 32)
                dve.wait_ge(zeroed, 1)
                moments(dve, own, xn, halves, gap, mv)
                root(1)
                with own.loop(NT // GROUP, GROUP) as i:
                    for y in range(GROUP):
                        own.did(normed(tile_of(xn, i * GROUP + y), i * GROUP + y))
                own.settle()
                moments(dve, own, xn, halves, gap, mv)
                root(2)
                dve.sem_inc(qk_out, 2)

                def hn_of(t):
                    dve.wait_ge(turned, t + 1)
                    normed(hn[:], t).then_inc(hn_set, 1)

                def hnT_of(t):
                    dve.wait_ge(turned, t + 2)
                    for c in range(CC):
                        dve.tensor_scalar(hnT[:, c, :], ps_b[:, c * P:(c + 1) * P], bias_cols[:, 0, c:c + 1],
                                          bias_cols[:, 1, c:c + 1], ALU.mult, ALU.add).then_inc(hnT_set, 1)

                def xmT_of(t):
                    dve.wait_ge(xm_done, t + 1)
                    for c in range(CC):
                        dve.tensor_scalar(xmT[:, c, :], ps_d[:, c * P:(c + 1) * P], bias_cols[:, 2, c:c + 1],
                                          None, ALU.add).then_inc(xmT_set, 1)

                def qk_of(t):
                    dve.wait_ge(qkv_done, t + 1)
                    copy(q[:, bass.ds(t, 1)].rearrange("p o h r -> p (o h r)"), ps_f[:, P:P + QK]).then_inc(qk_out, 1)
                    copy(kT[:, bass.ds(t * P, P)], ps_f[0:QK, 0:P]).then_inc(qk_out, 1)
                hn_of(0)
                hnT_of(0)
                hn_of(1)
                with dve.Fori(0, NT - 2) as t:
                    xmT_of(t)
                    hnT_of(t + 1)
                    hn_of(t + 2)
                    qk_of(t)
                xmT_of(NT - 2)
                hnT_of(NT - 1)
                qk_of(NT - 2)
                xmT_of(NT - 1)
                qk_of(NT - 1)
                dve.wait_ge(qk_out, 2 * NT + 2)
                link(dve.tensor_reduce(qm[:], q[:], AX.X, ALU.max))
                dve.tensor_tensor(q[:], q[:], qm[:].unsqueeze(3).to_broadcast([P, NT, MH, KR]), ALU.subtract).then_inc(q_set, 1)
                link(dve.tensor_reduce(kmax[:], kT[:, 0:N], AX.X, ALU.max))
                dve.tensor_scalar(kmax[:], kmax[:], -1.0, None, ALU.mult).then_inc(kmax_set, 1)
                dve.wait_ge(qexp_set, 1)
                link(dve.tensor_reduce(qm[:], q[:], AX.X, ALU.add))
                link(dve.reciprocal(qm[:], qm[:]))
                link(dve.tensor_tensor(q[:], q[:], qm[:].unsqueeze(3).to_broadcast([P, NT, MH, KR]), ALU.mult))
                own.did(dve.tensor_tensor(xn[:], xn[:], bo_b[:].unsqueeze(1).to_broadcast([P, NT, C]), ALU.add))
                dve.wait_ge(kexp_set, 1)
                dve.memset(kT[:, N:NP], 0.0).then_inc(qsoft_set, 1)

                def qT_ek(t, y):
                    dve.wait_ge(qk_turned, t + 2)
                    dve.wait_ge(kv_done, t + 1)
                    copy(qT[:, bass.ds(t * P, P)], ps_a[0:QK, 0:P]).then_inc(qT_set, 1)
                    dve.tensor_copy(ek[:, y, :], ps_b[:, 0:QK]).then_inc(qT_set, 1)
                with dve.Fori(0, NT // 2) as i:
                    qT_ek(i * 2, 0)
                    qT_ek(i * 2 + 1, 1)
                qT_ek(NT - 1, 0)
                dve.wait_ge(kv_done, NT + 3)
                link(dve.reciprocal(kvr[:], ps_c[0:QK, C:C + 1]))
                dve.scalar_tensor_tensor(kv[:], ps_c[0:QK, 0:C], kvr[:, 0:1], headmask[:], ALU.mult, ALU.mult).then_inc(kv_set, 1)
                dve.wait_ge(kv_turned, 1)
                dve.tensor_copy(kvT[:].rearrange("p c q -> p (c q)"), ps_a[:, 0:CC * QK]).then_inc(kvT_set, 1)
                dve.wait_ge(ko_done, 1)
                dve.tensor_copy(ko[:], ps_b[0:QK, 0:C]).then_inc(ko_set, 1)
                own.settle()

                def fx_of(t, y):
                    dve.wait_ge(attn_done, t + 3)
                    dve.tensor_tensor(tile_of(xn, t), ps_at[y][:, 0:C], tile_of(xn, t), ALU.add).then_inc(fx_set, 1)
                with dve.Fori(0, NT // 2) as i:
                    fx_of(i * 2, 0)
                    fx_of(i * 2 + 1, 1)
                fx_of(NT - 1, 0)
                dve.wait_ge(fx_set, NT + 2)
                moments(dve, own, xn, halves, gap, mv)
                root(3)

                def fn_of(t):
                    dve.wait_ge(fn_turned, t + 1)
                    normed(hn[:], t).then_inc(fn_set, 1)

                def fnT_of(t):
                    dve.wait_ge(fn_turned, t + 2)
                    for c in range(CC):
                        dve.tensor_scalar(hnT[:, c, :], ps_a[:, c * P:(c + 1) * P], bias_cols[:, 3, c:c + 1],
                                          bias_cols[:, 4, c:c + 1], ALU.mult, ALU.add).then_inc(fnT_set, 1)

                def mix_of(t):
                    dve.wait_ge(m_done, t + 3)
                    dve.wait_ge(mix_out, 16 * (t + 1))
                    dve.tensor_tensor(mixrow[:], ps_d[:, 0:C], tile_of(xn, t), ALU.add).then_inc(sum_set, 1)
                    dve.wait_ge(sum_set, t + 2)
                    dve.wait_ge(xrow_in, 16 * (t + 1))
                    dve.tensor_tensor(mixrow[:], mixrow[:], xrow[:], ALU.add).then_inc(mix_set, 1)
                fn_of(0)
                for t in range(2):
                    fnT_of(t)
                    fn_of(t + 1)
                with dve.Fori(0, NT - 3) as t:
                    fnT_of(t + 2)
                    fn_of(t + 3)
                    mix_of(t)
                fnT_of(NT - 1)
                for t in range(NT - 3, NT):
                    mix_of(t)

            @block.scalar
            def _(act):
                for n in range(2):
                    act.wait_ge(var_set, n + 1)
                    act.activation(std[:], rstd[:], ACT.Sqrt).then_inc(std_set, 1)
                act.sem_inc(h_out, 3)
                act.sem_inc(v_out, 1)

                def xcur_of(t):
                    act.wait_ge(hn_set, t + 1)
                    act.wait_ge(turned, t + 1)
                    act.activation(xcur[:], tile_of(xn, t), ACT.Copy).then_inc(xcur_set, 1)

                def xnT_of():
                    act.activation(xnT[:].rearrange("p c n -> p (c n)"), ps_a[:, 0:C], ACT.Copy).then_inc(xnT_set, 1)

                def outputs(t):
                    act.wait_ge(h_done, t + 1)
                    act.wait_ge(tab_out, 16 * (t + 1))
                    act.activation(tabrow[:], ps_c[:, 0:C + HEADS1], ACT.Copy).then_inc(row_set, 1)
                    act.activation(tile_of(h1, t), ps_c[:, 0:C], ACT.Copy).then_inc(h_out, 1)
                    act.activation(tile_of(es1, t), ps_c[:, C:C + HEADS1], ACT.Copy).then_inc(h_out, 1)
                    act.activation(tile_of(ed1, t), ps_c[:, C + HEADS1:C + 2 * HEADS1], ACT.Copy).then_inc(h_out, 1)
                    act.wait_ge(qkv_done, t + 1)
                    act.activation(v1[:, bass.ds(t, 1), 0:C].rearrange("p o c -> p (o c)"), ps_e[:, 0:C],
                                   ACT.Copy).then_inc(v_out, 1)
                xcur_of(0)
                act.wait_ge(turned, 2)
                xnT_of()
                xcur_of(1)
                with act.Fori(0, NT - 2) as t:
                    act.wait_ge(turned, t + 3)
                    xnT_of()
                    xcur_of(t + 2)
                    outputs(t)
                act.wait_ge(turned, NT + 1)
                xnT_of()
                outputs(NT - 2)
                outputs(NT - 1)
                act.wait_ge(q_set, 1)
                act.activation(q[:], q[:], ACT.Exp).then_inc(qexp_set, 1)
                act.wait_ge(kmax_set, 1)
                act.activation(kT[:, 0:N], kT[:, 0:N], ACT.Exp, bias=kmax[:, 0:1]).then_inc(kexp_set, 1)
                act.wait_ge(qsoft_set, 1)
                with act.Fori(0, NT) as t:
                    act.wait_ge(qk_turned, t + 1)
                    act.activation(qcur[:], q[:, bass.ds(t, 1)].rearrange("p o h r -> p (o h r)"), ACT.Copy).then_inc(cur_set, 1)
                    act.activation(kcur[:], kT[:, bass.ds(t * P, P)], ACT.Copy).then_inc(cur_set, 1)
                act.wait_ge(qT_set, 2 * NT + 2)

                def qTcur_of(t, y):
                    act.wait_ge(attn_done, t + 1)
                    act.activation(qTcur[:, y, :], qT[:, bass.ds(t * P, P)], ACT.Copy).then_inc(qTcur_set, 1)
                with act.Fori(0, NT // 2) as i:
                    qTcur_of(i * 2, 0)
                    qTcur_of(i * 2 + 1, 1)
                qTcur_of(NT - 1, 0)
                act.wait_ge(var_set, 3)
                act.activation(std[:], rstd[:], ACT.Sqrt).then_inc(std_set, 1)
                act.preload_act_table(ACT.Gelu)

                def gelu(t, y):
                    act.wait_ge(ff_done, t + 1)
                    act.wait_ge(m_done, t + 1)
                    for f in range(FM):
                        act.activation(gT[:, y, f, :], ps_ff[y][f // FB][:, f % FB * P:(f % FB + 1) * P], ACT.Gelu,
                                       bias=b1_col[:, f:f + 1]).then_inc(g_set, 1)
                with act.Fori(0, NT // 2) as i:
                    for y in range(2):
                        gelu(i * 2 + y, y)
                gelu(NT - 1, 0)

            @block.tensor
            def _(pe):
                pe.wait_ge(counted, 1)
                pe.matmul(ps_a[:, 0:NT], ones[:], cnt[:], start=True, stop=True).then_inc(prefixed, 1)
                pe.matmul(ps_b[:, 0:NT], below[:], cnt[:], start=True, stop=True).then_inc(prefixed, 1)
                pe.wait_ge(small_in, 16 * 3 * MH)
                pe.wait_ge(w_set, 1)
                pe.wait_ge(w_in, 16 * loads)
                pe.wait_ge(slots_set, 1)
                pe.sem_inc(turned, 1)

                def turn(t):
                    pe.wait_ge(hn_set, t + 1)
                    pe.wait_ge(xcur_set, t + 1)
                    for c in range(CC):
                        pe.transpose(ps_a[:, c * P:(c + 1) * P], xcur[:, c * P:(c + 1) * P], ident[:])
                    for c in range(CC):
                        last = pe.transpose(ps_b[:, c * P:(c + 1) * P], hn[:, c * P:(c + 1) * P], ident[:])
                    last.then_inc(turned, 1)

                def h_and_xm(t):
                    pe.wait_ge(xnT_set, t + 1)
                    pe.wait_ge(h_out, 3 * t + 3)
                    for c in range(CC):
                        last = pe.matmul(ps_c[:, 0:C + 2 * HEADS1], xnT[:, c, :], gat_w[:, c, :], start=c == 0, stop=c == CC - 1)
                    last.then_inc(h_done, 1)
                    pe.wait_ge(hnT_set, 2 * t + 2)
                    for m in range(CC):
                        for c in range(CC):
                            last = pe.matmul(ps_d[:, m * P:(m + 1) * P], wx[:, c, m * P:(m + 1) * P], hnT[:, c, :],
                                             start=c == 0, stop=c == CC - 1)
                    last.then_inc(xm_done, 1)

                def qkv(t):
                    pe.wait_ge(xmT_set, 2 * t + 2)
                    pe.wait_ge(v_out, t + 1)
                    pe.wait_ge(qk_out, 2 * t + 2)
                    for c in range(CC):
                        pe.matmul(ps_e[:, 0:C], xmT[:, c, :], wv[:, c, :], start=c == 0, stop=c == CC - 1)
                    for c in range(CC):
                        pe.matmul(ps_f[:, P:P + QK], xmT[:, c, :], wq[:, c, :], start=c == 0, stop=c == CC - 1)
                    for c in range(CC):
                        last = pe.matmul(ps_f[0:QK, 0:P], wk[:, c, :], xmT[:, c, :], start=c == 0, stop=c == CC - 1)
                    last.then_inc(qkv_done, 1)
                turn(0)
                with pe.Fori(0, NT - 1) as t:
                    h_and_xm(t)
                    turn(t + 1)
                    qkv(t)
                h_and_xm(NT - 1)
                qkv(NT - 1)
                pe.sem_inc(qk_turned, 1)
                pe.wait_ge(h_out, 3 * NT + 3)
                pe.matmul(ps_c[0:QK, 0:C + 1], zrow[:, 0:QK], zrow[:], start=True, stop=False,
                          skip_group_check=True).then_inc(kv_done, 1)
                pe.sem_inc(kv_done, 1)
                pe.sem_inc(qT_set, 2)

                def turn_qk(t):
                    pe.wait_ge(cur_set, 2 * t + 2)
                    pe.wait_ge(qT_set, 2 * t + 2)
                    pe.transpose(ps_a[0:QK, 0:P], qcur[:], ident[:])
                    pe.transpose(ps_b[:, 0:QK], kcur[:], ident[0:QK, 0:QK]).then_inc(qk_turned, 1)

                def add_kv(t, y):
                    pe.wait_ge(qT_set, 2 * t + 4)
                    pe.matmul(ps_c[0:QK, 0:C + 1], ek[:, y, :], tile_of(v1, t), start=False, stop=False,
                              skip_group_check=True).then_inc(kv_done, 1)
                turn_qk(0)
                with pe.Fori(0, NT // 2) as i:
                    for y in range(2):
                        turn_qk(i * 2 + y + 1)
                        add_kv(i * 2 + y, y)
                add_kv(NT - 1, 0)
                pe.matmul(ps_c[0:QK, 0:C + 1], zrow[:, 0:QK], zrow[:], start=False, stop=True,
                          skip_group_check=True).then_inc(kv_done, 1)
                pe.wait_ge(kv_set, 1)
                for c in range(CC):
                    last = pe.transpose(ps_a[:, c * QK:(c + 1) * QK], kv[:, c * P:(c + 1) * P], ident[0:QK, 0:QK])
                last.then_inc(kv_turned, 1)
                pe.wait_ge(kvT_set, 1)
                for c in range(CC):
                    last = pe.matmul(ps_b[0:QK, 0:C], kvT[:, c, :], wo[:, c, :], start=c == 0, stop=c == CC - 1)
                last.then_inc(ko_done, 1)
                pe.wait_ge(ko_set, 1)
                pe.sem_inc(fx_set, 2)
                pe.sem_inc(attn_done, 2)

                def attend(t, y):
                    pe.wait_ge(qTcur_set, t + 1)
                    pe.wait_ge(fx_set, t + 1)
                    pe.matmul(ps_at[y][:, 0:C], qTcur[:, y, :], ko[:], start=True, stop=True).then_inc(attn_done, 1)
                with pe.Fori(0, NT // 2) as i:
                    attend(i * 2, 0)
                    attend(i * 2 + 1, 1)
                attend(NT - 1, 0)
                pe.wait_ge(fx_set, NT + 2)

                def turn_fn(t):
                    pe.wait_ge(fn_set, t + 1)
                    pe.wait_ge(fnT_set, 2 * t + 2)
                    for c in range(CC):
                        last = pe.transpose(ps_a[:, c * P:(c + 1) * P], hn[:, c * P:(c + 1) * P], ident[:])
                    last.then_inc(fn_turned, 1)

                def up(t, y):
                    pe.wait_ge(fnT_set, 2 * t + 4)
                    pe.wait_ge(g_set, FM * (t + 1))
                    for f in range(FM):
                        for c in range(CC):
                            last = pe.matmul(ps_ff[y][f // FB][:, f % FB * P:(f % FB + 1) * P],
                                             w1[:, c, f * P:(f + 1) * P], hnT[:, c, :], start=c == 0, stop=c == CC - 1)
                    last.then_inc(ff_done, 1)

                def down(t, y):
                    pe.wait_ge(g_set, FM * (t + 3))
                    pe.wait_ge(sum_set, t + 1)
                    pe.matmul(ps_d[:, 0:C], ones[0:1, :], b2_row[:], start=True, stop=False)
                    for f in range(FM):
                        last = pe.matmul(ps_d[:, 0:C], gT[:, y, f, :], w2[:, f, :], start=False, stop=f == FM - 1)
                    last.then_inc(m_done, 1)
                pe.sem_inc(fn_turned, 1)
                pe.sem_inc(fnT_set, 2)
                pe.sem_inc(g_set, 2 * FM)
                pe.sem_inc(mix_set, 1)
                pe.sem_inc(sum_set, 1)
                pe.sem_inc(m_done, 2)
                turn_fn(0)
                up(0, 0)
                turn_fn(1)
                with pe.Fori(0, (NT - 3) // 2) as i:
                    for y in range(2):
                        up(i * 2 + y + 1, 1 - y)
                        turn_fn(i * 2 + y + 2)
                        down(i * 2 + y, y)
                up(NT - 2, 1)
                turn_fn(NT - 1)
                down(NT - 3, 0)
                up(NT - 1, 0)
                down(NT - 2, 1)
                down(NT - 1, 0)


def edge_tables(nc, k, alloc, sems, sorted_edges, dst_row, src_row):
    with ExitStack() as st:
        sb, sem = alloc(st), sems(st)
        rows = sb("rows", [TR, 4, P, 2], I32)
        part = sb("part", [TR, 4, P], I32)
        names = ("src_f", "dst_lo", "src_hi", "block", "src_lo", "pad")
        src_f, dst_lo, src_hi, block_f, src_lo, pad = (sb(n, [TR, 4, P]) for n in names)
        ps = [st.enter_context(nc.psum_tensor(f"ps_t{j}", [P, 512], F32)) for j in range(4)]
        rows_in, own_s, rows_set, turned = sem("rows_in"), sem("tables_own"), sem("rows_set"), sem("tables_turned")
        rows_out = sem("rows_out")
        with nc.Block() as block:
            @block.sync
            def _(sp):
                sp.dma_start(rows[:].rearrange("t c p w -> t c (p w)"),
                             sorted_edges.rearrange("(c t p) w -> t c (p w)", c=4, p=P)).then_inc(rows_in, 16)
                sp.wait_ge(rows_set, 1)
                sp.dma_start(dst_row.rearrange("(c t p) -> t c p", c=4, p=P), dst_lo[:]).then_inc(rows_out, 16)
                sp.dma_start(src_row.rearrange("(c t p) -> t c p", c=4, p=P), src_lo[:]).then_inc(rows_out, 16)
                sp.wait_ge(rows_out, 32)

            @block.vector
            def _(dve):
                own = Steps(dve, own_s)
                link = own.link
                dve.wait_ge(rows_in, 16)
                src, dst = rows[:, :, :, 0], rows[:, :, :, 1]
                own.did(dve.tensor_copy(src_f[:], src))
                link(dve.tensor_copy(pad[:], dst))
                own.did(dve.tensor_scalar(pad[:], pad[:], float(NP), float(P), ALU.is_ge, ALU.mult))
                link(dve.tensor_scalar(part[:], dst, P - 1, None, ALU.bitwise_and))
                link(dve.tensor_copy(dst_lo[:], part[:]))
                link(dve.tensor_tensor(dst_lo[:], dst_lo[:], pad[:], ALU.add))
                link(dve.tensor_scalar(part[:], src, P - 1, None, ALU.bitwise_and))
                link(dve.tensor_copy(src_lo[:], part[:]))
                link(dve.tensor_scalar(part[:], src, 7, None, ALU.arith_shift_right))
                link(dve.tensor_copy(src_hi[:], part[:]))
                link(dve.tensor_scalar(part[:], dst, 7, None, ALU.arith_shift_right))
                link(dve.tensor_copy(block_f[:], part[:]))
                dve.tensor_scalar(block_f[:], block_f[:], float(NT - 1), None, ALU.min).then_inc(rows_set, 1)
                dve.wait_ge(turned, 4)
                for j, dst_t in enumerate((k["src_col"][:], k["dst_col"][:], k["hi_col"][:])):
                    dve.tensor_copy(dst_t, ps[j][:, 0:TT])
                own.did(dve.memset(k["block_row"][:, 0:BATCH], 0))
                own.did(dve.tensor_copy(k["block_row"][:, BATCH:], ps[3][0:1, 0:TT]))
                own.settle()

            @block.tensor
            def _(pe):
                pe.wait_ge(rows_set, 1)
                for j, t in enumerate((src_f, dst_lo, src_hi, block_f)):
                    for c in range(4):
                        last = pe.transpose(ps[j][:, c * TR:(c + 1) * TR], t[:, c, :], k["ident"][0:TR, 0:TR])
                    last.then_inc(turned, 1)


def segment_max(nc, layer, H, k, es, ed, top_e, em, alloc, sems, src_row):
    with ExitStack() as st:
        sb, sem = alloc(st), sems(st)

        def s(name):
            return sem(f"{name}_{layer}")
        FETCH_FIRST = H > 1
        low, low_row, floor_ = sb("low", [P, 1]), sb("low_row", [1, 1]), sb("floor", [P, 1])
        raised = sb("raised", [P, NT, H])
        zeros = sb("zeros", [1, H * P])
        src_b = sb("src_b", [P, 2, BATCH * P])
        pick_lo = sb("pick_lo", [P, 2, BATCH * P])
        pick_hi = sb("pick_hi", [P, 2, BATCH, NT])
        picked = sb("picked", [P, BATCH, NT, H])
        es_e = sb("es_e", [P, 2, BATCH, H])
        spread = sb("spread", [P, 2, BATCH, H, P])
        best = sb("best", [P, BATCH, H])
        is_dst = sb("is_dst", [P, 2, BATCH, P])
        iota_row, iota_col = k["iota_row"], k["iota_col"]
        ps_f = [st.enter_context(nc.psum_tensor(f"ps_f{y}_{layer}", [P, 512], F32)) for y in range(2)]
        ps_v = st.enter_context(nc.psum_tensor(f"ps_v_{layer}", [P, BATCH, 512], F32))
        own_s, low_set, low_turned, low_spread = s("max_own"), s("low_set"), s("low_turned"), s("low_spread")
        src_in = [s(f"src_in{y}") for y in range(2)]
        picks_set, fetched, fetch_read = s("picks_set"), s("fetched"), s("fetch_read")
        es_set, dst_set, spread_set, turned, best_set = s("es_set"), s("dst_set"), s("spread_set"), s("spread_turned"), s("best_set")
        hi_set, dst_copied = s("hi_set"), s("dst_copied")
        dst_cur, scratch = sb("dst_cur", [P, 2, BATCH]), sb("pool_scratch_m", [1, 1])
        src_rows = src_row.rearrange("(b n) -> b n", n=BATCH * P)

        with nc.Block() as block:
            @block.sync
            def _(sp):
                def fetch(i, y):
                    b = i * 2 + y
                    sp.wait_ge(picks_set, b + 1)
                    sp.dma_start(src_b[:, y, :], src_rows[bass.ds(b, 1), :].to_broadcast([P, BATCH * P])).then_inc(src_in[y], 16)
                with sp.Fori(0, NB // 2) as i:
                    fetch(i, 0)
                    fetch(i, 1)
                fetch(NB // 2, 0)
                fetch(NB // 2, 1)

            @block.vector
            def _(dve):
                own = Steps(dve, own_s)
                link = own.link
                own.did(dve.memset(zeros[:], 0.0))
                link(dve.tensor_reduce(low[:], es[:].rearrange("p t h -> p (t h)"), AX.X, ALU.min))
                dve.sem_inc(low_set, 1)
                dve.wait_ge(low_turned, 1)
                dve.tensor_reduce(low_row[:], ps_f[0][0:1, 0:P], AX.X, ALU.min).then_inc(low_set, 1)
                dve.wait_ge(low_spread, 1)
                link(dve.tensor_scalar(floor_[:], ps_f[1][:, 0:1], -1.0, None, ALU.add))
                link(dve.tensor_scalar(raised[:], es[:], floor_[:, 0:1], None, ALU.subtract))
                link(dve.tensor_tensor(top_e[:], raised[:], k["loops"][:].unsqueeze(2).to_broadcast([P, NT, H]), ALU.mult))
                dve.sem_inc(picks_set, 2)
                dve.sem_inc(fetch_read, 2)
                dve.sem_inc(best_set, BATCH)

                def by_place(i, y):
                    b = i * 2 + y
                    dve.wait_ge(src_in[y], (i + 1) * 16)
                    dve.wait_ge(fetched, b + 1)
                    dve.tensor_scalar(pick_lo[:, y, :], src_b[:, y, :], iota_col[:, 0:1], None, ALU.is_equal).then_inc(picks_set, 1)

                def by_tile(b, y):
                    dve.tensor_tensor(pick_hi[:, y], iota_row[:, 0:NT].unsqueeze(1).to_broadcast([P, BATCH, NT]),
                                      k["hi_col"][:, bass.ds(b * BATCH, BATCH)].unsqueeze(2).to_broadcast([P, BATCH, NT]),
                                      ALU.is_equal).then_inc(hi_set, 1)

                def pick(b, y):
                    dve.wait_ge(fetched, b + 3)
                    dve.wait_ge(hi_set, b + 1)
                    dve.tensor_tensor(picked[:], ps_f[y][:, 0:BATCH * NT * H].rearrange("p (k t h) -> p k t h", k=BATCH, h=H),
                                      pick_hi[:, y].unsqueeze(3).to_broadcast([P, BATCH, NT, H]), ALU.mult).then_inc(fetch_read, 1)

                def es_of(b, y):
                    dve.wait_ge(fetch_read, b + 3)
                    dve.wait_ge(spread_set, BATCH * H * (b + 1))
                    dve.tensor_reduce(es_e[:, y], picked[:].rearrange("p k t h -> p k h t"), AX.X, ALU.add).then_inc(es_set, 1)

                def step(i, y):
                    b = i * 2 + y

                    def fetch_part(j):
                        if j == 0:
                            by_place(i + 1, y)
                        if j == 1:
                            by_tile(b + 2, y)
                        if j == 2:
                            dve.wait_ge(es_set, b + 1)
                            pick(b + 1, 1 - y)
                        if j == 3:
                            es_of(b + 1, 1 - y)
                    if FETCH_FIRST:
                        for j in range(BATCH):
                            fetch_part(j)
                    blocks = blocks_of(nc, mybir.EngineType.DVE, k, b - 1)
                    for j in range(BATCH + 1):
                        if j < BATCH:
                            dve.wait_ge(turned, BATCH * (b + 1) + j + 1)
                            dve.tensor_reduce(best[:, j, :], ps_v[:, j, 0:H * P].rearrange("p (h e) -> p h e", h=H), AX.X,
                                              ALU.max).then_inc(best_set, 1)
                        if not FETCH_FIRST:
                            fetch_part(j)
                        if j > 0:
                            at = top_e[:, bass.ds(blocks[j - 1], 1), :].rearrange("p o h -> p (o h)")
                            dve.wait_ge(best_set, BATCH * (b + 1) + j)
                            own.settle()
                            own.did(dve.tensor_tensor(at, at, best[:, j - 1, :], ALU.max))

                for y in range(2):
                    by_place(0, y)
                    by_tile(y, y)
                pick(0, 0)
                es_of(0, 0)
                with own.loop(NB // DEPTH, DEPTH * BATCH) as i:
                    for y in range(DEPTH):
                        step(i * (DEPTH // 2) + y // 2, y % 2)
                blocks = blocks_of(nc, mybir.EngineType.DVE, k, NB - 1)
                for j in range(BATCH):
                    at = top_e[:, bass.ds(blocks[j], 1), :].rearrange("p o h -> p (o h)")
                    dve.wait_ge(turned, BATCH * (NB + 1) + j + 1)
                    dve.tensor_reduce(best[:, j, :], ps_v[:, j, 0:H * P].rearrange("p (h e) -> p h e", h=H), AX.X,
                                      ALU.max).then_inc(best_set, 1)
                    dve.wait_ge(best_set, BATCH * (NB + 1) + j + 1)
                    own.settle()
                    own.did(dve.tensor_tensor(at, at, best[:, j, :], ALU.max))
                own.settle()
                m = em[:, :, H:2 * H]
                link(dve.tensor_copy(em[:, :, 0:H], ed[:]))
                link(dve.scalar_tensor_tensor(top_e[:], top_e[:], floor_[:, 0:1], ed[:], ALU.add, ALU.add))
                link(dve.scalar_tensor_tensor(m, top_e[:], SLOPE, top_e[:], ALU.mult, ALU.max))

            @block.gpsimd
            def _(pool):
                def to_dst(i, y):
                    b = i * 2 + y
                    pool.wait_ge(spread_set, BATCH * H * (b + 1))
                    pool.tensor_copy(dst_cur[:, y, :], k["dst_col"][:, bass.ds(b * BATCH, BATCH)]).then_inc(dst_copied, 1)
                    pool.wait_ge(dst_copied, b + 1)
                    pool.tensor_tensor(scratch[:], k["ones"][0:1, 0:1], k["ones"][0:1, 0:1], ALU.add)
                    for j in range(BATCH):
                        pool.tensor_scalar(is_dst[:, y, j, :], iota_row[:], dst_cur[:, y, j:j + 1],
                                           None, ALU.is_equal).then_inc(dst_set, 1)
                with pool.Fori(0, NB // DEPTH) as i:
                    for y in range(DEPTH):
                        to_dst(i * (DEPTH // 2) + y // 2, y % 2)

            @block.scalar
            def _(act):
                act.sem_inc(spread_set, 2 * BATCH * H)
                with act.Fori(0, NB // DEPTH) as i:
                    for y4 in range(DEPTH):
                        b, y = i * DEPTH + y4, y4 % 2
                        act.wait_ge(turned, BATCH * (b + 1))
                        act.wait_ge(es_set, b + 1)
                        for j in range(BATCH):
                            act.wait_ge(dst_set, BATCH * b + j + 1)
                            for h in range(H):
                                act.activation(spread[:, y, j, h, :], is_dst[:, y, j, :], ACT.Copy,
                                               scale=es_e[:, y, j, h:h + 1]).then_inc(spread_set, 1)

            @block.tensor
            def _(pe):
                pe.sem_inc(turned, BATCH)
                pe.wait_ge(low_set, 1)
                for j in range(BATCH):
                    pe.matmul(ps_v[:, j, 0:H * P], zeros[:, 0:P], zeros[:, 0:H * P], start=True, stop=True).then_inc(turned, 1)
                pe.transpose(ps_f[0][0:1, 0:P], low[:], k["ident"][:]).then_inc(low_turned, 1)
                pe.wait_ge(low_set, 2)
                pe.matmul(ps_f[1][:, 0:1], k["ones"][0:1, :], low_row[:], start=True, stop=True).then_inc(low_spread, 1)
                pe.sem_inc(fetched, 2)

                def fetch(i, y):
                    b = i * 2 + y
                    pe.wait_ge(picks_set, b + 3)
                    pe.wait_ge(fetch_read, b + 1)
                    for j in range(BATCH):
                        last = pe.matmul(ps_f[y][:, j * NT * H:(j + 1) * NT * H], pick_lo[:, y, j * P:(j + 1) * P],
                                         raised[:].rearrange("p t h -> p (t h)"), start=True, stop=True)
                    last.then_inc(fetched, 1)

                def step(i, y):
                    b = i * 2 + y
                    if FETCH_FIRST:
                        fetch(i + 1, y)
                    pe.wait_ge(spread_set, BATCH * H * (b + 3))
                    for j in range(BATCH):
                        pe.wait_ge(best_set, BATCH * (b + 1) + j + 1)
                        for h in range(H):
                            last = pe.transpose(ps_v[:, j, h * P:(h + 1) * P], spread[:, y, j, h, :], k["ident"][:])
                        last.then_inc(turned, 1)
                    if not FETCH_FIRST:
                        fetch(i + 1, y)

                fetch(0, 0)
                fetch(0, 1)
                with pe.Fori(0, NB // DEPTH) as i:
                    for y in range(DEPTH):
                        step(i * (DEPTH // 2) + y // 2, y % 2)


def weighted_sum(nc, layer, H, k, em, es, acc, wself, table, alloc, sems, dst_row):
    with ExitStack() as st:
        sb, sem = alloc(st), sems(st)

        def s(name):
            return sem(f"{name}_{layer}")
        W = C + H
        BY_ACT = 2 if H > 1 else BATCH
        zeros = sb("zeros", [1, W])
        dst_b = sb("dst_b", [P, 2, BATCH * P])
        to_edge = sb("to_edge", [P, 2, BATCH * P])
        to_dst = sb("to_dst", [P, DEPTH, BATCH, P])
        rows = sb("rows_h", [P, DEPTH, BATCH, W])
        logit, leaky = sb("logit", [P, 2, BATCH, H]), sb("leaky", [P, 2, BATCH, H])
        cur = sb("cur_src", [P, DEPTH // 2, 2 * BATCH], I32)
        scratch = sb("pool_scratch_h", [1, 1])
        tself = sb("tself", [P, NT, H])
        ps_e = [st.enter_context(nc.psum_tensor(f"ps_e{y}_{layer}", [P, 512], F32)) for y in range(2)]
        ps_o = st.enter_context(nc.psum_tensor(f"ps_o_{layer}", [P, BATCH, 512], F32))
        own_s, self_set, self_exp = s("sum_own"), s("self_set"), s("self_exp")
        dst_in = [s(f"dst_in{y}") for y in range(2)]
        gathered = [[s(f"gathered{y}{j}") for j in range(BATCH)] for y in range(DEPTH)]
        copied, onehots, fetched, ed_read = s("copied"), s("onehots"), s("ed_fetched"), s("ed_read")
        zeros_set, act_msg, to_dst_set = s("zeros_set"), s("act_msg"), s("to_dst_set")
        logit_set, w_set, msg_set, summed, added = s("logit_set"), s("w_set"), s("msg_set"), s("summed"), s("added")
        dst_rows = dst_row.rearrange("(b n) -> b n", n=BATCH * P)

        with nc.Block() as block:
            @block.sync
            def _(sp):
                def fetch(i, y):
                    b = i * 2 + y
                    sp.wait_ge(onehots, b + 1)
                    sp.dma_start(dst_b[:, y, :], dst_rows[bass.ds(b, 1), :].to_broadcast([P, BATCH * P])).then_inc(dst_in[y], 16)
                with sp.Fori(0, NB // 2) as i:
                    fetch(i, 0)
                    fetch(i, 1)
                fetch(NB // 2, 0)

            @block.gpsimd
            def _(pool):
                pool.memset(scratch[:], 0.0)

                def gather(i, y):
                    b = i * DEPTH + y
                    pool.wait_ge(summed, BATCH * (b + 2))
                    pool.tensor_copy(cur[:, y // 2, :], k["src_col"][:, bass.ds(b * BATCH, 2 * BATCH)]).then_inc(copied, 1)
                    pool.wait_ge(copied, i * (DEPTH // 2) + y // 2 + 1)
                    pool.tensor_tensor(scratch[:], k["ones"][0:1, 0:1], k["ones"][0:1, 0:1], ALU.add)
                    for j in range(2 * BATCH):
                        z, j4 = y + j // BATCH, j % BATCH
                        pool.indirect_dma_start(rows[:, z, j4, :], None, table,
                                                bass.IndirectOffsetOnAxis(cur[:, y // 2, j:j + 1], 0)).then_inc(gathered[z][j4], 16)
                with pool.Fori(0, NB // DEPTH) as i:
                    for y in range(0, DEPTH, 2):
                        gather(i, y)

            @block.vector
            def _(dve):
                own = Steps(dve, own_s)
                link = own.link
                m = em[:, :, H:2 * H]
                dve.memset(zeros[:], 0.0).then_inc(zeros_set, 1)
                own.did(dve.memset(acc[:], 0.0))
                link(dve.tensor_tensor(tself[:], es[:], em[:, :, 0:H], ALU.add))
                link(dve.scalar_tensor_tensor(tself[:], tself[:], SLOPE, tself[:], ALU.mult, ALU.max))
                link(dve.tensor_tensor(tself[:], tself[:], m, ALU.subtract))
                dve.tensor_scalar(tself[:], tself[:], 1.0, None, ALU.min).then_inc(self_set, 1)
                dve.sem_inc(onehots, 2)
                dve.sem_inc(ed_read, 2)
                dve.sem_inc(added, BATCH)

                def onehot(i, y4, j):
                    b = i * DEPTH + y4
                    if j == 0:
                        dve.wait_ge(summed, BATCH * (b + 1))
                    dve.tensor_scalar(to_dst[:, y4, j, :], k["iota_row"][:], k["dst_col"][:, bass.ds(b * BATCH + j, 1)],
                                      None, ALU.is_equal).then_inc(to_dst_set, 1)
                    if j == BATCH - 1:
                        y = y4 % 2
                        dve.wait_ge(dst_in[y], (i * (DEPTH // 2) + y4 // 2 + 1) * 16)
                        dve.wait_ge(fetched, b + 1)
                        dve.tensor_scalar(to_edge[:, y, :], dst_b[:, y, :], k["iota_col"][:, 0:1], None, ALU.is_equal).then_inc(onehots, 1)

                def add(b, between):
                    blocks = blocks_of(nc, mybir.EngineType.DVE, k, b)
                    for j in range(BATCH):
                        at = acc[:, bass.ds(blocks[j], 1), :].rearrange("p o c -> p (o c)")
                        dve.wait_ge(summed, BATCH * (b + DEPTH) + j + 1)
                        dve.wait_ge(added, BATCH * (b + 2) + j)
                        dve.tensor_tensor(at, at, ps_o[:, j, 0:W], ALU.add).then_inc(added, 1)
                        between(j)

                def step(i, y4):
                    b, y = i * DEPTH + y4, y4 % 2
                    after = (i, y4 + 1) if y4 + 1 < DEPTH else (i + 1, 0)
                    for j in range(BATCH):
                        dve.wait_ge(gathered[y4][j], (i + 1) * 16)
                    dve.wait_ge(fetched, b + 3)
                    edm = ps_e[y][:, 0:BATCH * 2 * H].rearrange("p (k w) -> p k w", w=2 * H)
                    own.did(dve.tensor_tensor(logit[:, y], rows[:, y4, :, C:W], edm[:, :, 0:H], ALU.add))
                    onehot(*after, 0)
                    own.settle()
                    own.did(dve.scalar_tensor_tensor(leaky[:, y], logit[:, y], SLOPE, logit[:, y], ALU.mult, ALU.max))
                    onehot(*after, 1)
                    own.settle()
                    dve.tensor_tensor(logit[:, y], leaky[:, y], edm[:, :, H:2 * H], ALU.subtract).then_inc(ed_read, 1)
                    onehot(*after, 2)
                    dve.wait_ge(ed_read, b + 3)
                    dve.tensor_scalar(leaky[:, y], logit[:, y], 1.0, None, ALU.min).then_inc(logit_set, 1)
                    onehot(*after, 3)

                    def message(j):
                        j += BY_ACT
                        if j < BATCH:
                            dve.wait_ge(w_set, b + 1)
                            msg = rows[:, y4, j, 0:C].rearrange("p (h d) -> p h d", h=H)
                            dve.tensor_tensor(msg, msg, rows[:, y4, j, C:W].unsqueeze(2).to_broadcast([P, H, C // H]),
                                              ALU.mult).then_inc(msg_set, 1)
                    add(b - 1, message)

                for j in range(BATCH):
                    onehot(0, 0, j)
                with own.loop(NB // DEPTH, DEPTH * 2) as i:
                    for y in range(DEPTH):
                        step(i, y)
                add(NB - 1, lambda j: None)
                dve.wait_ge(added, BATCH * (NB + 2))
                dve.wait_ge(self_exp, 1)
                link(dve.tensor_tensor(wself[:], wself[:], k["loops"][:].unsqueeze(2).to_broadcast([P, NT, H]), ALU.mult))

            @block.scalar
            def _(act):
                act.wait_ge(self_set, 1)
                act.activation(wself[:], tself[:], ACT.Exp).then_inc(self_exp, 1)
                with act.Fori(0, NB // DEPTH) as i:
                    for y in range(DEPTH):
                        b = i * DEPTH + y
                        act.wait_ge(logit_set, b + 1)
                        act.activation(rows[:, y, :, C:W], leaky[:, y % 2], ACT.Exp).then_inc(w_set, 1)
                        act.wait_ge(w_set, b + 1)
                        for j in range(BY_ACT):
                            for h in range(H):
                                msg = rows[:, y, j, h * (C // H):(h + 1) * (C // H)]
                                act.activation(msg, msg, ACT.Copy, scale=rows[:, y, j, C + h:C + h + 1]).then_inc(act_msg, 1)

            @block.tensor
            def _(pe):
                pe.sem_inc(fetched, 2)
                pe.sem_inc(summed, (DEPTH - 1) * BATCH)
                pe.wait_ge(zeros_set, 1)
                for j in range(BATCH):
                    pe.matmul(ps_o[:, j, 0:W], zeros[:, 0:P], zeros[:], start=True, stop=True).then_inc(summed, 1)

                def fetch(i, y4):
                    b, y = i * DEPTH + y4, y4 % 2
                    blocks = blocks_of(nc, mybir.EngineType.PE, k, b)
                    pe.wait_ge(onehots, b + 3)
                    pe.wait_ge(ed_read, b + 1)
                    for j in range(BATCH):
                        last = pe.matmul(ps_e[y][:, j * 2 * H:(j + 1) * 2 * H], to_edge[:, y, j * P:(j + 1) * P],
                                         em[:, bass.ds(blocks[j], 1), :].rearrange("p o w -> p (o w)"), start=True, stop=True)
                    last.then_inc(fetched, 1)

                def step(i, y4):
                    b = i * DEPTH + y4
                    fetch(*((i, y4 + 1) if y4 + 1 < DEPTH else (i + 1, 0)))
                    pe.wait_ge(to_dst_set, BATCH * (b + 1))
                    for j in range(BATCH):
                        if j < BY_ACT:
                            pe.wait_ge(act_msg, H * (BY_ACT * b + j + 1))
                        else:
                            pe.wait_ge(msg_set, (BATCH - BY_ACT) * b + j - BY_ACT + 1)
                        pe.wait_ge(added, BATCH * (b + 1) + j + 1)
                        pe.matmul(ps_o[:, j, 0:W], to_dst[:, y4, j, :], rows[:, y4, j, :], start=True, stop=True).then_inc(summed, 1)

                fetch(0, 0)
                with pe.Fori(0, NB // DEPTH) as i:
                    for y in range(DEPTH):
                        step(i, y)


def tile_of(t3, t):
    return t3[:, bass.ds(t, 1), :].rearrange("p o c -> p (o c)")


def aggregate(dve, own, H, h1, acc, wself, bias_b):
    link = own.link

    def by_head(ap):
        return ap.rearrange("p t (h d) -> p t h d", h=H)

    def wide(w):
        return w[:].unsqueeze(3).to_broadcast([P, NT, H, C // H])
    link(dve.tensor_tensor(by_head(h1[:]), by_head(h1[:]), wide(wself[0]), ALU.mult))
    link(dve.tensor_tensor(h1[:], h1[:], acc[:, :, 0:C], ALU.add))
    link(dve.tensor_tensor(by_head(h1[:]), by_head(h1[:]), wide(wself[1]), ALU.mult))
    link(dve.tensor_tensor(h1[:], h1[:], bias_b[:].unsqueeze(1).to_broadcast([P, NT, C]), ALU.add))


def moments(dve, own, src, halves, gap, mv):
    with own.loop(NT // GROUP, GROUP) as i:
        for y in range(GROUP):
            own.did(dve.bn_stats(tile_of(halves, i * GROUP + y), tile_of(src, i * GROUP + y)))
    own.settle()
    mean, var = mv[:, :, 0], mv[:, :, 1]
    own.did(dve.tensor_tensor(gap[:], halves[:, :, 1], halves[:, :, 4], ALU.subtract))
    own.did(dve.tensor_tensor(mean, halves[:, :, 1], halves[:, :, 4], ALU.add))
    own.link(dve.tensor_tensor(var, halves[:, :, 2], halves[:, :, 5], ALU.add))
    own.did(dve.tensor_scalar(mean, mean, 0.5, None, ALU.mult))
    own.did(dve.tensor_scalar(var, var, 1.0 / C, None, ALU.mult))
    own.link(dve.tensor_tensor(gap[:], gap[:], gap[:], ALU.mult))
    own.link(dve.scalar_tensor_tensor(var, gap[:], 0.25, var, ALU.mult, ALU.add))


def between_layers(nc, a, k, acc, wself, alloc, sems, table2):
    with ExitStack() as st:
        sb, sem = alloc(st), sems(st)
        h1, gat_w = k["h1"], k["gat2_w"]
        bias_b, hn = sb("gnn_b1_b", [P, C]), sb("on", [P, C])
        g_col, b_col = sb("g_col", [P, CC]), sb("b_col", [P, CC])
        rden = sb("rden", [P, NT, HEADS1])
        halves, gap, mv = sb("halves_o", [P, NT, 6]), sb("gap_o", [P, NT]), sb("mv_o", [P, NT, 2])
        std, rstd = sb("std_o", [P, NT]), sb("rstd_o", [P, NT])
        rT = sb("rT", [P, 2, CC, P])
        tabrow = sb("tabrow2", [P, C + 1])
        ps_t = st.enter_context(nc.psum_tensor("ps_t", [P, 512], F32))
        ps_h = st.enter_context(nc.psum_tensor("ps_h", [P, 512], F32))
        b_in, own_s, var_set, std_set, on_set = (sem(n) for n in ("mid_in", "mid_own", "mid_var", "mid_std", "on_set"))
        bias_in = sem("mid_bias_in")
        turned, rT_set, h_done, row_set, h_out, row_out = (sem(n) for n in ("mid_turned", "rT_set", "mid_h", "row2_set", "h2_out", "row2_out"))
        with nc.Block() as block:
            @block.sync
            def _(sp):
                sp.dma_start(bias_b[:], a["L0_gnn_b1"].partition_broadcast(P)).then_inc(bias_in, 16)
                with nc.allow_non_contiguous_dma(reason="a bias of a few hundred values, one a partition"):
                    sp.dma_start(g_col[:], a["L0_gnn_ln_g"].rearrange("(c p) -> p c", p=P)).then_inc(b_in, 16)
                    sp.dma_start(b_col[:], a["L0_gnn_ln_b"].rearrange("(c p) -> p c", p=P)).then_inc(b_in, 16)
                sp.sem_inc(row_out, 16)
                with sp.Fori(0, NT) as t:
                    sp.wait_ge(row_set, t + 1)
                    sp.dma_start(table2[bass.ds(t * P, P), :], tabrow[:]).then_inc(row_out, 16)
                sp.wait_ge(row_out, 16 * (NT + 1))

            @block.vector
            def _(dve):
                own = Steps(dve, own_s)
                link = own.link
                link(dve.tensor_tensor(rden[:], acc[:, :, C:C + HEADS1], wself[:], ALU.add))
                link(dve.tensor_scalar(rden[:], rden[:], 1e-30, None, ALU.max))
                link(dve.reciprocal(rden[:], rden[:]))
                dve.wait_ge(bias_in, 16)
                aggregate(dve, own, HEADS1, h1, acc, (wself, rden), bias_b)
                moments(dve, own, h1, halves, gap, mv)
                dve.tensor_scalar(rstd[:], mv[:, :, 1], EPS, None, ALU.add).then_inc(var_set, 1)
                dve.wait_ge(std_set, 1)
                link(dve.reciprocal(rstd[:], std[:]))
                with own.loop(NT, 0) as t:
                    dve.wait_ge(turned, t + 1)
                    dve.tensor_scalar(hn[:], tile_of(h1, t), mv[:, bass.ds(t, 1), 0:1].rearrange("p o c -> p (o c)"),
                                      rstd[:, bass.ds(t, 1)], ALU.subtract, ALU.mult).then_inc(on_set, 1)

            @block.scalar
            def _(act):
                act.wait_ge(var_set, 1)
                act.activation(std[:], rstd[:], ACT.Sqrt).then_inc(std_set, 1)
                act.wait_ge(b_in, 32)
                act.sem_inc(h_out, 3)

                def relu(t, y):
                    act.wait_ge(turned, t + 2)
                    for c in range(CC):
                        act.activation(rT[:, y, c, :], ps_t[:, c * P:(c + 1) * P], ACT.Relu, bias=b_col[:, c:c + 1],
                                       scale=g_col[:, c:c + 1]).then_inc(rT_set, 1)

                def outputs(t):
                    act.wait_ge(h_done, t + 1)
                    act.wait_ge(row_out, 16 * (t + 1))
                    act.activation(tabrow[:], ps_h[:, 0:C + 1], ACT.Copy).then_inc(row_set, 1)
                    act.activation(tile_of(h1, t), ps_h[:, 0:C], ACT.Copy).then_inc(h_out, 1)
                    act.activation(k["es2"][:, bass.ds(t, 1), 0], ps_h[:, C:C + 1], ACT.Copy).then_inc(h_out, 1)
                    act.activation(k["ed2"][:, bass.ds(t, 1), 0], ps_h[:, C + 1:C + 2], ACT.Copy).then_inc(h_out, 1)
                relu(0, 0)
                with act.Fori(0, NT // 2) as i:
                    for y in range(2):
                        relu(i * 2 + y + 1, 1 - y)
                        outputs(i * 2 + y)
                outputs(NT - 1)

            @block.tensor
            def _(pe):
                pe.sem_inc(turned, 1)
                pe.sem_inc(rT_set, 2)

                def turn(t):
                    pe.wait_ge(on_set, t + 1)
                    pe.wait_ge(rT_set, 2 * t + 2)
                    for c in range(CC):
                        last = pe.transpose(ps_t[:, c * P:(c + 1) * P], hn[:, c * P:(c + 1) * P], k["ident"][:])
                    last.then_inc(turned, 1)

                def product(t, y):
                    pe.wait_ge(rT_set, 2 * t + 4)
                    pe.wait_ge(h_out, 3 * t + 3)
                    for c in range(CC):
                        last = pe.matmul(ps_h[:, 0:C + 2], rT[:, y, c, :], gat_w[:, c, :], start=c == 0, stop=c == CC - 1)
                    last.then_inc(h_done, 1)
                turn(0)
                with pe.Fori(0, NT // 2) as i:
                    for y in range(2):
                        turn(i * 2 + y + 1)
                        product(i * 2 + y, y)
                product(NT - 1, 0)


def experts(nc, a, k, acc, wself, alloc, sems, mixed, out):
    with ExitStack() as st:
        sb, sem = alloc(st), sems(st)
        r = k["h1"]
        bias_b, hn = sb("gnn_b2_b", [P, C]), sb("rn", [P, C])
        rden = sb("rden_r", [P, NT, 1])
        halves, gap, mv = sb("halves_r", [P, NT, 6]), sb("gap_r", [P, NT]), sb("mv_r", [P, NT, 2])
        std, rstd = sb("std_r", [P, NT]), sb("rstd_r", [P, NT])
        add = sb("add", [P, 2, GROUP, C])
        w1, w2 = sb("ffn_w1", [P, EX * CC, ED]), sb("ffn_w2", [P, EX * FE, C])
        b1_col, b2 = sb("ffn_b1_col", [P, EX * FE]), sb("ffn_b2", [EX, C])
        wg = sb("wg", [P, CC, EX])
        gate_b = sb("gate_b", [P, 2, EX])
        xT_cur = sb("xT_cur", [P, 2, CC, P])
        lg, lg2 = sb("lg", [P, NT, EX]), sb("lg2", [P, NT, EX])
        eq, first, second = (sb(n, [P, NT, EX]) for n in ("eq", "first", "second"))
        v0, v1, w0, w1_ = (sb(n, [P, NT]) for n in ("v0", "v1", "w0", "w1_"))
        c_cur, cT = sb("c_cur", [P, EX]), sb("cT", [EX, P])
        hT = sb("hT", [P, 2, FE, P])
        xT = acc[:].rearrange("p t c -> p (t c)")[:, 0:CC * NP].rearrange("p (c n) -> p c n", c=CC)
        ps_t = st.enter_context(nc.psum_tensor("ps_xt", [P, 512], F32))
        ps_c = st.enter_context(nc.psum_tensor("ps_cb", [P, 512], F32))
        ps_h = [st.enter_context(nc.psum_tensor(f"ps_eh{y}", [P, 512], F32)) for y in range(2)]
        ps_turn, ps_lg = (ps_t, ps_h[0]), (ps_c, ps_h[1])
        ps_y = [st.enter_context(nc.psum_tensor(f"ps_ey{y}", [P, 512], F32)) for y in range(2)]
        names = ("small_in", "bias_in", "b1_in", "w_in", "own", "var", "std", "rn_set", "turned", "xT_set", "lg_done", "lg_set",
                 "gap_set", "gap_exp", "comb_set", "c_set", "c_turned", "cT_set", "bias_done", "w1_done", "h_set",
                 "w2_done", "added", "stored", "used", "xT_all")
        S = {n: sem("ffn_" + n) for n in names}
        add_in = [sem(f"ffn_add_in{y}") for y in range(2)]
        comb = lg2

        with nc.Block() as block:
            @block.sync
            def _(sp):
                sp.dma_start(bias_b[:], a["L0_gnn_b2"].partition_broadcast(P)).then_inc(S["bias_in"], 16)
                sp.dma_start(wg[:], a["L0_ffn_Wg"].rearrange("(c p) n -> p c n", p=P)).then_inc(S["small_in"], 16)
                sp.dma_start(gate_b[:, 0, :], a["L0_ffn_bg"].partition_broadcast(P)).then_inc(S["small_in"], 16)
                sp.dma_start(gate_b[:, 1, :], a["L0_ffn_bias"].partition_broadcast(P)).then_inc(S["small_in"], 16)
                sp.dma_start(b2[:], a["L0_ffn_b2"]).then_inc(S["small_in"], 16)
                for gr in range(NT // GROUP):
                    if gr > 1:
                        sp.wait_ge(S["used"], gr - 1)
                    rows = mixed[gr * GROUP * P:(gr + 1) * GROUP * P, :]
                    sp.dma_start(add[:, gr % 2], rows.rearrange("(t p) c -> p t c", p=P)).then_inc(add_in[gr % 2], 16)
                with nc.allow_non_contiguous_dma(reason="biases, one a partition"):
                    for e in range(EX):
                        sp.dma_start(b1_col[:, e * FE:(e + 1) * FE], a["L0_ffn_b1"][e].rearrange("(f p) -> p f", p=P)).then_inc(S["b1_in"], 16)
                with sp.Fori(0, NT - 1) as t:
                    sp.wait_ge(S["added"], (EX + 1) * (t + 1) + 2)
                    sp.dma_start(out[bass.ds(t * P, P), :], tile_of(r, t)).then_inc(S["stored"], 16)
                sp.wait_ge(S["added"], (EX + 1) * NT + 2)
                sp.dma_start(out[(NT - 1) * P:N, :], r[0:LAST, NT - 1, :]).then_inc(S["stored"], 16)
                sp.wait_ge(S["stored"], 16 * NT)

            @block.vector
            def _(dve):
                own = Steps(dve, S["own"])
                link = own.link
                link(dve.tensor_tensor(rden[:], acc[:, :, C:C + 1], wself[:], ALU.add))
                link(dve.tensor_scalar(rden[:], rden[:], 1e-30, None, ALU.max))
                link(dve.reciprocal(rden[:], rden[:]))
                dve.wait_ge(S["bias_in"], 16)
                aggregate(dve, own, 1, r, acc, (wself, rden), bias_b)
                for gr in range(NT // GROUP):
                    at = r[:, gr * GROUP:(gr + 1) * GROUP, :]
                    dve.wait_ge(add_in[gr % 2], 16 * (gr // 2 + 1))
                    dve.tensor_tensor(at, at, add[:, gr % 2], ALU.add).then_inc(S["used"], 1)
                dve.wait_ge(S["used"], NT // GROUP)
                moments(dve, own, r, halves, gap, mv)
                dve.tensor_scalar(rstd[:], mv[:, :, 1], EPS, None, ALU.add).then_inc(S["var"], 1)
                dve.wait_ge(S["std"], 1)
                link(dve.reciprocal(rstd[:], std[:]))

                def normed(t):
                    dve.wait_ge(S["turned"], t + 1)
                    dve.tensor_scalar(hn[:], tile_of(r, t), mv[:, bass.ds(t, 1), 0:1].rearrange("p o c -> p (o c)"),
                                      rstd[:, bass.ds(t, 1)], ALU.subtract, ALU.mult).then_inc(S["rn_set"], 1)

                def logits(t, y):
                    dve.wait_ge(S["lg_done"], t + 1)
                    dve.tensor_scalar(tile_of(lg, t), ps_lg[y][:, 0:EX], 1.0, None, ALU.mult).then_inc(S["lg_set"], 1)
                normed(0)
                normed(1)
                with dve.Fori(0, (NT - 3) // 2) as i:
                    for y in range(2):
                        normed(i * 2 + y + 2)
                        logits(i * 2 + y, y)
                normed(NT - 1)
                for t in range(NT - 3, NT):
                    logits(t, t % 2)
                dve.wait_ge(S["lg_set"], NT + 2)
                dve.wait_ge(S["small_in"], 16 * 4)
                for j in range(2):
                    link(dve.tensor_tensor(lg[:], lg[:], gate_b[:, j:j + 1, :].to_broadcast([P, NT, EX]), ALU.add))

                def wide(v):
                    return v[:].unsqueeze(2).to_broadcast([P, NT, EX])
                number = k["iota_row"][:, 0:EX].unsqueeze(1).to_broadcast([P, NT, EX])

                def largest(src, value, onehot):
                    link(dve.tensor_reduce(value[:], src[:], AX.X, ALU.max))
                    link(dve.tensor_tensor(eq[:], src[:], wide(value), ALU.is_equal))
                    link(dve.tensor_scalar(eq[:], eq[:], -float(EX), float(EX), ALU.mult, ALU.add))
                    link(dve.tensor_tensor(eq[:], eq[:], number, ALU.add))
                    link(dve.tensor_reduce(w0[:], eq[:], AX.X, ALU.min))
                    link(dve.tensor_tensor(onehot[:], number, wide(w0), ALU.is_equal))
                largest(lg, v0, first)
                link(dve.scalar_tensor_tensor(lg2[:], first[:], -3e38, lg[:], ALU.mult, ALU.add))
                largest(lg2, v1, second)
                dve.tensor_tensor(v1[:], v1[:], v0[:], ALU.subtract).then_inc(S["gap_set"], 1)
                dve.wait_ge(S["gap_exp"], 1)
                link(dve.tensor_scalar(w0[:], w1_[:], 1.0, None, ALU.add))
                link(dve.reciprocal(w0[:], w0[:]))
                link(dve.tensor_tensor(w1_[:], w1_[:], w0[:], ALU.mult))
                link(dve.tensor_tensor(first[:], first[:], wide(w0), ALU.mult))
                link(dve.tensor_tensor(second[:], second[:], wide(w1_), ALU.mult))
                link(dve.tensor_tensor(comb[:], first[:], second[:], ALU.add))
                dve.sem_inc(S["comb_set"], 1)
                dve.sem_inc(S["added"], 2)
                with own.loop(NT, 0) as t:
                    def add_to(pos):
                        dve.wait_ge(S["added"], (EX + 1) * t + pos + 2)
                    at = tile_of(r, t)
                    dve.wait_ge(S["c_turned"], t + 1)
                    dve.tensor_scalar(c_cur[:], tile_of(comb, t), 1.0, None, ALU.mult).then_inc(S["c_set"], 1)
                    for e in range(EX):
                        if e == 3:
                            dve.wait_ge(S["c_turned"], t + 2)
                            dve.tensor_copy(cT[:], ps_c[0:EX, 0:P]).then_inc(S["cT_set"], 1)
                        if e == 5:
                            dve.wait_ge(S["bias_done"], t + 1)
                            add_to(e)
                            dve.tensor_tensor(at, at, ps_t[:, 0:C], ALU.add).then_inc(S["added"], 1)
                        dve.wait_ge(S["w2_done"], EX * t + e + 3)
                        add_to(e + (e >= 5))
                        dve.scalar_tensor_tensor(at, ps_y[e % 2][:, 0:C], comb[:, bass.ds(t, 1), e:e + 1].rearrange("p o c -> p (o c)"),
                                                 at, ALU.mult, ALU.add).then_inc(S["added"], 1)

            @block.scalar
            def _(act):
                act.dma_start(w1[:], a["L0_ffn_W1"].rearrange("e (c p) n -> p (e c) n", p=P)).then_inc(S["w_in"], 16)
                act.dma_start(w2[:], a["L0_ffn_W2"].rearrange("e (f p) n -> p (e f) n", p=P)).then_inc(S["w_in"], 16)
                act.wait_ge(S["var"], 1)
                act.activation(std[:], rstd[:], ACT.Sqrt).then_inc(S["std"], 1)
                act.sem_inc(S["xT_all"], 2)

                def leave(t, y):
                    act.wait_ge(S["turned"], t + 2)
                    act.wait_ge(S["lg_set"], t + 1)
                    act.activation(xT_cur[:, y].rearrange("p c n -> p (c n)"), ps_turn[y][:, 0:C], ACT.Copy).then_inc(S["xT_set"], 1)
                    act.activation(xT[:, :, bass.ds(t * P, P)], ps_turn[y][:, 0:C].rearrange("p (c n) -> p c n", c=CC),
                                   ACT.Copy).then_inc(S["xT_all"], 1)
                with act.Fori(0, NT // 2) as i:
                    leave(i * 2, 0)
                    leave(i * 2 + 1, 1)
                leave(NT - 1, 0)
                act.wait_ge(S["gap_set"], 1)
                act.activation(w1_[:], v1[:], ACT.Exp).then_inc(S["gap_exp"], 1)
                act.sem_inc(S["h_set"], 2 * FE)
                act.wait_ge(S["b1_in"], 16 * EX)
                with act.Fori(0, NT) as t:
                    for e in range(EX):
                        act.wait_ge(S["w1_done"], EX * t + e + 1)
                        act.wait_ge(S["w2_done"], EX * t + e + 1)
                        for f in range(FE):
                            act.activation(hT[:, e % 2, f, :], ps_h[e % 2][:, f * P:(f + 1) * P], ACT.Relu,
                                           bias=b1_col[:, e * FE + f:e * FE + f + 1]).then_inc(S["h_set"], 1)

            @block.tensor
            def _(pe):
                pe.wait_ge(S["small_in"], 16 * 4)
                pe.sem_inc(S["turned"], 1)
                pe.sem_inc(S["lg_set"], 2)

                def turn(t, y):
                    pe.wait_ge(S["rn_set"], t + 1)
                    pe.wait_ge(S["xT_all"], t + 1)
                    for c in range(CC):
                        last = pe.transpose(ps_turn[y][:, c * P:(c + 1) * P], hn[:, c * P:(c + 1) * P], k["ident"][:])
                    last.then_inc(S["turned"], 1)

                def gate(t, y):
                    pe.wait_ge(S["xT_set"], t + 1)
                    pe.wait_ge(S["lg_set"], t + 1)
                    for c in range(CC):
                        last = pe.matmul(ps_lg[y][:, 0:EX], xT_cur[:, y, c, :], wg[:, c, :], start=c == 0, stop=c == CC - 1)
                    last.then_inc(S["lg_done"], 1)
                turn(0, 0)
                with pe.Fori(0, NT // 2) as i:
                    for y in range(2):
                        turn(i * 2 + y + 1, 1 - y)
                        gate(i * 2 + y, y)
                gate(NT - 1, 0)
                pe.wait_ge(S["comb_set"], 1)
                pe.wait_ge(S["xT_all"], NT + 2)
                pe.wait_ge(S["w_in"], 32)
                pe.sem_inc(S["c_turned"], 1)
                pe.sem_inc(S["w2_done"], 2)

                def up(t, e):
                    pe.wait_ge(S["h_set"], FE * (EX * t + e) + FE)
                    for f in range(FE):
                        for c in range(CC):
                            last = pe.matmul(ps_h[e % 2][:, f * P:(f + 1) * P], w1[:, e * CC + c, f * P:(f + 1) * P],
                                             xT[:, c, bass.ds(t * P, P)], start=c == 0, stop=c == CC - 1)
                    last.then_inc(S["w1_done"], 1)

                def tile(t, ends):
                    for e in range(EX):
                        if e + 1 < EX:
                            up(t, e + 1)
                        elif not ends:
                            up(t + 1, 0)
                        if e == 1:
                            pe.wait_ge(S["c_set"], t + 1)
                            pe.transpose(ps_c[0:EX, 0:P], c_cur[:], k["ident"][:]).then_inc(S["c_turned"], 1)
                        if e == 3:
                            pe.wait_ge(S["cT_set"], t + 1)
                            pe.matmul(ps_t[:, 0:C], cT[:], b2[:], start=True, stop=True).then_inc(S["bias_done"], 1)
                        pe.wait_ge(S["h_set"], FE * (EX * t + e) + 3 * FE)
                        before = e - 2
                        pe.wait_ge(S["added"], (EX + 1) * t + before + (before >= 5) + 3)
                        for f in range(FE):
                            last = pe.matmul(ps_y[e % 2][:, 0:C], hT[:, e % 2, f, :], w2[:, e * FE + f, :], start=f == 0, stop=f == FE - 1)
                        last.then_inc(S["w2_done"], 1)
                up(0, 0)
                with pe.Fori(0, NT - 1) as t:
                    tile(t, False)
                tile(NT - 1, True)


_INS = ["x", "src", "dst"] + ["L0_gnn_" + n for n in ("W1", "a1_src", "a1_dst", "b1", "ln_g", "ln_b", "W2", "a2_src", "a2_dst", "b2")] \
    + ["L0_mix_" + n for n in ("ln1_g", "ln1_b", "Wx", "bx", "Wq", "Wk", "Wv", "Wo", "bo", "ln2_g", "ln2_b", "W1", "b1", "W2", "b2")] \
    + ["L0_ffn_" + n for n in ("Wg", "bg", "bias", "W1", "b1", "W2", "b2")]


def kernel(**inputs):
    import numpy as _np
    import concourse.bacc as _bacc
    from concourse import mybir as _mybir
    from concourse.bass_utils import run_bass_kernel_spmd as _run

    nc = _bacc.Bacc("TRN2", target_bir_lowering=False, num_devices=1)
    arrays, args = {}, {}
    for name in _INS:
        array = _np.ascontiguousarray(inputs[name])
        arrays[f"in_{name}"] = array
        args[name] = nc.dram_tensor(f"in_{name}", array.shape, _mybir.dt.from_np(array.dtype), kind="ExternalInput").ap()
    out = nc.dram_tensor("out", [N, C], F32, kind="ExternalOutput").ap()
    build(nc, args, out)
    r = _run(nc, [arrays], core_ids=[0])
    return r.results[0]["out"]
```
